# Optimizing a Trainium2 kernel written in Bass

```python
import numpy as np
import jax
import jax.numpy as jnp

def _softmax(x, axis=-1):
    return jax.nn.softmax(x, axis=axis)

def _gelu(x):
    return jax.nn.gelu(x, approximate=True)

def _silu(x):
    return jax.nn.silu(x)

def _sigmoid(x):
    return jax.nn.sigmoid(x)

def _layernorm(x, axis=-1, eps=1e-05):
    m = jnp.mean(x, axis=axis, keepdims=True)
    v = jnp.var(x, axis=axis, keepdims=True)
    return (x - m) / jnp.sqrt(v + eps)

def _scatter_add(tgt, idx, src, axis=0):
    return tgt.at[idx].add(src)

def _segment_sum(src, seg, n):
    return jax.ops.segment_sum(src, seg, n)
kernel_name = 'mk_gnn_preln_d2_gnn_r8_c2b661'

def setup_inputs(seed: int=0):
    np.random.seed(seed)
    _w = jnp.asarray

    def _rec_inputs():
        import jax
        import jax.numpy as jnp
        _gk = jax.random.key(seed)
        x = -0.0003713 + 1 * jax.random.normal(jax.random.fold_in(_gk, 1), (6250, 256), jnp.float32)
        _s = jax.random.randint(jax.random.fold_in(_gk, 2), (50000,), 0, 6250, jnp.int32)
        _d = jax.random.randint(jax.random.fold_in(_gk, 3), (50000,), 0, 6250, jnp.int32)
        _loop = jnp.arange(6250, dtype=jnp.int32)
        src = jnp.concatenate([_s, _d, _loop])
        dst = jnp.concatenate([_d, _s, _loop])
        _o = jnp.argsort(dst, stable=True)
        src = src[_o]
        dst = dst[_o]
        edge_type_16 = jax.random.randint(jax.random.fold_in(_gk, 12), (106250,), 0, 16, jnp.int32)
        return (x, src, dst, edge_type_16)
    x, src, dst, edge_type_16 = _rec_inputs()

    def _L0_gnn_setup():
        import jax, jax.numpy as jnp
        import numpy as np
        N_NODES = 6250
        IN_DIM = 256
        OUT_DIM = 128
        NUM_HEADS = 2
        N_EDGES = 100000

        def _gat_forward(x, edge_index, W_w, W_b, a):
            N = x.shape[0]
            H, D = (NUM_HEADS, OUT_DIM)
            Wh = (x @ W_w + W_b).reshape(N, H, D)
            src, dst = (edge_index[0], edge_index[1])
            a_src, a_dst = (a[:D], a[D:])
            s = jnp.einsum('nhd,d->nh', Wh, a_src)
            t = jnp.einsum('nhd,d->nh', Wh, a_dst)
            e = jax.nn.leaky_relu(s[src] + t[dst], negative_slope=0.2)
            m = jax.ops.segment_max(e, src, num_segments=N)
            ex = jnp.exp(e - m[src])
            denom = jax.ops.segment_sum(ex, src, num_segments=N)
            alpha = ex / denom[src]
            agg = jax.ops.segment_sum(alpha[:, :, None] * Wh[dst], src, num_segments=N)
            deg = jax.ops.segment_sum(jnp.ones_like(src, dtype=Wh.dtype), src, num_segments=N)
            h_prime = jnp.where(deg[:, None, None] > 0, agg, Wh)
            return h_prime.reshape(N, H * D)
        key = jax.random.key(seed)
        k1, k2, k3, k4, k5 = jax.random.split(key, 5)
        x = jax.random.normal(k1, (N_NODES, IN_DIM), dtype=jnp.float32)
        edge_index = jax.random.randint(k2, (2, N_EDGES), 0, N_NODES, dtype=jnp.int64)
        fan = IN_DIM + OUT_DIM * NUM_HEADS
        W_w = jax.random.uniform(k3, (IN_DIM, OUT_DIM * NUM_HEADS), dtype=jnp.float32, minval=-np.sqrt(6.0 / fan), maxval=np.sqrt(6.0 / fan))
        W_b = jnp.zeros((OUT_DIM * NUM_HEADS,), dtype=jnp.float32)
        fa = 1 + 2 * OUT_DIM
        a = jax.random.uniform(k4, (2 * OUT_DIM,), dtype=jnp.float32, minval=-np.sqrt(6.0 / fa), maxval=np.sqrt(6.0 / fa))
        return {'x': x, 'edge_index': edge_index, 'W_w': W_w, 'W_b': W_b, 'a': a}
    _L0_gnn_all = _L0_gnn_setup()
    _L0_gnn_in = {k: v for k, v in _L0_gnn_all.items() if k in ('W_w', 'W_b', 'a')}
    del _L0_gnn_all

    def _L1_gnn_setup():
        import jax, jax.numpy as jnp
        import numpy as np
        N_NODES = 1250
        N_EDGES = 40000
        IN_DIM = 256
        OUT_DIM = 256
        N_REL = 16
        key = jax.random.key(seed)
        k_x, k_src, k_dst, k_et, k_wr, k_w0 = jax.random.split(key, 6)
        x = jax.random.normal(k_x, (N_NODES, IN_DIM), dtype=jnp.float32)
        src = jax.random.randint(k_src, (N_EDGES,), 0, N_NODES)
        dst = jax.random.randint(k_dst, (N_EDGES,), 0, N_NODES)
        edge_index = jnp.stack([src, dst], axis=0)
        edge_type = jax.random.randint(k_et, (N_EDGES,), 0, N_REL)
        lim_r = float(np.sqrt(6.0 / (IN_DIM + OUT_DIM)))
        W_r = jax.random.uniform(k_wr, (N_REL, IN_DIM, OUT_DIM), minval=-lim_r, maxval=lim_r, dtype=jnp.float32)
        W0_w = jax.random.uniform(k_w0, (OUT_DIM, IN_DIM), minval=-lim_r, maxval=lim_r, dtype=jnp.float32)
        W0_b = jnp.zeros((OUT_DIM,), dtype=jnp.float32)
        return {'x': x, 'W_r': W_r, 'W0_w': W0_w, 'W0_b': W0_b, 'edge_index': edge_index, 'edge_type': edge_type, 'num_nodes_local': N_NODES}
    _L1_gnn_all = _L1_gnn_setup()
    _L1_gnn_in = {k: v for k, v in _L1_gnn_all.items() if k in ('W_r', 'W0_w', 'W0_b')}
    del _L1_gnn_all
    return {'x': x, 'src': src, 'dst': dst, 'edge_type_16': edge_type_16, 'L0_gnn_W_w': _L0_gnn_in['W_w'], 'L0_gnn_W_b': _L0_gnn_in['W_b'], 'L0_gnn_a': _L0_gnn_in['a'], 'L1_gnn_W_r': _L1_gnn_in['W_r'], 'L1_gnn_W0_w': _L1_gnn_in['W0_w'], 'L1_gnn_W0_b': _L1_gnn_in['W0_b']}

def reference(x, src, dst, edge_type_16, L0_gnn_W_w, L0_gnn_W_b, L0_gnn_a, L1_gnn_W_r, L1_gnn_W0_w, L1_gnn_W0_b):
    import jax
    import jax.numpy as jnp

    def _L0_gnn_ref(x, edge_index, W_w, W_b, a):
        import jax, jax.numpy as jnp
        import numpy as np
        N_NODES = 6250
        IN_DIM = 256
        OUT_DIM = 128
        NUM_HEADS = 2
        N_EDGES = 100000

        def _gat_forward(x, edge_index, W_w, W_b, a):
            N = x.shape[0]
            H, D = (NUM_HEADS, OUT_DIM)
            Wh = (x @ W_w + W_b).reshape(N, H, D)
            src, dst = (edge_index[0], edge_index[1])
            a_src, a_dst = (a[:D], a[D:])
            s = jnp.einsum('nhd,d->nh', Wh, a_src)
            t = jnp.einsum('nhd,d->nh', Wh, a_dst)
            e = jax.nn.leaky_relu(s[src] + t[dst], negative_slope=0.2)
            m = jax.ops.segment_max(e, src, num_segments=N)
            ex = jnp.exp(e - m[src])
            denom = jax.ops.segment_sum(ex, src, num_segments=N)
            alpha = ex / denom[src]
            agg = jax.ops.segment_sum(alpha[:, :, None] * Wh[dst], src, num_segments=N)
            deg = jax.ops.segment_sum(jnp.ones_like(src, dtype=Wh.dtype), src, num_segments=N)
            h_prime = jnp.where(deg[:, None, None] > 0, agg, Wh)
            return h_prime.reshape(N, H * D)
        return _gat_forward(x, edge_index, W_w, W_b, a)

    def _L1_gnn_ref(x, W_r, W0_w, W0_b, edge_index, edge_type, num_nodes_local):
        import jax, jax.numpy as jnp
        import numpy as np
        N_NODES = 1250
        N_EDGES = 40000
        IN_DIM = 256
        OUT_DIM = 256
        N_REL = 16
        N = num_nodes_local
        R = W_r.shape[0]
        src = edge_index[0]
        dst = edge_index[1]
        deg = jnp.zeros((R, N), dtype=x.dtype).at[edge_type, dst].add(1.0)
        deg = jnp.maximum(deg, 1.0)
        h_all = jnp.einsum('nd,rdo->rno', x, W_r)
        msg = h_all[edge_type, src] / deg[edge_type, dst][:, None]
        agg = jax.ops.segment_sum(msg, dst, num_segments=N)
        return agg + x @ W0_w.T + W0_b
    edge_index = jnp.stack([src, dst])
    h = jnp.maximum(_layernorm(x, axis=-1), 0.0)
    x = x + _L0_gnn_ref(h, edge_index, L0_gnn_W_w, L0_gnn_W_b, L0_gnn_a)
    h = jnp.maximum(_layernorm(x, axis=-1), 0.0)
    x = x + _L1_gnn_ref(h, L1_gnn_W_r, L1_gnn_W0_w, L1_gnn_W0_b, edge_index, edge_type_16, 6250)
    return x

_drawn_inputs = setup_inputs


def setup_inputs(seed=0):
    import zlib

    import numpy as np

    out = dict(_drawn_inputs(seed))
    spreads = {'L0_gnn_W_b': (0.0, 0.1), 'L1_gnn_W0_b': (0.0, 0.1)}
    factors = {}
    for name, (base, spread) in spreads.items():
        noise = np.random.default_rng([zlib.crc32(name.encode()), seed]).standard_normal(out[name].shape)
        drawn = base * np.exp(spread * noise) if base else spread * noise
        out[name] = jnp.asarray(drawn.astype(out[name].dtype))
    for name, factor in factors.items():
        out[name] = (out[name] * factor).astype(out[name].dtype)
    return out
```

```python
from contextlib import ExitStack

import numpy as np

import concourse.bass as bass
from concourse import mybir

F32 = mybir.dt.float32
BF16 = mybir.dt.bfloat16
I32 = mybir.dt.int32
ALU = mybir.AluOpType
ACT = mybir.ActivationFunctionType
AX = mybir.AxisListType

P = 128
NODES, DIM, HEADS, HD, RELS, EDGES = 6250, 256, 2, 128, 16, 106250
TILES = -(-NODES // P)
FULL = NODES // P
REST = NODES - FULL * P
EPART = 125
ECOL = EDGES // EPART
CCOL = 50
CHUNKS = ECOL // CCOL
SORTS = 2
ALLC = SORTS * CHUNKS
GRAN = 8
GCOLS = -(-(EPART * CCOL + TILES * (GRAN - 1)) // (P * GRAN))
HI = GCOLS * GRAN
SUB = 4
GROUP = SUB * P
GPG = GROUP // GRAN
UNROLL = 4
MAXGRAN = (EDGES + CHUNKS * TILES * (GRAN - 1)) // GRAN
GROUPS = (MAXGRAN + TILES * (GPG - 1)) // GPG
GROUPS = -(-GROUPS // UNROLL) * UNROLL
REGION = GROUPS * GPG + CHUNKS * GCOLS * P
PADLOC = 1000.0
BIG = float(2.0 ** 100)
SLOPE = 0.2
EPS = 1e-5
TW = 260
HW = HD + 1
TCOL = 2 * HW


class Step:

    def __init__(self, v, least, rnd):
        self.v, self.least, self.round = v, least, rnd

    def slot(self, ring):
        return self.least % ring

    def past(self, n):
        return self.least >= n


def repeat(eng, n, unroll, stages):
    lags = [lag for lag, _ in stages]
    first = -(-(max(lags) + unroll) // unroll) * unroll
    rounds = max(0, (n - first) // unroll)

    def static(j):
        for lag, fn in stages:
            if 0 <= j - lag < n:
                fn(Step(j - lag, j - lag, (j - lag) // unroll))

    for j in range(first):
        static(j)
    if rounds:
        with eng.Fori(0, rounds) as it:
            for u in range(unroll):
                for lag, fn in stages:
                    base = first + u - lag
                    fn(Step(it * unroll + base, base, it + base // unroll))
    for j in range(first + rounds * unroll, n + max(lags)):
        static(j)


def build(nc, A, out):
    ctx = ExitStack()
    with ctx:
        def sb(name, shape, dt=F32):
            return ctx.enter_context(nc.sbuf_tensor(name, shape, dt))

        def sem(name):
            return ctx.enter_context(nc.semaphore(name))

        wh_table = nc.dram_tensor("wh_table", [TILES * P, TW], F32, kind="Internal").ap()
        rel_table = nc.dram_tensor("rel_table", [TILES * P * RELS, DIM], F32, kind="Internal").ap()
        records = nc.dram_tensor("records", [SORTS * REGION, GRAN], F32, kind="Internal").ap()
        gtile_dram = nc.dram_tensor("gtile_dram", [SORTS, 3 * P], I32, kind="Internal").ap()

        X = sb("X", [P, TILES, DIM])
        ident = sb("ident", [P, P])
        identb = sb("identb", [P, P], BF16)
        iota = sb("iota", [P, P])
        gtile = sb("gtile", [1, SORTS, GROUPS], I32)
        SM = sb("SM", [P, TILES, 4])
        mv = sb("mv", [P, TILES, 2])
        rstd = sb("rstd", [P, TILES])
        nbias = sb("nbias", [P, TILES])
        eps = sb("eps", [P, 1])
        ones_row = sb("ones_row", [1, P])
        row1 = sb("row1", [1, TW + 2])
        row2 = sb("row2", [1, DIM])
        ARENA = 25500
        arena = sb("arena", [P, ARENA])
        ACCW = TILES * TCOL
        acc = arena[:, 0:ACCW].rearrange("p (t c) -> p t c", c=TCOL)

        class Carve:
            def __init__(self, at=0):
                self.at = at

            def __call__(self, shape, dt=F32):
                n = int(np.prod(shape))
                w = n if dt in (F32, I32) else -(-n // 2)
                v = arena[:, self.at:self.at + w]
                if dt is not F32:
                    v = v.bitcast(dt)
                self.at += w
                assert self.at <= ARENA, self.at
                if len(shape) == 1:
                    return v
                names = "abcd"[:len(shape)]
                return v.rearrange(f"p ({' '.join(names)}) -> p {' '.join(names)}",
                                   **{m: s for m, s in zip(names[1:], shape[1:])})

        def psum(stack, name, shape, dt=F32):
            return stack.enter_context(nc.psum_tensor(name, shape, dt))

        carve = Carve()
        tile_hot = [carve([TILES, CCOL], BF16) for _ in range(2)]
        rank = [carve([TILES, CCOL]) for _ in range(2)]
        lo_hot = [carve([CCOL, P]) for _ in range(1)]
        hi_val = [carve([CCOL, HI]) for _ in range(1)]
        scan_keep = carve([TILES, CCOL], BF16)
        edge_tile = carve([SORTS, ECOL])
        edge_val = carve([SORTS, ECOL])
        edge_i = carve([3, ECOL], I32)
        ints = carve([2, ECOL], I32)
        early = ctx.enter_context(ExitStack())

        def sbe(name, shape, dt=F32):
            return early.enter_context(nc.sbuf_tensor(name, shape, dt))

        hbuf = [sb(f"hbuf{i}", [P, DIM]) for i in range(2)]
        hT = [sb(f"hT{i}", [P, 2, P]) for i in range(2)]
        proj = [sb(f"proj{i}", [P, TW + 2]) for i in range(2)]
        stats = sb("stats", [P, TILES, 6])
        Wx = sbe("Wx", [P, 2, TW + 2])
        abc = sbe("abc", [P, 2 * HD])
        w_in = sbe("w_in", [P, 2, DIM])
        prod = sbe("prod", [P, HD])
        b_in = sbe("b_in", [1, DIM])
        below = sbe("below", [P, P], BF16)
        allone = sbe("allone", [P, P], BF16)
        iota_i = sbe("iota_i", [P, P], I32)
        totals = [sbe(f"totals{i}", [P, TILES], BF16) for i in range(2)]
        gran_i = [sbe(f"gran_i{i}", [P, 2, TILES], I32) for i in range(2)]
        gran_f = [sbe(f"gran_f{i}", [P, 2, TILES]) for i in range(2)]
        pos_f = [sbe(f"pos_f{i}", [P, CCOL]) for i in range(2)]
        pos_i = [sbe(f"pos_i{i}", [P, 4, CCOL], I32) for i in range(2)]
        gran_n = sbe("gran_n", [P, TILES, ALLC])
        gran_at = sbe("gran_at", [P, ALLC, TILES + 1])
        packed = sbe("packed", [P, ALLC, GCOLS, GRAN])
        one_row = sbe("one_row", [P, TILES])
        zero = sbe("zero", [P, 512])

        with ExitStack() as ps:
            pT = [psum(ps, f"pT{i}", [P, 2, P]) for i in range(2)]
            pP = [psum(ps, f"pP{i}", [P, 512]) for i in range(2)]
            pB = [psum(ps, f"pB{i}", [P, 512]) for i in range(2)]
            pC = [psum(ps, f"pC{i}", [P, 512]) for i in range(2)]
            edges_in, weights_in, x_in, zeroed = sem("edges_in"), sem("weights_in"), sem("x_in"), sem("zeroed")
            pool_c, consts, dve_c = sem("pool_c"), sem("consts"), sem("dve_c")
            x_padded, stats_done, std_done, ln_ready = (sem("x_padded"), sem("stats_done"), sem("std_done"), sem("ln_ready"))
            w_ready = sem("w_ready")
            h_ready, hT_ps, hT_ready, proj_ps, proj_ready = (sem("h_ready"), sem("hT_ps"), sem("hT_ready"),
                                                             sem("proj_ps"), sem("proj_ready"))
            proj_out = [sem(f"proj_out{i}") for i in range(2)]
            st_a = sem("st_a")
            sort_a, sort_c, sort_d = sem("sort_a"), sem("sort_c"), sem("sort_d")
            counted, ranked_in, hots, compact, packed_ready = (sem("counted"), sem("totals_ready"), sem("hots"),
                                                               sem("compact"), sem("packed_ready"))
            with nc.Block() as block:

                @block.sync
                def _(sp):
                    for n, name in enumerate(("src", "dst", "edge_type_16")):
                        sp.dma_start(edge_i[0:EPART, n, :], A[name].rearrange("(p c) -> p c", c=ECOL)).then_inc(edges_in, 16)
                    sp.wait_ge(x_padded, 1)
                    sp.dma_start(X[:, 0:FULL, :], A["x"][0:FULL * P, :].rearrange("(t p) d -> p t d", p=P)).then_inc(x_in, 16)
                    sp.dma_start(X[0:REST, FULL, :], A["x"][FULL * P:NODES, :]).then_inc(x_in, 16)
                    sp.dma_start(w_in[:, :, :], A["L0_gnn_W_w"].rearrange("(k p) n -> p k n", p=P)).then_inc(weights_in, 16)
                    sp.dma_start(abc[:, :], A["L0_gnn_a"].rearrange("(o n) -> o n", o=1).to_broadcast([P, 2 * HD])).then_inc(weights_in, 16)
                    sp.dma_start(b_in[:, :], A["L0_gnn_W_b"].rearrange("(o n) -> o n", o=1)).then_inc(weights_in, 16)
                    sp.wait_ge(x_padded, 2)
                    for s in range(SORTS):
                        rows = records[s * REGION:s * REGION + GROUPS * GPG, :].rearrange("(g r) w -> g (r w)", r=GPG)
                        for g in range(0, GROUPS, P):
                            m = min(P, GROUPS - g)
                            sp.dma_start(rows[g:g + m, :], zero[0:m, :]).then_inc(zeroed, 16)

                    def store(k):
                        sp.wait_ge(proj_ready, k.v + 1)
                        sp.dma_start(wh_table.rearrange("(t p) c -> t p c", p=P)[bass.ds(k.v, 1), :, :].rearrange("t p c -> p (t c)"),
                                     proj[k.slot(2)][:, 0:TW]).then_inc(proj_out[k.slot(2)], 16)
                    repeat(sp, TILES, 2, [(0, store)])
                    sp.wait_ge(proj_out[0], 16 * (TILES - TILES // 2))
                    sp.wait_ge(proj_out[1], 16 * (TILES // 2))
                    sp.wait_ge(zeroed, 16 * SORTS * -(-GROUPS // P))

                @block.gpsimd
                def _(g):
                    g.iota(iota_i[:, :], pattern=[[1, P]], base=0, channel_multiplier=0).then_inc(pool_c, 1)
                    g.memset(ident[:, :], 0.0).then_inc(pool_c, 1)
                    g.memset(below[:, :], 1.0).then_inc(pool_c, 1)
                    g.wait_ge(pool_c, 3)
                    g.affine_select(out=ident[:, :], in_=ident[:, :], compare_op=ALU.not_equal, fill=1.0, base=0,
                                    pattern=[[-1, P]], channel_multiplier=1).then_inc(pool_c, 1)
                    g.affine_select(out=below[:, :], in_=below[:, :], compare_op=ALU.is_gt, fill=0.0, base=0,
                                    pattern=[[1, P]], channel_multiplier=-1).then_inc(pool_c, 1)

                @block.scalar
                def _(act):
                    act.wait_ge(stats_done, TILES)
                    act.activation(rstd[:, :], mv[:, :, 1], ACT.Sqrt, bias=eps[:, 0:1]).then_inc(std_done, 1)
                    act.wait_ge(ln_ready, 1)

                    def norm(k):
                        if k.past(2):
                            act.wait_ge(hT_ps, k.v - 1)
                        act.activation(hbuf[k.slot(2)][:, :], X[:, bass.ds(k.v, 1), :].rearrange("p t d -> p (t d)"), ACT.Relu,
                                       bias=nbias[:, bass.ds(k.v, 1)], scale=rstd[:, bass.ds(k.v, 1)]).then_inc(h_ready, 1)

                    def move_hT(k):
                        act.wait_ge(hT_ps, k.v + 1)
                        if k.past(2):
                            act.wait_ge(proj_ps, k.v - 1)
                        act.activation(hT[k.slot(2)][:, :, :], pT[k.slot(2)][:, :, :], ACT.Copy).then_inc(hT_ready, 1)

                    def move_proj(k):
                        act.wait_ge(proj_ps, k.v + 1)
                        if k.past(2):
                            act.wait_ge(proj_out[k.slot(2)], k.round * 16)
                        act.activation(proj[k.slot(2)][:, 0:TW], pP[k.slot(2)][:, 0:TW], ACT.Copy)
                        act.activation(SM[:, bass.ds(k.v, 1), 0:2].rearrange("p t c -> p (t c)"), pP[k.slot(2)][:, TW:TW + 2], ACT.Copy).then_inc(proj_ready, 1)
                    repeat(act, TILES, 2, [(0, norm), (1, move_hT), (2, move_proj)])

                    def move_packed(k):
                        act.wait_ge(compact, k.v + 1)
                        act.activation(packed[:, bass.ds(k.v, 1), :, :].rearrange("p c g r -> p (c g r)"),
                                       pC[k.slot(2)][:, 0:HI], ACT.Copy).then_inc(packed_ready, 1)
                    repeat(act, ALLC, 2, [(0, move_packed)])

                def layernorm_stats(v):
                    def one(k):
                        v.bn_stats(stats[:, bass.ds(k.v, 1), :].rearrange("p t c -> p (t c)"),
                                   X[:, bass.ds(k.v, 1), :].rearrange("p t d -> p (t d)")).then_inc(st_a, 1)
                    repeat(v, TILES, 2, [(0, one)])
                    v.wait_ge(st_a, TILES)
                    for t in range(TILES):
                        v.bn_aggr(mv[:, t, :], stats[:, t, :]).then_inc(stats_done, 1)
                    v.wait_ge(std_done, 1)
                    v.reciprocal(rstd[:, :], rstd[:, :]).then_inc(std_done, 1)
                    v.wait_ge(std_done, 2)
                    v.scalar_tensor_tensor(nbias[:, :], mv[:, :, 0], -1.0, rstd[:, :], ALU.mult, ALU.mult).then_inc(ln_ready, 1)

                @block.vector
                def _(v):
                    n = [0]

                    def chain(ins):
                        n[0] += 1
                        ins.then_inc(dve_c, 1)
                        v.wait_ge(dve_c, n[0])

                    v.memset(X[:, FULL, :], 0.0).then_inc(x_padded, 1)
                    v.memset(zero[:, :], 0.0).then_inc(x_padded, 1)
                    v.memset(eps[:, :], EPS)
                    v.memset(ones_row[:, :], 1.0)
                    v.memset(allone[:, :], 1.0)
                    v.memset(one_row[:, :], 1.0)
                    v.memset(SM[:, :, 2:4], -BIG)
                    v.memset(scan_keep[:, :, :], 1.0)
                    v.memset(edge_tile[:, :, :], -1.0)
                    v.memset(edge_val[:, :, :], 0.0)
                    v.memset(Wx[:, :, :], 0.0)
                    chain(v.memset(row1[:, :], 0.0))
                    v.memset(scan_keep[:, :, 0:1], 0.0)
                    v.memset(row1[:, HD:HD + 1], 1.0)
                    v.memset(row1[:, HW + HD:HW + HD + 1], 1.0)
                    v.wait_ge(pool_c, 5)
                    v.tensor_copy(iota[:, :], iota_i[:, :])
                    v.tensor_copy(identb[:, :], ident[:, :])
                    E = slice(0, EPART)
                    v.wait_ge(edges_in, 48)
                    v.tensor_single_scalar(ints[E, 0, :], edge_i[E, 0, :], 7, ALU.arith_shift_right)
                    chain(v.tensor_single_scalar(ints[E, 1, :], edge_i[E, 0, :], 127, ALU.bitwise_and))
                    v.tensor_copy(edge_tile[E, 0, :], ints[E, 0, :])
                    chain(v.scalar_tensor_tensor(edge_val[E, 0, :], edge_i[E, 1, :], float(P), ints[E, 1, :], ALU.mult, ALU.add))
                    chain(v.tensor_scalar(edge_val[E, 0, :], edge_val[E, 0, :], 1.0, None, ALU.add))
                    v.scalar_tensor_tensor(edge_val[E, 1, :], edge_i[E, 0, :], float(RELS), edge_i[E, 2, :], ALU.mult, ALU.add)
                    v.tensor_single_scalar(ints[E, 0, :], edge_i[E, 1, :], 7, ALU.arith_shift_right)
                    chain(v.tensor_single_scalar(ints[E, 1, :], edge_i[E, 1, :], 127, ALU.bitwise_and))
                    v.tensor_copy(edge_tile[E, 1, :], ints[E, 0, :])
                    chain(v.scalar_tensor_tensor(edge_val[E, 1, :], edge_val[E, 1, :], float(P), ints[E, 1, :], ALU.mult, ALU.add))
                    chain(v.tensor_scalar(edge_val[E, 1, :], edge_val[E, 1, :], 1.0, None, ALU.add))
                    v.wait_ge(weights_in, 48)
                    for k in range(3):
                        w_rows, w_to = (w_in[:, k, :], Wx[:, k, :]) if k < 2 else (b_in[0:1, :], row1[0:1, :])
                        q = slice(0, P if k < 2 else 1)
                        for h in range(HEADS):
                            v.tensor_copy(w_to[:, h * HW:h * HW + HD], w_rows[:, h * HD:(h + 1) * HD])
                            for c, a in ((TCOL + h, HD), (TW + h, 0)):
                                chain(v.tensor_tensor_reduce(out=prod[q, :], in0=w_rows[:, h * HD:(h + 1) * HD], in1=abc[q, a:a + HD],
                                                             scale=1.0, scalar=0.0, op0=ALU.mult, op1=ALU.add,
                                                             accum_out=w_to[:, c:c + 1]))
                    v.tensor_copy(row1[0:1, HD:HD + 1], row1[0:1, HD:HD + 1]).then_inc(w_ready, 1)
                    v.wait_ge(x_in, 32)
                    layernorm_stats(v)

                    def count(k):
                        sl = k.slot(2)
                        s = bass.ds(k.v * CCOL, CCOL)
                        keys = edge_tile.rearrange("p s c -> p (s c)")[:, s]
                        if k.past(2):
                            v.wait_ge(hots, k.v - 1)
                        v.tensor_tensor(tile_hot[sl], keys[:, None, :].to_broadcast([P, TILES, CCOL]),
                                        iota[:, 0:TILES, None].to_broadcast([P, TILES, CCOL]), ALU.is_equal).then_inc(sort_a, 1)
                        v.wait_ge(sort_a, 2 * k.v + 1)
                        v.tensor_tensor_scan(rank[sl].rearrange("p b t -> p (b t)"), scan_keep.rearrange("p b t -> p (b t)"),
                                             tile_hot[sl].rearrange("p b t -> p (b t)"), 0.0, ALU.mult, ALU.add).then_inc(sort_a, 1)
                        v.wait_ge(sort_a, 2 * k.v + 2)
                        v.tensor_copy(totals[sl][:, :], rank[sl][:, :, CCOL - 1]).then_inc(ranked_in, 1)

                    def place(k):
                        sl = k.slot(2)
                        s = bass.ds(k.v * CCOL, CCOL)
                        vals = edge_val.rearrange("p s c -> p (s c)")[:, s]
                        gi, gf = gran_i[sl], gran_f[sl]
                        step = [0]

                        def link(ins):
                            step[0] += 1
                            ins.then_inc(sort_c, 1)
                            v.wait_ge(sort_c, 9 * k.v + step[0])
                        v.wait_ge(counted, k.v + 1)
                        base, cnt = pB[sl][:, 0:TILES], pB[sl][:, TILES:2 * TILES]
                        link(v.tensor_scalar(gi[:, 0, :], cnt, float(GRAN - 1), None, ALU.add))
                        link(v.tensor_single_scalar(gi[:, 1, :], gi[:, 0, :], 3, ALU.arith_shift_right))
                        v.tensor_scalar(gran_n[:, :, bass.ds(k.v, 1)].rearrange("p b c -> p (b c)"), gi[:, 1, :], 0.0, None, ALU.add)
                        link(v.tensor_tensor_scan(gf[:, 0, :], one_row[:, :], gi[:, 1, :], 0.0, ALU.mult, ALU.add))
                        v.tensor_scalar(gran_at[:, bass.ds(k.v, 1), TILES:TILES + 1].rearrange("p c b -> p (c b)"), gf[:, 0, TILES - 1:TILES], 0.0, None, ALU.add)
                        link(v.tensor_tensor(gf[:, 1, :], gf[:, 0, :], gi[:, 1, :], ALU.subtract))
                        v.tensor_scalar(gran_at[:, bass.ds(k.v, 1), 0:TILES].rearrange("p c b -> p (c b)"), gf[:, 1, :], 0.0, None, ALU.add)
                        link(v.scalar_tensor_tensor(gf[:, 0, :], gf[:, 1, :], float(GRAN), base, ALU.mult, ALU.add))
                        link(v.tensor_tensor(rank[sl], rank[sl], gf[:, 0, :, None].to_broadcast([P, TILES, CCOL]), ALU.add))
                        link(v.tensor_tensor(rank[sl], rank[sl], tile_hot[sl], ALU.mult))
                        link(v.tensor_reduce(pos_f[sl][:, :], rank[sl].rearrange("p b t -> p t b"), AX.X, ALU.add))
                        pi = pos_i[sl]
                        link(v.tensor_scalar(pi[:, 0, :], pos_f[sl][:, :], -1.0, 0.0, ALU.add, ALU.max))
                        v.tensor_scalar(pi[:, 1, :], pi[:, 0, :], 3, P - 1, ALU.arith_shift_right, ALU.bitwise_and)
                        v.tensor_scalar(pi[:, 2, :], pi[:, 0, :], 10, 3, ALU.arith_shift_right, ALU.logical_shift_left)
                        v.tensor_single_scalar(pi[:, 3, :], pi[:, 0, :], GRAN - 1, ALU.bitwise_and).then_inc(sort_d, 1)
                        v.wait_ge(sort_d, 3 * k.v + 1)
                        v.tensor_tensor(pi[:, 3, :], pi[:, 3, :], pi[:, 2, :], ALU.bitwise_or).then_inc(sort_d, 1)
                        v.wait_ge(sort_d, 3 * k.v + 2)
                        if k.past(1):
                            v.wait_ge(compact, k.v)
                        v.tensor_tensor(hi_val[0], iota[:, None, 0:HI].to_broadcast([P, CCOL, HI]),
                                        pi[:, 3, :, None].to_broadcast([P, CCOL, HI]), ALU.is_equal).then_inc(sort_d, 1)
                        v.tensor_tensor(lo_hot[0], iota[:, None, :].to_broadcast([P, CCOL, P]),
                                        pi[:, 1, :, None].to_broadcast([P, CCOL, P]), ALU.is_equal)
                        v.wait_ge(sort_d, 3 * k.v + 3)
                        v.tensor_tensor(hi_val[0], hi_val[0], vals[:, :, None].to_broadcast([P, CCOL, HI]), ALU.mult).then_inc(hots, 1)

                    repeat(v, ALLC, 2, [(0, count), (1, place)])

                @block.tensor
                def _(pe):
                    pe.wait_ge(w_ready, 1)

                    def transpose_h(k):
                        pe.wait_ge(h_ready, k.v + 1)
                        if k.past(2):
                            pe.wait_ge(hT_ready, k.v - 1)
                        for j in range(2):
                            last = pe.transpose(pT[k.slot(2)][:, j, :], hbuf[k.slot(2)][:, j * P:(j + 1) * P], ident[:, :])
                        last.then_inc(hT_ps, 1)

                    def project(k):
                        pe.wait_ge(hT_ready, k.v + 1)
                        if k.past(2):
                            pe.wait_ge(proj_ready, k.v - 1)
                        o = pP[k.slot(2)][:, 0:TW + 2]
                        pe.matmul(o, hT[k.slot(2)][:, 0, :], Wx[:, 0, :], start=True, stop=False)
                        pe.matmul(o, hT[k.slot(2)][:, 1, :], Wx[:, 1, :], start=False, stop=False)
                        pe.matmul(o, ones_row[0:1, :], row1[0:1, :], start=False, stop=True).then_inc(proj_ps, 1)
                    repeat(pe, TILES, 2, [(0, transpose_h), (1, project)])

                    def count(k):
                        pe.wait_ge(ranked_in, k.v + 1)
                        if k.past(2):
                            pe.wait_ge(hots, k.v - 1)
                        pe.matmul(pB[k.slot(2)][:, 0:TILES], below[:, :], totals[k.slot(2)][:, :], start=True, stop=True)
                        pe.matmul(pB[k.slot(2)][:, TILES:2 * TILES], allone[:, :], totals[k.slot(2)][:, :], start=True, stop=True).then_inc(counted, 1)

                    def compaction(k):
                        pe.wait_ge(hots, k.v + 1)
                        if k.past(2):
                            pe.wait_ge(packed_ready, k.v - 1)
                        for t in range(CCOL):
                            last = pe.matmul(pC[k.slot(2)][:, 0:HI], lo_hot[0][:, t, :], hi_val[0][:, t, :], start=(t == 0), stop=(t == CCOL - 1))
                        last.then_inc(compact, 1)
                    repeat(pe, ALLC, 2, [(0, count), (1, compaction)])
        carve = Carve()
        after = carve([TILES, ALLC])
        keep_c = carve([TILES, ALLC])
        shift = carve([ALLC, TILES + 1])
        delta = carve([ALLC, TILES + 1])
        ge = carve([CHUNKS, GCOLS, TILES + 1])
        dest = carve([ALLC, GCOLS])
        dest_i = carve([ALLC, GCOLS], I32)
        gid = carve([GCOLS])
        gid_i = carve([GCOLS], I32)
        unused = carve([ALLC])
        unused_i = carve([ALLC], I32)
        group_id = carve([3])
        group_i = carve([3], I32)
        sup_i = carve([SORTS, TILES], I32)
        sup_f = carve([2, SORTS, TILES])
        tile_of = carve([3, TILES])
        tile_f = carve([3])
        tile_i = carve([SORTS, 3], I32)
        with ExitStack() as ps:
            p2p, p2, dest_ready, gtile_ready, gt_out, gt_in = (sem("p2p"), sem("p2"), sem("dest_ready"), sem("gtile_ready"),
                                                               sem("gt_out"), sem("gt_in"))
            staged = sem("staged")
            scattered = [sem(f"scattered{i}") for i in range(2)]
            stage_v = [sbe(f"stage_v{i}", [P, GCOLS, GRAN]) for i in range(2)]
            stage_d = [sbe(f"stage_d{i}", [P, GCOLS], I32) for i in range(2)]
            with nc.Block() as block:

                @block.gpsimd
                def _(g):
                    g.iota(gid_i, pattern=[[P, GCOLS]], base=0, channel_multiplier=1).then_inc(p2p, 1)
                    g.iota(group_i, pattern=[[P, 3]], base=0, channel_multiplier=1).then_inc(p2p, 1)
                    for s in range(SORTS):
                        g.iota(unused_i[:, s * CHUNKS:(s + 1) * CHUNKS], pattern=[[GCOLS * P, CHUNKS]],
                               base=s * REGION + GROUPS * GPG, channel_multiplier=0).then_inc(p2p, 1)

                    def scatter(k):
                        sl = k.slot(2)
                        g.wait_ge(staged, k.v + 1)
                        g.nop(nofuse=True)
                        for j in range(GCOLS):
                            g.indirect_dma_start(records, bass.IndirectOffsetOnAxis(ap=stage_d[sl][:, j:j + 1], axis=0),
                                                 stage_v[sl][:, j, :], None).then_inc(scattered[sl], 16)
                    repeat(g, ALLC, 2, [(0, scatter)])
                    for i in range(2):
                        g.wait_ge(scattered[i], 16 * GCOLS * ALLC // 2)

                @block.scalar
                def _(act):
                    act.wait_ge(dest_ready, 1)

                    def stage(k):
                        sl = k.slot(2)
                        if k.past(2):
                            act.wait_ge(scattered[sl], k.round * (16 * GCOLS))
                        act.activation(stage_v[sl].rearrange("p g r -> p (g r)"), packed[:, bass.ds(k.v, 1), :, :].rearrange("p c g r -> p (c g r)"), ACT.Copy)
                        act.copy(stage_d[sl][:, :], dest_i[:, bass.ds(k.v, 1), :].rearrange("p c g -> p (c g)")).then_inc(staged, 1)
                    repeat(act, ALLC, 2, [(0, stage)])

                @block.sync
                def _(sp):
                    sp.wait_ge(gtile_ready, 1)
                    for s in range(SORTS):
                        with nc.allow_non_contiguous_dma(reason="three numbers of a partition"):
                            sp.dma_start(gtile_dram[s, :].rearrange("(q p) -> p q", p=P), tile_i[:, s, :]).then_inc(gt_out, 16)
                    sp.wait_ge(gt_out, 16 * SORTS)
                    sp.dma_start(gtile[0:1, :, :], gtile_dram[:, 0:GROUPS].rearrange("(o s) g -> o s g", o=1)).then_inc(gt_in, 16)
                    sp.wait_ge(gt_in, 16)

                @block.vector
                def _(v):
                    n = [0]

                    def chain(ins):
                        n[0] += 1
                        ins.then_inc(p2, 1)
                        v.wait_ge(p2, n[0])
                    chain(v.memset(keep_c[:, :, :], 1.0))
                    v.memset(keep_c[:, :, 0:1], 0.0)
                    chain(v.memset(keep_c[:, :, CHUNKS:CHUNKS + 1], 0.0))
                    v.wait_ge(p2p, 4)
                    v.tensor_copy(gid, gid_i)
                    v.tensor_copy(group_id, group_i)
                    v.tensor_copy(unused, unused_i)
                    chain(v.tensor_tensor_scan(after.rearrange("p b c -> p (b c)"), keep_c.rearrange("p b c -> p (b c)"),
                                               gran_n[:, :, :].rearrange("p b c -> p (b c)"), 0.0, ALU.mult, ALU.add))
                    for s in range(SORTS):
                        total = after[:, :, s * CHUNKS + CHUNKS - 1]
                        chain(v.tensor_scalar(sup_i[:, s, :], total, float(GPG - 1), None, ALU.add))
                        chain(v.tensor_single_scalar(sup_i[:, s, :], sup_i[:, s, :], GPG.bit_length() - 1, ALU.arith_shift_right))
                        chain(v.tensor_tensor_scan(sup_f[:, 0, s, :], one_row[:, :], sup_i[:, s, :], 0.0, ALU.mult, ALU.add))
                        chain(v.tensor_tensor(sup_f[:, 0, s, :], sup_f[:, 0, s, :], sup_i[:, s, :], ALU.subtract))
                        chain(v.tensor_tensor(tile_of, group_id[:, :, None].to_broadcast([P, 3, TILES]),
                                              sup_f[:, 0, s, None, :].to_broadcast([P, 3, TILES]), ALU.is_ge))
                        chain(v.tensor_reduce(tile_f, tile_of, AX.X, ALU.add))
                        chain(v.tensor_scalar(tile_i[:, s, :], tile_f, -1.0, None, ALU.add))
                        chain(v.tensor_scalar(sup_f[:, 1, s, :], sup_f[:, 0, s, :], float(GPG), float(s * REGION), ALU.mult, ALU.add))
                    v.tensor_copy(tile_i[:, 0, 0:1], tile_i[:, 0, 0:1]).then_inc(gtile_ready, 1)
                    chain(v.tensor_tensor(after, after, gran_n[:, :, :], ALU.subtract))
                    for s in range(SORTS):
                        cs = slice(s * CHUNKS, (s + 1) * CHUNKS)
                        v.tensor_tensor(shift[:, cs, 0:TILES].rearrange("p c b -> p b c"), after[:, :, cs],
                                        sup_f[:, 1, s, :, None].to_broadcast([P, TILES, CHUNKS]), ALU.add)
                    chain(v.tensor_copy(shift[:, :, TILES], unused))
                    chain(v.tensor_tensor(shift[:, :, 0:TILES], shift[:, :, 0:TILES], gran_at[:, :, 0:TILES], ALU.subtract))
                    v.tensor_copy(delta[:, :, 0], shift[:, :, 0])
                    chain(v.tensor_tensor(delta[:, :, 1:], shift[:, :, 1:], shift[:, :, 0:TILES], ALU.subtract))
                    for s in range(SORTS):
                        cs = slice(s * CHUNKS, (s + 1) * CHUNKS)
                        full = [P, CHUNKS, GCOLS, TILES + 1]
                        chain(v.tensor_tensor(ge, gid[:, None, :, None].to_broadcast(full), gran_at[:, cs, None, :].to_broadcast(full), ALU.is_ge))
                        chain(v.tensor_tensor(ge, ge, delta[:, cs, None, :].to_broadcast(full), ALU.mult))
                        chain(v.tensor_reduce(dest[:, cs, :], ge, AX.X, ALU.add))
                    v.tensor_tensor(dest_i, dest, gid[:, None, :].to_broadcast([P, ALLC, GCOLS]), ALU.add).then_inc(dest_ready, 1)

        early.close()
        slot_idx = [sb(f"slot_idx{s}", [P, GROUPS, SUB], I32) for s in range(SORTS)]
        slot_loc = [sb(f"slot_loc{s}", [P, GROUPS, SUB]) for s in range(SORTS)]
        slot_rel = sb("slot_rel", [P, GROUPS, SUB])
        inv_deg = sb("inv_deg", [P, TILES, RELS])
        carve = Carve()
        QG = -(-GROUPS // P)
        rec_in = carve([SORTS, QG, GROUP])
        pk = carve([SORTS, GROUPS, SUB])
        nul = carve([GROUPS * SUB])
        qi = carve([GROUPS * SUB], I32)
        loc_i = carve([GROUPS * SUB], I32)
        rel_i = carve([GROUPS * SUB], I32)
        deg = carve([TILES, RELS])
        node_hot = [carve([SUB, P], BF16) for _ in range(2)]
        rel_hot = [carve([SUB, RELS], BF16) for _ in range(2)]
        with ExitStack() as ps:
            pR = [psum(ps, f"pR{i}", [P, SUB, P]) for i in range(2)]
            pD = [psum(ps, f"pD{i}", [P, 512]) for i in range(2)]
            rec_ld, rec_ps, rec_mv, p3, deg_hot, deg_ps, deg_add = (sem("rec_ld"), sem("rec_ps"), sem("rec_mv"), sem("p3"), sem("deg_hot"),
                                                                    sem("deg_ps"), sem("deg_add"))
            blocks = [(s, q) for s in range(SORTS) for q in range(QG)]
            with nc.Block() as block:

                @block.sync
                def _(sp):
                    for s, q in blocks:
                        m = min(P, GROUPS - q * P)
                        rows = records[s * REGION:s * REGION + GROUPS * GPG, :].rearrange("(g r) w -> g (r w)", r=GPG)
                        sp.dma_start(rec_in[0:m, s, q, :], rows[q * P:q * P + m, :]).then_inc(rec_ld, 16)

                @block.tensor
                def _(pe):
                    pe.wait_ge(rec_ld, 16 * len(blocks))
                    for n, (s, q) in enumerate(blocks):
                        m = min(P, GROUPS - q * P)
                        if n >= 2:
                            pe.wait_ge(rec_mv, n - 1)
                        view = rec_in[0:m, s, q, :].rearrange("g (p j) -> g j p", j=SUB)
                        for j in range(SUB):
                            last = pe.transpose(pR[n % 2][:, j, 0:m], view[:, j, :], ident[0:m, 0:m])
                        last.then_inc(rec_ps, 1)

                    def count(k):
                        pe.wait_ge(deg_hot, k.v + 1)
                        if k.past(2):
                            pe.wait_ge(deg_add, k.v - 1)
                        for c in range(SUB):
                            last = pe.matmul(pD[k.slot(2)][:, 0:RELS], node_hot[k.slot(2)][:, c, :], rel_hot[k.slot(2)][:, c, :],
                                             start=(c == 0), stop=(c == SUB - 1))
                        last.then_inc(deg_ps, 1)
                    repeat(pe, GROUPS, UNROLL, [(0, count)])

                @block.vector
                def _(v):
                    n = [0]

                    def chain(ins):
                        n[0] += 1
                        ins.then_inc(p3, 1)
                        v.wait_ge(p3, n[0])
                    v.memset(deg, 0.0)
                    for i, (s, q) in enumerate(blocks):
                        m = min(P, GROUPS - q * P)
                        v.wait_ge(rec_ps, i + 1)
                        v.tensor_copy(pk[:, s, q * P:q * P + m, :].rearrange("p g j -> p j g"), pR[i % 2][:, :, 0:m]).then_inc(rec_mv, 1)
                    v.wait_ge(rec_mv, len(blocks))
                    for s in range(SORTS):
                        val = pk[:, s, :, :].rearrange("p g j -> p (g j)")
                        loc = slot_loc[s][:, :, :].rearrange("p g j -> p (g j)")
                        row = slot_idx[s][:, :, :].rearrange("p g j -> p (g j)")
                        v.tensor_scalar(nul, val, 0.0, PADLOC, ALU.is_equal, ALU.mult)
                        chain(v.tensor_scalar(qi, val, -1.0, 0.0, ALU.add, ALU.max))
                        v.tensor_single_scalar(row, qi, 7, ALU.arith_shift_right)
                        chain(v.tensor_single_scalar(loc_i, qi, P - 1, ALU.bitwise_and))
                        chain(v.tensor_tensor(loc, loc_i, nul, ALU.add))
                    chain(v.tensor_single_scalar(rel_i, slot_idx[1][:, :, :].rearrange("p g j -> p (g j)"), RELS - 1, ALU.bitwise_and))
                    chain(v.tensor_copy(slot_rel[:, :, :].rearrange("p g j -> p (g j)"), rel_i))

                    def hot(k):
                        sl = k.slot(2)
                        if k.past(2):
                            v.wait_ge(deg_ps, k.v - 1)
                        for c in range(SUB):
                            v.tensor_scalar(node_hot[sl][:, c, :], iota[:, :], slot_loc[1][:, bass.ds(k.v, 1), c], None, ALU.is_equal)
                        v.tensor_tensor(rel_hot[sl], iota[:, None, 0:RELS].to_broadcast([P, SUB, RELS]),
                                        slot_rel[:, bass.ds(k.v, 1), :].rearrange("p g j -> p (g j)")[:, :, None].to_broadcast([P, SUB, RELS]), ALU.is_equal).then_inc(deg_hot, 1)

                    def add(k):
                        b = v.value_load(gtile[0:1, 1, bass.ds(k.v, 1)], min_val=0, max_val=TILES - 1)
                        v.wait_ge(deg_ps, k.v + 1)
                        if k.past(1):
                            v.wait_ge(deg_add, k.v)
                        d = deg[:, bass.ds(b, 1), :].rearrange("p t r -> p (t r)")
                        v.tensor_tensor(d, d, pD[k.slot(2)][:, 0:RELS], ALU.add).then_inc(deg_add, 1)
                    repeat(v, GROUPS, UNROLL, [(0, hot), (1, add)])
                    v.wait_ge(deg_add, GROUPS)
                    chain(v.tensor_scalar(deg, deg, 1.0, None, ALU.max))
                    v.reciprocal(inv_deg[:, :, :], deg)

        carve = Carve(ACCW)
        G = [carve([SUB, TW]) for _ in range(UNROLL)]
        neg = [carve([SUB, P]) for _ in range(2)]
        tm = [carve([HEADS, SUB, P]) for _ in range(2)]
        OT = [carve([SUB, P]) for _ in range(2)]
        WH = [carve([HEADS, SUB, P]) for _ in range(2)]
        idx_ring = [sb(f"idx_ring{i}", [P, SUB], I32) for i in range(UNROLL)]
        tmax = [sb(f"tmax{i}", [P, 2]) for i in range(2)]
        cand = [sb(f"cand{i}", [P, 2]) for i in range(2)]
        cand2 = [sb(f"cand2{i}", [P, 2]) for i in range(2)]
        drop = [sb(f"drop{i}", [P, 2]) for i in range(2)]
        fade = [sb(f"fade{i}", [P, 2]) for i in range(2)]
        ez = [[sb(f"ez{i}{j}", [P, SUB, 2]) for j in range(4)] for i in range(2)]
        ex = [sb(f"ex{i}", [P, SUB, 2]) for i in range(2)]
        with ExitStack() as ps:
            pX = [psum(ps, f"pX{i}", [P, HEADS, SUB, P]) for i in range(2)]
            pA = [psum(ps, f"pA{i}", [P, 512]) for i in range(2)]
            pE = [psum(ps, f"pE{i}", [P, 512]) for i in range(2)]
            idx_ready, neg_ready, tm_ready, tmT_ps, ot_ready, m_ready, fade_ready, ex_ps, z_ready, ex_ready, w_done, agg_ps, acc_done = (
                sem(x) for x in ("idx_ready", "neg_ready", "tm_ready", "tmT_ps", "ot_ready", "m_ready", "fade_ready", "ex_ps", "z_ready",
                                 "ex_ready", "w_done", "agg_ps", "acc_done"))
            b_c, c_c, a_init = sem("b_c"), sem("c_c"), sem("a_init")
            got = [sem(f"got{i}") for i in range(UNROLL)]
            with nc.Block() as block:

                @block.gpsimd
                def _(g):
                    def gather(k):
                        sl = k.slot(UNROLL)
                        g.wait_ge(idx_ready, k.v + 1)
                        if k.past(UNROLL):
                            g.wait_ge(agg_ps, k.v - (UNROLL - 1))
                        g.nop(nofuse=True)
                        for c in range(SUB):
                            g.indirect_dma_start(G[sl][:, c, :], None, wh_table,
                                                 bass.IndirectOffsetOnAxis(ap=idx_ring[sl][:, c:c + 1], axis=0)).then_inc(got[sl], 16)
                    repeat(g, GROUPS, UNROLL, [(0, gather)])

                @block.scalar
                def _(act):
                    def index(k):
                        sl = k.slot(UNROLL)
                        if k.past(UNROLL):
                            act.wait_ge(got[sl], k.round * (16 * SUB))
                        act.copy(idx_ring[sl][:, :], slot_idx[0][:, bass.ds(k.v, 1), :].rearrange("p g j -> p (g j)")).then_inc(idx_ready, 1)

                    def fades(k):
                        act.wait_ge(m_ready, k.v + 1)
                        if k.past(2):
                            act.wait_ge(acc_done, k.v - 1)
                        act.activation(fade[k.slot(2)][:, :], drop[k.slot(2)][:, :], ACT.Exp).then_inc(fade_ready, 1)

                    def exps(k):
                        act.wait_ge(z_ready, k.v + 1)
                        if k.past(2):
                            act.wait_ge(w_done, k.v - 1)
                        act.activation(ex[k.slot(2)][:, :, :], ez[k.slot(2)][3][:, :, :], ACT.Exp).then_inc(ex_ready, 1)

                    def mask(k):
                        sl = k.slot(2)
                        act.wait_ge(neg_ready, k.v + 1)
                        act.wait_ge(got[k.slot(UNROLL)], (k.round + 1) * (16 * SUB))
                        if k.past(2):
                            act.wait_ge(tmT_ps, k.v - 1)
                        for c in range(SUB):
                            for h in range(HEADS):
                                last = act.activation(tm[sl][:, h, c, :], neg[sl][:, c, :], ACT.Identity,
                                                      bias=G[k.slot(UNROLL)][:, c, TCOL + h:TCOL + h + 1])
                        last.then_inc(tm_ready, 1)
                    repeat(act, GROUPS, UNROLL, [(0, index), (3, mask), (4, fades), (4, exps)])

                @block.tensor
                def _(pe):
                    def spread(k):
                        sl = k.slot(2)
                        pe.wait_ge(tm_ready, k.v + 1)
                        if k.past(2):
                            pe.wait_ge(ot_ready, k.v - 1)
                        for h in range(HEADS):
                            for c in range(SUB):
                                last = pe.transpose(pX[sl][:, h, c, :], tm[sl][:, h, c, :], ident[:, :])
                        last.then_inc(tmT_ps, 1)

                    def expand(k):
                        sl = k.slot(2)
                        b = pe.value_load(gtile[0:1, 0, bass.ds(k.v, 1)], min_val=0, max_val=TILES - 1)
                        pe.wait_ge(ot_ready, k.v + 1)
                        pe.wait_ge(m_ready, k.v + 1)
                        if k.past(2):
                            pe.wait_ge(z_ready, k.v - 1)
                        for c in range(SUB):
                            last = pe.matmul(pE[sl][:, 4 * c:4 * c + 4], OT[sl][:, c, :], SM[:, bass.ds(b, 1), :].rearrange("p t c -> p (t c)"),
                                             start=True, stop=True)
                        last.then_inc(ex_ps, 1)

                    def aggregate(k):
                        sl = k.slot(2)
                        pe.wait_ge(w_done, k.v + 1)
                        if k.past(2):
                            pe.wait_ge(acc_done, k.v - 1)
                        for h in range(HEADS):
                            for c in range(SUB):
                                last = pe.matmul(pA[sl][:, h * HW:(h + 1) * HW], WH[sl][:, h, c, :],
                                                 G[k.slot(UNROLL)][:, c, h * HW:(h + 1) * HW], start=(c == 0), stop=(c == SUB - 1))
                        last.then_inc(agg_ps, 1)
                    repeat(pe, GROUPS, UNROLL, [(0, spread), (1, expand), (2, aggregate)])

                @block.vector
                def _(v):
                    v.memset(arena[:, 0:ACCW], 0.0).then_inc(a_init, 1)
                    v.wait_ge(a_init, 1)

                    def hide(k):
                        sl = k.slot(2)
                        if k.past(2):
                            v.wait_ge(tm_ready, k.v - 1)
                        for c in range(SUB):
                            last = v.tensor_scalar(neg[sl][:, c, :], iota[:, :], slot_loc[0][:, bass.ds(k.v, 1), c], -BIG, ALU.not_equal, ALU.mult)
                        last.then_inc(neg_ready, 1)

                    def maxima(k):
                        sl = k.slot(2)
                        b = v.value_load(gtile[0:1, 0, bass.ds(k.v, 1)], min_val=0, max_val=TILES - 1)
                        v.wait_ge(tmT_ps, k.v + 1)
                        v.tensor_reduce(tmax[sl][:, :], pX[sl][:, :, :, :].rearrange("p h c e -> p h (c e)"), AX.X, ALU.max).then_inc(b_c, 1)
                        if k.past(2):
                            v.wait_ge(ex_ps, k.v - 1)
                        v.tensor_scalar(OT[sl], pX[sl][:, 0, :, :], -BIG / 2, None, ALU.is_gt).then_inc(ot_ready, 1)
                        S = SM[:, bass.ds(b, 1), 0:2].rearrange("p t c -> p (t c)")
                        M = SM[:, bass.ds(b, 1), 2:4].rearrange("p t c -> p (t c)")
                        v.wait_ge(b_c, 4 * k.v + 1)
                        v.tensor_tensor(cand[sl][:, :], tmax[sl][:, :], S, ALU.add).then_inc(b_c, 1)
                        v.wait_ge(b_c, 4 * k.v + 2)
                        v.scalar_tensor_tensor(cand2[sl][:, :], cand[sl][:, :], SLOPE, cand[sl][:, :], ALU.mult, ALU.max).then_inc(b_c, 1)
                        v.wait_ge(b_c, 4 * k.v + 3)
                        if k.past(1):
                            v.wait_ge(m_ready, k.v)
                        v.tensor_tensor(tmax[sl][:, :], cand2[sl][:, :], M, ALU.max).then_inc(b_c, 1)
                        v.wait_ge(b_c, 4 * k.v + 4)
                        if k.past(2):
                            v.wait_ge(fade_ready, k.v - 1)
                        v.tensor_tensor(drop[sl][:, :], M, tmax[sl][:, :], ALU.subtract).then_inc(c_m, 1)
                        if k.past(1):
                            v.wait_ge(ex_ps, k.v)
                        v.wait_ge(c_m, k.v + 1)
                        v.tensor_tensor(M, cand2[sl][:, :], M, ALU.max).then_inc(m_ready, 1)

                    def exponents(k):
                        sl = k.slot(2)
                        t = G[k.slot(UNROLL)][:, :, TCOL:TCOL + 2]
                        e = pE[sl][:, 0:4 * SUB].rearrange("p (c w) -> p c w", w=4)
                        z = ez[sl]
                        v.wait_ge(ex_ps, k.v + 1)
                        v.wait_ge(got[k.slot(UNROLL)], (k.round + 1) * (16 * SUB))
                        v.tensor_tensor(z[0][:, :, :], t, e[:, :, 0:2], ALU.add).then_inc(c_c, 1)
                        v.wait_ge(c_c, 3 * k.v + 1)
                        v.scalar_tensor_tensor(z[1][:, :, :], z[0][:, :, :], SLOPE, z[0][:, :, :], ALU.mult, ALU.max).then_inc(c_c, 1)
                        v.wait_ge(c_c, 3 * k.v + 2)
                        v.tensor_tensor(z[2][:, :, :], z[1][:, :, :], e[:, :, 2:4], ALU.subtract).then_inc(c_c, 1)
                        v.wait_ge(c_c, 3 * k.v + 3)
                        if k.past(2):
                            v.wait_ge(ex_ready, k.v - 1)
                        v.tensor_scalar(z[3][:, :, :], z[2][:, :, :], 0.0, None, ALU.min).then_inc(z_ready, 1)

                    def weigh(k):
                        sl = k.slot(2)
                        v.wait_ge(ex_ready, k.v + 1)
                        if k.past(2):
                            v.wait_ge(agg_ps, k.v - 1)
                        for h in range(HEADS):
                            for c in range(SUB):
                                last = v.tensor_scalar(WH[sl][:, h, c, :], iota[:, :], slot_loc[0][:, bass.ds(k.v, 1), c],
                                                       ex[sl][:, c, h:h + 1], ALU.is_equal, ALU.mult)
                        last.then_inc(w_done, 1)

                    def add(k):
                        sl = k.slot(2)
                        b = v.value_load(gtile[0:1, 0, bass.ds(k.v, 1)], min_val=0, max_val=TILES - 1)
                        v.wait_ge(agg_ps, k.v + 1)
                        v.wait_ge(fade_ready, k.v + 1)
                        if k.past(1):
                            v.wait_ge(acc_done, k.v)
                        for h in range(HEADS):
                            a = acc[:, bass.ds(b, 1), h * HW:(h + 1) * HW].rearrange("p t c -> p (t c)")
                            last = v.scalar_tensor_tensor(a, a, fade[sl][:, h:h + 1], pA[sl][:, h * HW:(h + 1) * HW], ALU.mult, ALU.add)
                        last.then_inc(acc_done, 1)
                    c_m = sem("c_m")
                    repeat(v, GROUPS, UNROLL, [(3, maxima), (0, hide), (3, exponents), (4, add), (3, weigh)])

        carve = Carve(ACCW)
        wr = carve([2, RELS * DIM])
        rel_out = [arena[:, 0:RELS * DIM], arena[:, RELS * DIM:2 * RELS * DIM]]
        W0T = sb("W0T", [P, 2, DIM])
        w0 = sb("w0", [P, 2, DIM])
        own = [sb(f"own{i}", [P, TW]) for i in range(2)]
        rden = sb("rden", [P, TILES, HEADS])
        alone = sb("alone", [P, TILES, HEADS])
        with ExitStack() as ps:
            pT = [psum(ps, f"qT{i}", [P, 2, P]) for i in range(1)]
            pO = [psum(ps, f"qO{i}", [P, 512]) for i in range(1)]
            pH = [psum(ps, f"qH{i}", [P, 512]) for i in range(UNROLL)]
            w_ld, own_ready, d_c, x_c, x2_done, st2, st2_done, std2, ln2 = (sem(x) for x in (
                "w_ld", "own_ready", "d_c", "x_c", "x2_done", "st2", "st2_done", "std2", "ln2"))
            own_in = [sem(f"own_in{i}") for i in range(2)]
            own_used = sem("own_used")
            h2_ready, h2T_ps, h2T_ready, root_ps, root_add, rel_ps, w0_ps, w0_ready = (sem(x) for x in (
                "h2_ready", "h2T_ps", "h2T_ready", "root_ps", "root_add", "rel_ps", "w0_ps", "w0_ready"))
            rel_act, rel_dve = sem("rel_act"), sem("rel_dve")
            rel_st = [sem(f"rel_st{i}") for i in range(2)]
            with nc.Block() as block:

                @block.sync
                def _(sp):
                    for k in range(2):
                        sp.dma_start(wr[:, k, :].rearrange("p (r n) -> p r n", r=RELS),
                                     A["L1_gnn_W_r"][:, k * P:(k + 1) * P, :].rearrange("r p n -> p r n")).then_inc(w_ld, 16)
                    sp.dma_start(w0[:, :, :], A["L1_gnn_W0_w"].rearrange("(k p) n -> p k n", p=P)).then_inc(w_ld, 16)
                    sp.dma_start(row2[:, :], A["L1_gnn_W0_b"].rearrange("(o n) -> o n", o=1)).then_inc(w_ld, 16)

                    def own_rows(k):
                        if k.past(2):
                            sp.wait_ge(own_used, k.v - 1)
                        sp.dma_start(own[k.slot(2)][:, :], wh_table.rearrange("(t p) c -> t p c", p=P)[bass.ds(k.v, 1), :, :].rearrange("t p c -> p (t c)")
                                     ).then_inc(own_in[k.slot(2)], 16)
                    repeat(sp, TILES, 2, [(0, own_rows)])

                    def store(k):
                        sp.wait_ge(rel_act, (k.v + 1) * 4)
                        sp.wait_ge(rel_dve, (k.v + 1) * 4)
                        sp.dma_start(rel_table.rearrange("(t p r) n -> t p (r n)", p=P, r=RELS)[bass.ds(k.v, 1), :, :].rearrange("t p c -> p (t c)"),
                                     rel_out[k.slot(2)]).then_inc(rel_st[k.slot(2)], 16)
                    repeat(sp, TILES, 2, [(0, store)])
                    sp.wait_ge(rel_st[0], 16 * (TILES - TILES // 2))
                    sp.wait_ge(rel_st[1], 16 * (TILES // 2))

                @block.vector
                def _(v):
                    den = acc[:, :, :].rearrange("p t (h w) -> p t h w", w=HW)[:, :, :, HD]
                    v.tensor_scalar(alone[:, :, :], den, 0.0, None, ALU.is_equal)
                    v.tensor_scalar(rden[:, :, :], den, 1e-30, None, ALU.max).then_inc(d_c, 1)
                    v.wait_ge(d_c, 1)
                    v.reciprocal(rden[:, :, :], rden[:, :, :]).then_inc(d_c, 1)
                    v.wait_ge(d_c, 2)

                    def residual(k):
                        t = bass.ds(k.v, 1)
                        for h in range(HEADS):
                            x = X[:, t, h * HD:(h + 1) * HD].rearrange("p t d -> p (t d)")
                            last = v.scalar_tensor_tensor(x, acc[:, t, h * HW:h * HW + HD].rearrange("p t d -> p (t d)"),
                                                          rden[:, t, h], x, ALU.mult, ALU.add)
                        last.then_inc(x_c, 1)
                        v.wait_ge(x_c, k.v + 1)
                        v.wait_ge(own_in[k.slot(2)], (k.round + 1) * 16)
                        for h in range(HEADS):
                            x = X[:, t, h * HD:(h + 1) * HD].rearrange("p t d -> p (t d)")
                            last = v.scalar_tensor_tensor(x, own[k.slot(2)][:, h * HW:h * HW + HD], alone[:, t, h], x, ALU.mult, ALU.add)
                        last.then_inc(own_used, 1)

                    def stat(k):
                        v.bn_stats(stats[:, bass.ds(k.v, 1), :].rearrange("p t c -> p (t c)"),
                                   X[:, bass.ds(k.v, 1), :].rearrange("p t d -> p (t d)")).then_inc(st2, 1)
                    repeat(v, TILES, 2, [(0, residual)])
                    v.wait_ge(own_used, TILES)
                    repeat(v, TILES, 2, [(0, stat)])
                    v.wait_ge(st2, TILES)
                    for t in range(TILES):
                        v.bn_aggr(mv[:, t, :], stats[:, t, :]).then_inc(st2_done, 1)
                    v.wait_ge(std2, 1)
                    v.reciprocal(rstd[:, :], rstd[:, :]).then_inc(std2, 1)
                    v.wait_ge(std2, 2)
                    v.scalar_tensor_tensor(nbias[:, :], mv[:, :, 0], -1.0, rstd[:, :], ALU.mult, ALU.mult).then_inc(ln2, 1)
                    v.wait_ge(w0_ps, 1)
                    v.tensor_copy(W0T[:, :, :].rearrange("p k n -> p (k n)"), pO[0][:, :]).then_inc(w0_ready, 1)

                    def move_hT(k):
                        v.wait_ge(h2T_ps, k.v + 1)
                        if k.past(2):
                            v.wait_ge(rel_ps, (k.v - 1) * 8)
                        v.tensor_copy(hT[k.slot(2)][:, :, :], pT[0][:, :, :]).then_inc(h2T_ready, 1)

                    def root(k):
                        v.wait_ge(root_ps, k.v + 1)
                        v.wait_ge(h2_ready, k.v + 1)
                        x = X[:, bass.ds(k.v, 1), :].rearrange("p t d -> p (t d)")
                        v.tensor_tensor(x, x, pO[0][:, 0:DIM], ALU.add).then_inc(root_add, 1)

                    def move_rel(k):
                        if k.past(2):
                            v.wait_ge(rel_st[k.slot(2)], k.round * 16)
                        for j in range(1, 8, 2):
                            v.wait_ge(rel_ps, k.v * 8 + j + 1)
                            v.tensor_copy(rel_out[k.slot(2)][:, j * 512:(j + 1) * 512], pH[j % 4][:, :]).then_inc(rel_dve, 1)
                    repeat(v, TILES, 2, [(0, move_hT), (1, root), (1, move_rel)])

                @block.scalar
                def _(act):
                    act.wait_ge(st2_done, TILES)
                    act.activation(rstd[:, :], mv[:, :, 1], ACT.Sqrt, bias=eps[:, 0:1]).then_inc(std2, 1)
                    act.wait_ge(ln2, 1)

                    def norm(k):
                        if k.past(2):
                            act.wait_ge(h2T_ps, k.v - 1)
                        act.activation(hbuf[k.slot(2)][:, :], X[:, bass.ds(k.v, 1), :].rearrange("p t d -> p (t d)"), ACT.Relu,
                                       bias=nbias[:, bass.ds(k.v, 1)], scale=rstd[:, bass.ds(k.v, 1)]).then_inc(h2_ready, 1)

                    def move_rel(k):
                        if k.past(2):
                            act.wait_ge(rel_st[k.slot(2)], k.round * 16)
                        for j in range(0, 8, 2):
                            act.wait_ge(rel_ps, k.v * 8 + j + 1)
                            act.activation(rel_out[k.slot(2)][:, j * 512:(j + 1) * 512], pH[j % 4][:, :], ACT.Copy).then_inc(rel_act, 1)
                    repeat(act, TILES, 2, [(0, norm), (2, move_rel)])

                @block.tensor
                def _(pe):
                    pe.wait_ge(w_ld, 64)
                    for k in range(2):
                        for m in range(2):
                            last = pe.transpose(pO[0][:, k * DIM + m * P:k * DIM + (m + 1) * P], w0[:, m, k * P:(k + 1) * P], ident[:, :])
                    last.then_inc(w0_ps, 1)
                    pe.wait_ge(w0_ready, 1)

                    def transpose_h(k):
                        pe.wait_ge(h2_ready, k.v + 1)
                        if k.past(1):
                            pe.wait_ge(h2T_ready, k.v)
                        for j in range(2):
                            last = pe.transpose(pT[0][:, j, :], hbuf[k.slot(2)][:, j * P:(j + 1) * P], ident[:, :])
                        last.then_inc(h2T_ps, 1)

                    def products(k):
                        h = hT[k.slot(2)]
                        pe.wait_ge(h2T_ready, k.v + 1)
                        if k.past(1):
                            pe.wait_ge(root_add, k.v)
                        pe.matmul(pO[0][:, 0:DIM], h[:, 0, :], W0T[:, 0, :], start=True, stop=False)
                        pe.matmul(pO[0][:, 0:DIM], h[:, 1, :], W0T[:, 1, :], start=False, stop=False)
                        pe.matmul(pO[0][:, 0:DIM], ones_row[0:1, :], row2[0:1, :], start=False, stop=True).then_inc(root_ps, 1)
                        for j in range(8):
                            moved = rel_dve if j % 2 else rel_act
                            if k.past(1) or j >= 4:
                                pe.wait_ge(moved, k.v * 4 + (j // 2 - 1))
                            for i in range(2):
                                last = pe.matmul(pH[j % 4][:, :], h[:, i, :], wr[:, i, j * 512:(j + 1) * 512], start=(i == 0), stop=(i == 1))
                            last.then_inc(rel_ps, 1)
                    repeat(pe, TILES, 2, [(0, transpose_h), (1, products)])

        carve = Carve()
        G1 = [carve([SUB, DIM]) for _ in range(UNROLL)]
        hot = [carve([SUB, P], BF16) for _ in range(2)]
        rhot = [carve([SUB, RELS]) for _ in range(2)]
        rprod = [carve([SUB, RELS]) for _ in range(2)]
        OT1 = [carve([SUB, P]) for _ in range(2)]
        W1 = [carve([SUB, P]) for _ in range(2)]
        wt = [carve([SUB]) for _ in range(2)]
        with ExitStack() as ps:
            qX = [psum(ps, f"rX{i}", [P, SUB, P], BF16) for i in range(2)]
            qE = [psum(ps, f"rE{i}", [P, 512]) for i in range(2)]
            qA = [psum(ps, f"rA{i}", [P, 512]) for i in range(2)]
            idx1, hot1, hotT, ot1, deg_ex, w_c, w1_done, agg1, add1 = (sem(x) for x in (
                "idx1", "hot1", "hotT", "ot1", "deg_ex", "w_c", "w1_done", "agg1", "add1"))
            got1 = [sem(f"got1{i}") for i in range(UNROLL)]
            out_done = sem("out_done")
            with nc.Block() as block:

                @block.gpsimd
                def _(g):
                    def gather(k):
                        sl = k.slot(UNROLL)
                        g.wait_ge(idx1, k.v + 1)
                        if k.past(UNROLL):
                            g.wait_ge(agg1, k.v - (UNROLL - 1))
                        g.nop(nofuse=True)
                        for c in range(SUB):
                            g.indirect_dma_start(G1[sl][:, c, :], None, rel_table,
                                                 bass.IndirectOffsetOnAxis(ap=idx_ring[sl][:, c:c + 1], axis=0)).then_inc(got1[sl], 16)
                    repeat(g, GROUPS, UNROLL, [(0, gather)])

                @block.scalar
                def _(act):
                    def index(k):
                        sl = k.slot(UNROLL)
                        if k.past(UNROLL):
                            act.wait_ge(got1[sl], k.round * (16 * SUB))
                        act.copy(idx_ring[sl][:, :], slot_idx[1][:, bass.ds(k.v, 1), :].rearrange("p g j -> p (g j)")).then_inc(idx1, 1)

                    def move(k):
                        act.wait_ge(hotT, k.v + 1)
                        if k.past(2):
                            act.wait_ge(deg_ex, k.v - 1)
                        act.activation(OT1[k.slot(2)], qX[k.slot(2)][:, :, :], ACT.Copy).then_inc(ot1, 1)
                    repeat(act, GROUPS, UNROLL, [(2, move), (0, index)])

                @block.tensor
                def _(pe):
                    def spread(k):
                        sl = k.slot(2)
                        pe.wait_ge(hot1, k.v + 1)
                        if k.past(2):
                            pe.wait_ge(ot1, k.v - 1)
                        for c in range(SUB):
                            last = pe.transpose(qX[sl][:, c, :], hot[sl][:, c, :], identb[:, :])
                        last.then_inc(hotT, 1)

                    def expand(k):
                        sl = k.slot(2)
                        b = pe.value_load(gtile[0:1, 1, bass.ds(k.v, 1)], min_val=0, max_val=TILES - 1)
                        pe.wait_ge(ot1, k.v + 1)
                        if k.past(2):
                            pe.wait_ge(w1_done, k.v - 1)
                        for c in range(SUB):
                            last = pe.matmul(qE[sl][:, c * RELS:(c + 1) * RELS], OT1[sl][:, c, :],
                                             inv_deg[:, bass.ds(b, 1), :].rearrange("p t r -> p (t r)"), start=True, stop=True)
                        last.then_inc(deg_ex, 1)

                    def aggregate(k):
                        sl = k.slot(2)
                        pe.wait_ge(w1_done, k.v + 1)
                        pe.wait_ge(got1[k.slot(UNROLL)], (k.round + 1) * (16 * SUB))
                        if k.past(2):
                            pe.wait_ge(add1, k.v - 1)
                        for c in range(SUB):
                            last = pe.matmul(qA[sl][:, 0:DIM], W1[sl][:, c, :], G1[k.slot(UNROLL)][:, c, :], start=(c == 0), stop=(c == SUB - 1))
                        last.then_inc(agg1, 1)
                    repeat(pe, GROUPS, UNROLL, [(0, spread), (1, expand), (2, aggregate)])

                @block.vector
                def _(v):
                    def hots1(k):
                        sl = k.slot(2)
                        if k.past(2):
                            v.wait_ge(hotT, k.v - 1)
                            v.wait_ge(w_c, 2 * (k.v - 1))
                        for c in range(SUB):
                            v.tensor_scalar(hot[sl][:, c, :], iota[:, :], slot_loc[1][:, bass.ds(k.v, 1), c], None, ALU.is_equal)
                        v.tensor_tensor(rhot[sl], iota[:, None, 0:RELS].to_broadcast([P, SUB, RELS]),
                                        slot_rel[:, bass.ds(k.v, 1), :].rearrange("p g j -> p (g j)")[:, :, None].to_broadcast([P, SUB, RELS]), ALU.is_equal).then_inc(hot1, 1)

                    def weigh(k):
                        sl = k.slot(2)
                        v.wait_ge(deg_ex, k.v + 1)
                        v.wait_ge(hot1, k.v + 1)
                        if k.past(2):
                            v.wait_ge(w1_done, k.v - 1)
                        v.tensor_tensor(rprod[sl], rhot[sl], qE[sl][:, 0:SUB * RELS].rearrange("p (c r) -> p c r", r=RELS), ALU.mult).then_inc(w_c, 1)
                        v.wait_ge(w_c, 2 * k.v + 1)
                        v.tensor_reduce(wt[sl], rprod[sl], AX.X, ALU.add).then_inc(w_c, 1)
                        v.wait_ge(w_c, 2 * k.v + 2)
                        if k.past(2):
                            v.wait_ge(agg1, k.v - 1)
                        for c in range(SUB):
                            last = v.tensor_scalar(W1[sl][:, c, :], iota[:, :], slot_loc[1][:, bass.ds(k.v, 1), c], wt[sl][:, c:c + 1], ALU.is_equal, ALU.mult)
                        last.then_inc(w1_done, 1)

                    def add(k):
                        sl = k.slot(2)
                        b = v.value_load(gtile[0:1, 1, bass.ds(k.v, 1)], min_val=0, max_val=TILES - 1)
                        v.wait_ge(agg1, k.v + 1)
                        if k.past(1):
                            v.wait_ge(add1, k.v)
                        x = X[:, bass.ds(b, 1), :].rearrange("p t d -> p (t d)")
                        v.tensor_tensor(x, x, qA[sl][:, 0:DIM], ALU.add).then_inc(add1, 1)
                    repeat(v, GROUPS, UNROLL, [(2, weigh), (0, hots1), (3, add)])

                @block.sync
                def _(sp):
                    sp.wait_ge(add1, GROUPS)
                    sp.dma_start(out[0:FULL * P, :].rearrange("(t p) d -> p t d", p=P), X[:, 0:FULL, :]).then_inc(out_done, 16)
                    sp.dma_start(out[FULL * P:NODES, :], X[0:REST, FULL, :]).then_inc(out_done, 16)
                    sp.wait_ge(out_done, 32)



_INS = ["x", "src", "dst", "edge_type_16", "L0_gnn_W_w", "L0_gnn_W_b", "L0_gnn_a", "L1_gnn_W_r", "L1_gnn_W0_w", "L1_gnn_W0_b"]


def kernel(**inputs):
    import concourse.bacc as bacc
    from concourse.bass_utils import run_bass_kernel_spmd as run

    nc = bacc.Bacc("TRN2", target_bir_lowering=False, num_devices=1)
    arrays, args = {}, {}
    for name in _INS:
        a = np.ascontiguousarray(inputs[name])
        arrays[f"in_{name}"] = a
        args[name] = nc.dram_tensor(f"in_{name}", a.shape, mybir.dt.from_np(a.dtype), kind="ExternalInput").ap()
    out = nc.dram_tensor("out", (NODES, DIM), F32, kind="ExternalOutput").ap()
    build(nc, args, out)
    r = run(nc, [arrays], core_ids=[0])
    return r.results[0]["out"]
```

```python
from contextlib import ExitStack

import numpy as np

import concourse.bass as bass
from concourse import mybir

F32 = mybir.dt.float32
BF16 = mybir.dt.bfloat16
I32 = mybir.dt.int32
ALU = mybir.AluOpType
ACT = mybir.ActivationFunctionType
AX = mybir.AxisListType

P = 128
NODES, DIM, HEADS, HD, RELS, EDGES = 6250, 256, 2, 128, 16, 106250
TILES = -(-NODES // P)
FULL = NODES // P
REST = NODES - FULL * P
EPART = 125
ECOL = EDGES // EPART
CCOL = 50
CHUNKS = ECOL // CCOL
SORTS = 2
ALLC = SORTS * CHUNKS
GRAN = 8
GCOLS = -(-(EPART * CCOL + TILES * (GRAN - 1)) // (P * GRAN))
HI = GCOLS * GRAN
SUB = 4
GROUP = SUB * P
GPG = GROUP // GRAN
UNROLL = 4
MAXGRAN = (EDGES + CHUNKS * TILES * (GRAN - 1)) // GRAN
GROUPS = (MAXGRAN + TILES * (GPG - 1)) // GPG
GROUPS = -(-GROUPS // UNROLL) * UNROLL
REGION = GROUPS * GPG + CHUNKS * GCOLS * P
PADLOC = 1000.0
BIG = float(2.0 ** 100)
SLOPE = 0.2
EPS = 1e-5
TW = 260
HW = HD + 1
TCOL = 2 * HW


class Step:

    def __init__(self, v, least, rnd):
        self.v, self.least, self.round = v, least, rnd

    def slot(self, ring):
        return self.least % ring

    def past(self, n):
        return self.least >= n


def repeat(eng, n, unroll, stages):
    lags = [lag for lag, _ in stages]
    first = -(-(max(lags) + unroll) // unroll) * unroll
    rounds = max(0, (n - first) // unroll)

    def static(j):
        for lag, fn in stages:
            if 0 <= j - lag < n:
                fn(Step(j - lag, j - lag, (j - lag) // unroll))

    for j in range(first):
        static(j)
    if rounds:
        with eng.Fori(0, rounds) as it:
            for u in range(unroll):
                for lag, fn in stages:
                    base = first + u - lag
                    fn(Step(it * unroll + base, base, it + base // unroll))
    for j in range(first + rounds * unroll, n + max(lags)):
        static(j)


def build(nc, A, out):
    ctx = ExitStack()
    with ctx:
        def sb(name, shape, dt=F32):
            return ctx.enter_context(nc.sbuf_tensor(name, shape, dt))

        def sem(name):
            return ctx.enter_context(nc.semaphore(name))

        wh_table = nc.dram_tensor("wh_table", [TILES * P, TW], F32, kind="Internal").ap()
        rel_table = nc.dram_tensor("rel_table", [TILES * P * RELS, DIM], F32, kind="Internal").ap()
        records = nc.dram_tensor("records", [SORTS * REGION, GRAN], F32, kind="Internal").ap()
        gtile_dram = nc.dram_tensor("gtile_dram", [SORTS, 3 * P], I32, kind="Internal").ap()

        X = sb("X", [P, TILES, DIM])
        ident = sb("ident", [P, P])
        identb = sb("identb", [P, P], BF16)
        iota = sb("iota", [P, P])
        iotab = sb("iotab", [P, P], BF16)
        gtile = sb("gtile", [1, SORTS, GROUPS], I32)
        SM = sb("SM", [P, TILES, 4])
        mv = sb("mv", [P, TILES, 2])
        rstd = sb("rstd", [P, TILES])
        nbias = sb("nbias", [P, TILES])
        eps = sb("eps", [P, 1])
        ones_row = sb("ones_row", [1, P])
        row1 = sb("row1", [1, TW + 2])
        row2 = sb("row2", [1, DIM])
        ARENA = 29190
        arena = sb("arena", [P, ARENA])
        ACCW = TILES * TCOL
        acc = arena[:, 0:ACCW].rearrange("p (t c) -> p t c", c=TCOL)

        class Carve:
            def __init__(self, at=0):
                self.at = at

            def __call__(self, shape, dt=F32):
                n = int(np.prod(shape))
                w = n if dt in (F32, I32) else -(-n // 2)
                v = arena[:, self.at:self.at + w]
                if dt is not F32:
                    v = v.bitcast(dt)
                self.at += w
                assert self.at <= ARENA, self.at
                if len(shape) == 1:
                    return v
                names = "abcd"[:len(shape)]
                return v.rearrange(f"p ({' '.join(names)}) -> p {' '.join(names)}",
                                   **{m: s for m, s in zip(names[1:], shape[1:])})

        def psum(stack, name, shape, dt=F32):
            return stack.enter_context(nc.psum_tensor(name, shape, dt))

        carve = Carve()
        tile_hot = [carve([TILES, CCOL], BF16) for _ in range(2)]
        rank = [carve([TILES, CCOL]) for _ in range(2)]
        lo_hot = [carve([CCOL, P]) for _ in range(1)]
        hi_val = [carve([CCOL, HI]) for _ in range(1)]
        scan_keep = carve([TILES, CCOL], BF16)
        edge_tile = carve([SORTS, ECOL])
        edge_val = carve([SORTS, ECOL])
        edge_i = carve([3, ECOL], I32)
        ints = carve([2, ECOL], I32)
        zero = carve([512])
        abc = carve([2 * HD])
        w_in = carve([2, DIM])
        prod = carve([HD])
        early = ctx.enter_context(ExitStack())

        def sbe(name, shape, dt=F32):
            return early.enter_context(nc.sbuf_tensor(name, shape, dt))

        hbuf = [sb(f"hbuf{i}", [P, DIM]) for i in range(2)]
        hT = [sb(f"hT{i}", [P, 2, P]) for i in range(2)]
        proj = [sb(f"proj{i}", [P, TW + 2]) for i in range(2)]
        stats = sb("stats", [P, TILES, 6])
        Wx = sbe("Wx", [P, 2, TW + 2])
        b_in = sbe("b_in", [1, DIM])
        below = sbe("below", [P, P], BF16)
        allone = sbe("allone", [P, P], BF16)
        iota_i = sbe("iota_i", [P, P], I32)
        totals = [sbe(f"totals{i}", [P, TILES], BF16) for i in range(2)]
        gran_i = [sbe(f"gran_i{i}", [P, 2, TILES], I32) for i in range(2)]
        gran_f = [sbe(f"gran_f{i}", [P, 2, TILES]) for i in range(2)]
        pos_f = [sbe(f"pos_f{i}", [P, CCOL]) for i in range(2)]
        pos_i = [sbe(f"pos_i{i}", [P, 4, CCOL], I32) for i in range(2)]
        gran_n = sbe("gran_n", [P, TILES, ALLC])
        gran_at = sbe("gran_at", [P, ALLC, TILES + 1])
        packed = sbe("packed", [P, ALLC, GCOLS, GRAN])
        one_row = sbe("one_row", [P, TILES])


        with ExitStack() as ps:
            pT = [psum(ps, f"pT{i}", [P, 2, P]) for i in range(2)]
            pP = [psum(ps, f"pP{i}", [P, 512]) for i in range(2)]
            pB = [psum(ps, f"pB{i}", [P, 512]) for i in range(2)]
            pC = [psum(ps, f"pC{i}", [P, 512]) for i in range(2)]
            edges_in, weights_in, x_in, zeroed = sem("edges_in"), sem("weights_in"), sem("x_in"), sem("zeroed")
            pool_c, consts, dve_c = sem("pool_c"), sem("consts"), sem("dve_c")
            x_padded, stats_done, std_done, ln_ready = (sem("x_padded"), sem("stats_done"), sem("std_done"), sem("ln_ready"))
            w_ready = sem("w_ready")
            h_ready, hT_ps, hT_ready, proj_ps, proj_ready = (sem("h_ready"), sem("hT_ps"), sem("hT_ready"),
                                                             sem("proj_ps"), sem("proj_ready"))
            proj_out = [sem(f"proj_out{i}") for i in range(2)]
            st_a = sem("st_a")
            sort_a, sort_c, sort_d = sem("sort_a"), sem("sort_c"), sem("sort_d")
            counted, ranked_in, hots, compact, packed_ready = (sem("counted"), sem("totals_ready"), sem("hots"),
                                                               sem("compact"), sem("packed_ready"))
            with nc.Block() as block:

                @block.sync
                def _(sp):
                    for n, name in enumerate(("src", "dst", "edge_type_16")):
                        sp.dma_start(edge_i[0:EPART, n, :], A[name].rearrange("(p c) -> p c", c=ECOL)).then_inc(edges_in, 16)
                    sp.wait_ge(x_padded, 1)
                    sp.dma_start(X[:, 0:FULL, :], A["x"][0:FULL * P, :].rearrange("(t p) d -> p t d", p=P)).then_inc(x_in, 16)
                    sp.dma_start(X[0:REST, FULL, :], A["x"][FULL * P:NODES, :]).then_inc(x_in, 16)
                    sp.dma_start(w_in[:, :, :], A["L0_gnn_W_w"].rearrange("(k p) n -> p k n", p=P)).then_inc(weights_in, 16)
                    sp.dma_start(abc, A["L0_gnn_a"].rearrange("(o n) -> o n", o=1).to_broadcast([P, 2 * HD])).then_inc(weights_in, 16)
                    sp.dma_start(b_in[:, :], A["L0_gnn_W_b"].rearrange("(o n) -> o n", o=1)).then_inc(weights_in, 16)
                    sp.wait_ge(x_padded, 2)
                    for s in range(SORTS):
                        rows = records[s * REGION:s * REGION + GROUPS * GPG, :].rearrange("(g r) w -> g (r w)", r=GPG)
                        for g in range(0, GROUPS, P):
                            m = min(P, GROUPS - g)
                            sp.dma_start(rows[g:g + m, :], zero[0:m, :]).then_inc(zeroed, 16)

                    def store(k):
                        sp.wait_ge(proj_ready, k.v + 1)
                        sp.dma_start(wh_table.rearrange("(t p) c -> t p c", p=P)[bass.ds(k.v, 1), :, :].rearrange("t p c -> p (t c)"),
                                     proj[k.slot(2)][:, 0:TW]).then_inc(proj_out[k.slot(2)], 16)
                    repeat(sp, TILES, 2, [(0, store)])
                    sp.wait_ge(proj_out[0], 16 * (TILES - TILES // 2))
                    sp.wait_ge(proj_out[1], 16 * (TILES // 2))
                    sp.wait_ge(zeroed, 16 * SORTS * -(-GROUPS // P))

                @block.gpsimd
                def _(g):
                    g.iota(iota_i[:, :], pattern=[[1, P]], base=0, channel_multiplier=0).then_inc(pool_c, 1)
                    g.memset(ident[:, :], 0.0).then_inc(pool_c, 1)
                    g.memset(below[:, :], 1.0).then_inc(pool_c, 1)
                    g.wait_ge(pool_c, 3)
                    g.affine_select(out=ident[:, :], in_=ident[:, :], compare_op=ALU.not_equal, fill=1.0, base=0,
                                    pattern=[[-1, P]], channel_multiplier=1).then_inc(pool_c, 1)
                    g.affine_select(out=below[:, :], in_=below[:, :], compare_op=ALU.is_gt, fill=0.0, base=0,
                                    pattern=[[1, P]], channel_multiplier=-1).then_inc(pool_c, 1)

                @block.scalar
                def _(act):
                    act.wait_ge(stats_done, TILES)
                    act.activation(rstd[:, :], mv[:, :, 1], ACT.Sqrt, bias=eps[:, 0:1]).then_inc(std_done, 1)
                    act.wait_ge(ln_ready, 1)

                    def norm(k):
                        if k.past(2):
                            act.wait_ge(hT_ps, k.v - 1)
                        act.activation(hbuf[k.slot(2)][:, :], X[:, bass.ds(k.v, 1), :].rearrange("p t d -> p (t d)"), ACT.Relu,
                                       bias=nbias[:, bass.ds(k.v, 1)], scale=rstd[:, bass.ds(k.v, 1)]).then_inc(h_ready, 1)

                    def move_hT(k):
                        act.wait_ge(hT_ps, k.v + 1)
                        if k.past(2):
                            act.wait_ge(proj_ps, k.v - 1)
                        act.activation(hT[k.slot(2)][:, :, :], pT[k.slot(2)][:, :, :], ACT.Copy).then_inc(hT_ready, 1)

                    def move_proj(k):
                        act.wait_ge(proj_ps, k.v + 1)
                        if k.past(2):
                            act.wait_ge(proj_out[k.slot(2)], k.round * 16)
                        act.activation(proj[k.slot(2)][:, 0:TW], pP[k.slot(2)][:, 0:TW], ACT.Copy)
                        act.activation(SM[:, bass.ds(k.v, 1), 0:2].rearrange("p t c -> p (t c)"), pP[k.slot(2)][:, TW:TW + 2], ACT.Copy).then_inc(proj_ready, 1)
                    repeat(act, TILES, 2, [(0, norm), (1, move_hT), (2, move_proj)])

                    def move_packed(k):
                        act.wait_ge(compact, k.v + 1)
                        act.activation(packed[:, bass.ds(k.v, 1), :, :].rearrange("p c g r -> p (c g r)"),
                                       pC[k.slot(2)][:, 0:HI], ACT.Copy).then_inc(packed_ready, 1)
                    repeat(act, ALLC, 2, [(0, move_packed)])

                def layernorm_stats(v):
                    def one(k):
                        v.bn_stats(stats[:, bass.ds(k.v, 1), :].rearrange("p t c -> p (t c)"),
                                   X[:, bass.ds(k.v, 1), :].rearrange("p t d -> p (t d)")).then_inc(st_a, 1)
                    repeat(v, TILES, 2, [(0, one)])
                    v.wait_ge(st_a, TILES)
                    for t in range(TILES):
                        v.bn_aggr(mv[:, t, :], stats[:, t, :]).then_inc(stats_done, 1)
                    v.wait_ge(std_done, 1)
                    v.reciprocal(rstd[:, :], rstd[:, :]).then_inc(std_done, 1)
                    v.wait_ge(std_done, 2)
                    v.scalar_tensor_tensor(nbias[:, :], mv[:, :, 0], -1.0, rstd[:, :], ALU.mult, ALU.mult).then_inc(ln_ready, 1)

                @block.vector
                def _(v):
                    n = [0]

                    def chain(ins):
                        n[0] += 1
                        ins.then_inc(dve_c, 1)
                        v.wait_ge(dve_c, n[0])

                    v.memset(X[:, FULL, :], 0.0).then_inc(x_padded, 1)
                    v.memset(zero, 0.0).then_inc(x_padded, 1)
                    v.memset(eps[:, :], EPS)
                    v.memset(ones_row[:, :], 1.0)
                    v.memset(allone[:, :], 1.0)
                    v.memset(one_row[:, :], 1.0)
                    v.memset(SM[:, :, 2:4], -BIG)
                    v.memset(scan_keep[:, :, :], 1.0)
                    v.memset(edge_tile[:, :, :], -1.0)
                    v.memset(edge_val[:, :, :], 0.0)
                    v.memset(Wx[:, :, :], 0.0)
                    chain(v.memset(row1[:, :], 0.0))
                    v.memset(scan_keep[:, :, 0:1], 0.0)
                    v.memset(row1[:, HD:HD + 1], 1.0)
                    v.memset(row1[:, HW + HD:HW + HD + 1], 1.0)
                    v.wait_ge(pool_c, 5)
                    v.tensor_copy(iota[:, :], iota_i[:, :])
                    v.tensor_copy(identb[:, :], ident[:, :])
                    v.tensor_copy(iotab[:, :], iota_i[:, :])
                    E = slice(0, EPART)
                    v.wait_ge(edges_in, 48)
                    v.tensor_single_scalar(ints[E, 0, :], edge_i[E, 0, :], 7, ALU.arith_shift_right)
                    chain(v.tensor_single_scalar(ints[E, 1, :], edge_i[E, 0, :], 127, ALU.bitwise_and))
                    v.tensor_copy(edge_tile[E, 0, :], ints[E, 0, :])
                    chain(v.scalar_tensor_tensor(edge_val[E, 0, :], edge_i[E, 1, :], float(P), ints[E, 1, :], ALU.mult, ALU.add))
                    chain(v.tensor_scalar(edge_val[E, 0, :], edge_val[E, 0, :], 1.0, None, ALU.add))
                    v.scalar_tensor_tensor(edge_val[E, 1, :], edge_i[E, 0, :], float(RELS), edge_i[E, 2, :], ALU.mult, ALU.add)
                    v.tensor_single_scalar(ints[E, 0, :], edge_i[E, 1, :], 7, ALU.arith_shift_right)
                    chain(v.tensor_single_scalar(ints[E, 1, :], edge_i[E, 1, :], 127, ALU.bitwise_and))
                    v.tensor_copy(edge_tile[E, 1, :], ints[E, 0, :])
                    chain(v.scalar_tensor_tensor(edge_val[E, 1, :], edge_val[E, 1, :], float(P), ints[E, 1, :], ALU.mult, ALU.add))
                    chain(v.tensor_scalar(edge_val[E, 1, :], edge_val[E, 1, :], 1.0, None, ALU.add))
                    v.wait_ge(weights_in, 48)
                    for k in range(3):
                        w_rows, w_to = (w_in[:, k, :], Wx[:, k, :]) if k < 2 else (b_in[0:1, :], row1[0:1, :])
                        q = slice(0, P if k < 2 else 1)
                        for h in range(HEADS):
                            v.tensor_copy(w_to[:, h * HW:h * HW + HD], w_rows[:, h * HD:(h + 1) * HD])
                            for c, a in ((TCOL + h, HD), (TW + h, 0)):
                                chain(v.tensor_tensor_reduce(out=prod[q], in0=w_rows[:, h * HD:(h + 1) * HD], in1=abc[q, a:a + HD],
                                                             scale=1.0, scalar=0.0, op0=ALU.mult, op1=ALU.add,
                                                             accum_out=w_to[:, c:c + 1]))
                    v.tensor_copy(row1[0:1, HD:HD + 1], row1[0:1, HD:HD + 1]).then_inc(w_ready, 1)
                    v.wait_ge(x_in, 32)
                    layernorm_stats(v)

                    def count(k):
                        sl = k.slot(2)
                        s = bass.ds(k.v * CCOL, CCOL)
                        keys = edge_tile.rearrange("p s c -> p (s c)")[:, s]
                        if k.past(2):
                            v.wait_ge(hots, k.v - 1)
                        v.tensor_tensor(tile_hot[sl], keys[:, None, :].to_broadcast([P, TILES, CCOL]),
                                        iota[:, 0:TILES, None].to_broadcast([P, TILES, CCOL]), ALU.is_equal).then_inc(sort_a, 1)
                        v.wait_ge(sort_a, 2 * k.v + 1)
                        v.tensor_tensor_scan(rank[sl].rearrange("p b t -> p (b t)"), scan_keep.rearrange("p b t -> p (b t)"),
                                             tile_hot[sl].rearrange("p b t -> p (b t)"), 0.0, ALU.mult, ALU.add).then_inc(sort_a, 1)
                        v.wait_ge(sort_a, 2 * k.v + 2)
                        v.tensor_copy(totals[sl][:, :], rank[sl][:, :, CCOL - 1]).then_inc(ranked_in, 1)

                    def place(k):
                        sl = k.slot(2)
                        s = bass.ds(k.v * CCOL, CCOL)
                        vals = edge_val.rearrange("p s c -> p (s c)")[:, s]
                        gi, gf = gran_i[sl], gran_f[sl]
                        step = [0]

                        def link(ins):
                            step[0] += 1
                            ins.then_inc(sort_c, 1)
                            v.wait_ge(sort_c, 9 * k.v + step[0])
                        v.wait_ge(counted, k.v + 1)
                        base, cnt = pB[sl][:, 0:TILES], pB[sl][:, TILES:2 * TILES]
                        link(v.tensor_scalar(gi[:, 0, :], cnt, float(GRAN - 1), None, ALU.add))
                        link(v.tensor_single_scalar(gi[:, 1, :], gi[:, 0, :], 3, ALU.arith_shift_right))
                        v.tensor_scalar(gran_n[:, :, bass.ds(k.v, 1)].rearrange("p b c -> p (b c)"), gi[:, 1, :], 0.0, None, ALU.add)
                        link(v.tensor_tensor_scan(gf[:, 0, :], one_row[:, :], gi[:, 1, :], 0.0, ALU.mult, ALU.add))
                        v.tensor_scalar(gran_at[:, bass.ds(k.v, 1), TILES:TILES + 1].rearrange("p c b -> p (c b)"), gf[:, 0, TILES - 1:TILES], 0.0, None, ALU.add)
                        link(v.tensor_tensor(gf[:, 1, :], gf[:, 0, :], gi[:, 1, :], ALU.subtract))
                        v.tensor_scalar(gran_at[:, bass.ds(k.v, 1), 0:TILES].rearrange("p c b -> p (c b)"), gf[:, 1, :], 0.0, None, ALU.add)
                        link(v.scalar_tensor_tensor(gf[:, 0, :], gf[:, 1, :], float(GRAN), base, ALU.mult, ALU.add))
                        link(v.tensor_tensor(rank[sl], rank[sl], gf[:, 0, :, None].to_broadcast([P, TILES, CCOL]), ALU.add))
                        link(v.tensor_tensor(rank[sl], rank[sl], tile_hot[sl], ALU.mult))
                        link(v.tensor_reduce(pos_f[sl][:, :], rank[sl].rearrange("p b t -> p t b"), AX.X, ALU.add))
                        pi = pos_i[sl]
                        link(v.tensor_scalar(pi[:, 0, :], pos_f[sl][:, :], -1.0, 0.0, ALU.add, ALU.max))
                        v.tensor_scalar(pi[:, 1, :], pi[:, 0, :], 3, P - 1, ALU.arith_shift_right, ALU.bitwise_and)
                        v.tensor_scalar(pi[:, 2, :], pi[:, 0, :], 10, 3, ALU.arith_shift_right, ALU.logical_shift_left)
                        v.tensor_single_scalar(pi[:, 3, :], pi[:, 0, :], GRAN - 1, ALU.bitwise_and).then_inc(sort_d, 1)
                        v.wait_ge(sort_d, 3 * k.v + 1)
                        v.tensor_tensor(pi[:, 3, :], pi[:, 3, :], pi[:, 2, :], ALU.bitwise_or).then_inc(sort_d, 1)
                        v.wait_ge(sort_d, 3 * k.v + 2)
                        if k.past(1):
                            v.wait_ge(compact, k.v)
                        v.tensor_tensor(hi_val[0], iota[:, None, 0:HI].to_broadcast([P, CCOL, HI]),
                                        pi[:, 3, :, None].to_broadcast([P, CCOL, HI]), ALU.is_equal).then_inc(sort_d, 1)
                        v.tensor_tensor(lo_hot[0], iota[:, None, :].to_broadcast([P, CCOL, P]),
                                        pi[:, 1, :, None].to_broadcast([P, CCOL, P]), ALU.is_equal)
                        v.wait_ge(sort_d, 3 * k.v + 3)
                        v.tensor_tensor(hi_val[0], hi_val[0], vals[:, :, None].to_broadcast([P, CCOL, HI]), ALU.mult).then_inc(hots, 1)

                    repeat(v, ALLC, 2, [(0, count), (1, place)])

                @block.tensor
                def _(pe):
                    pe.wait_ge(w_ready, 1)

                    def transpose_h(k):
                        pe.wait_ge(h_ready, k.v + 1)
                        if k.past(2):
                            pe.wait_ge(hT_ready, k.v - 1)
                        for j in range(2):
                            last = pe.transpose(pT[k.slot(2)][:, j, :], hbuf[k.slot(2)][:, j * P:(j + 1) * P], ident[:, :])
                        last.then_inc(hT_ps, 1)

                    def project(k):
                        pe.wait_ge(hT_ready, k.v + 1)
                        if k.past(2):
                            pe.wait_ge(proj_ready, k.v - 1)
                        o = pP[k.slot(2)][:, 0:TW + 2]
                        pe.matmul(o, hT[k.slot(2)][:, 0, :], Wx[:, 0, :], start=True, stop=False)
                        pe.matmul(o, hT[k.slot(2)][:, 1, :], Wx[:, 1, :], start=False, stop=False)
                        pe.matmul(o, ones_row[0:1, :], row1[0:1, :], start=False, stop=True).then_inc(proj_ps, 1)
                    repeat(pe, TILES, 2, [(0, transpose_h), (1, project)])

                    def count(k):
                        pe.wait_ge(ranked_in, k.v + 1)
                        if k.past(2):
                            pe.wait_ge(hots, k.v - 1)
                        pe.matmul(pB[k.slot(2)][:, 0:TILES], below[:, :], totals[k.slot(2)][:, :], start=True, stop=True)
                        pe.matmul(pB[k.slot(2)][:, TILES:2 * TILES], allone[:, :], totals[k.slot(2)][:, :], start=True, stop=True).then_inc(counted, 1)

                    def compaction(k):
                        pe.wait_ge(hots, k.v + 1)
                        if k.past(2):
                            pe.wait_ge(packed_ready, k.v - 1)
                        for t in range(CCOL):
                            last = pe.matmul(pC[k.slot(2)][:, 0:HI], lo_hot[0][:, t, :], hi_val[0][:, t, :], start=(t == 0), stop=(t == CCOL - 1))
                        last.then_inc(compact, 1)
                    repeat(pe, ALLC, 2, [(0, count), (1, compaction)])
        carve = Carve()
        after = carve([TILES, ALLC])
        keep_c = carve([TILES, ALLC])
        shift = carve([ALLC, TILES + 1])
        delta = carve([ALLC, TILES + 1])
        ge = carve([CHUNKS, GCOLS, TILES + 1])
        dest = carve([ALLC, GCOLS])
        dest_i = carve([ALLC, GCOLS], I32)
        gid = carve([GCOLS])
        gid_i = carve([GCOLS], I32)
        unused = carve([ALLC])
        unused_i = carve([ALLC], I32)
        group_id = carve([3])
        group_i = carve([3], I32)
        sup_i = carve([SORTS, TILES], I32)
        sup_f = carve([2, SORTS, TILES])
        tile_of = carve([3, TILES])
        tile_f = carve([3])
        tile_i = carve([SORTS, 3], I32)
        with ExitStack() as ps:
            p2p, p2, dest_ready, gtile_ready, gt_out, gt_in = (sem("p2p"), sem("p2"), sem("dest_ready"), sem("gtile_ready"),
                                                               sem("gt_out"), sem("gt_in"))
            staged = sem("staged")
            scattered = [sem(f"scattered{i}") for i in range(2)]
            stage_v = [sbe(f"stage_v{i}", [P, GCOLS, GRAN]) for i in range(2)]
            stage_d = [sbe(f"stage_d{i}", [P, GCOLS], I32) for i in range(2)]
            with nc.Block() as block:

                @block.gpsimd
                def _(g):
                    g.iota(gid_i, pattern=[[P, GCOLS]], base=0, channel_multiplier=1).then_inc(p2p, 1)
                    g.iota(group_i, pattern=[[P, 3]], base=0, channel_multiplier=1).then_inc(p2p, 1)
                    for s in range(SORTS):
                        g.iota(unused_i[:, s * CHUNKS:(s + 1) * CHUNKS], pattern=[[GCOLS * P, CHUNKS]],
                               base=s * REGION + GROUPS * GPG, channel_multiplier=0).then_inc(p2p, 1)

                    def scatter(k):
                        sl = k.slot(2)
                        g.wait_ge(staged, k.v + 1)
                        g.nop(nofuse=True)
                        for j in range(GCOLS):
                            g.indirect_dma_start(records, bass.IndirectOffsetOnAxis(ap=stage_d[sl][:, j:j + 1], axis=0),
                                                 stage_v[sl][:, j, :], None).then_inc(scattered[sl], 16)
                    repeat(g, ALLC, 2, [(0, scatter)])
                    for i in range(2):
                        g.wait_ge(scattered[i], 16 * GCOLS * ALLC // 2)

                @block.scalar
                def _(act):
                    act.wait_ge(dest_ready, 1)

                    def stage(k):
                        sl = k.slot(2)
                        if k.past(2):
                            act.wait_ge(scattered[sl], k.round * (16 * GCOLS))
                        act.activation(stage_v[sl].rearrange("p g r -> p (g r)"), packed[:, bass.ds(k.v, 1), :, :].rearrange("p c g r -> p (c g r)"), ACT.Copy)
                        act.copy(stage_d[sl][:, :], dest_i[:, bass.ds(k.v, 1), :].rearrange("p c g -> p (c g)")).then_inc(staged, 1)
                    repeat(act, ALLC, 2, [(0, stage)])

                @block.sync
                def _(sp):
                    sp.wait_ge(gtile_ready, 1)
                    for s in range(SORTS):
                        with nc.allow_non_contiguous_dma(reason="three numbers of a partition"):
                            sp.dma_start(gtile_dram[s, :].rearrange("(q p) -> p q", p=P), tile_i[:, s, :]).then_inc(gt_out, 16)
                    sp.wait_ge(gt_out, 16 * SORTS)
                    sp.dma_start(gtile[0:1, :, :], gtile_dram[:, 0:GROUPS].rearrange("(o s) g -> o s g", o=1)).then_inc(gt_in, 16)
                    sp.wait_ge(gt_in, 16)

                @block.vector
                def _(v):
                    n = [0]

                    def chain(ins):
                        n[0] += 1
                        ins.then_inc(p2, 1)
                        v.wait_ge(p2, n[0])
                    chain(v.memset(keep_c[:, :, :], 1.0))
                    v.memset(keep_c[:, :, 0:1], 0.0)
                    chain(v.memset(keep_c[:, :, CHUNKS:CHUNKS + 1], 0.0))
                    v.wait_ge(p2p, 4)
                    v.tensor_copy(gid, gid_i)
                    v.tensor_copy(group_id, group_i)
                    v.tensor_copy(unused, unused_i)
                    chain(v.tensor_tensor_scan(after.rearrange("p b c -> p (b c)"), keep_c.rearrange("p b c -> p (b c)"),
                                               gran_n[:, :, :].rearrange("p b c -> p (b c)"), 0.0, ALU.mult, ALU.add))
                    for s in range(SORTS):
                        total = after[:, :, s * CHUNKS + CHUNKS - 1]
                        chain(v.tensor_scalar(sup_i[:, s, :], total, float(GPG - 1), None, ALU.add))
                        chain(v.tensor_single_scalar(sup_i[:, s, :], sup_i[:, s, :], GPG.bit_length() - 1, ALU.arith_shift_right))
                        chain(v.tensor_tensor_scan(sup_f[:, 0, s, :], one_row[:, :], sup_i[:, s, :], 0.0, ALU.mult, ALU.add))
                        chain(v.tensor_tensor(sup_f[:, 0, s, :], sup_f[:, 0, s, :], sup_i[:, s, :], ALU.subtract))
                        chain(v.tensor_tensor(tile_of, group_id[:, :, None].to_broadcast([P, 3, TILES]),
                                              sup_f[:, 0, s, None, :].to_broadcast([P, 3, TILES]), ALU.is_ge))
                        chain(v.tensor_reduce(tile_f, tile_of, AX.X, ALU.add))
                        chain(v.tensor_scalar(tile_i[:, s, :], tile_f, -1.0, None, ALU.add))
                        chain(v.tensor_scalar(sup_f[:, 1, s, :], sup_f[:, 0, s, :], float(GPG), float(s * REGION), ALU.mult, ALU.add))
                    v.tensor_copy(tile_i[:, 0, 0:1], tile_i[:, 0, 0:1]).then_inc(gtile_ready, 1)
                    chain(v.tensor_tensor(after, after, gran_n[:, :, :], ALU.subtract))
                    for s in range(SORTS):
                        cs = slice(s * CHUNKS, (s + 1) * CHUNKS)
                        v.tensor_tensor(shift[:, cs, 0:TILES].rearrange("p c b -> p b c"), after[:, :, cs],
                                        sup_f[:, 1, s, :, None].to_broadcast([P, TILES, CHUNKS]), ALU.add)
                    chain(v.tensor_copy(shift[:, :, TILES], unused))
                    chain(v.tensor_tensor(shift[:, :, 0:TILES], shift[:, :, 0:TILES], gran_at[:, :, 0:TILES], ALU.subtract))
                    v.tensor_copy(delta[:, :, 0], shift[:, :, 0])
                    chain(v.tensor_tensor(delta[:, :, 1:], shift[:, :, 1:], shift[:, :, 0:TILES], ALU.subtract))
                    for s in range(SORTS):
                        cs = slice(s * CHUNKS, (s + 1) * CHUNKS)
                        full = [P, CHUNKS, GCOLS, TILES + 1]
                        chain(v.tensor_tensor(ge, gid[:, None, :, None].to_broadcast(full), gran_at[:, cs, None, :].to_broadcast(full), ALU.is_ge))
                        chain(v.tensor_tensor(ge, ge, delta[:, cs, None, :].to_broadcast(full), ALU.mult))
                        chain(v.tensor_reduce(dest[:, cs, :], ge, AX.X, ALU.add))
                    v.tensor_tensor(dest_i, dest, gid[:, None, :].to_broadcast([P, ALLC, GCOLS]), ALU.add).then_inc(dest_ready, 1)

        early.close()
        slot_idx = [sb(f"slot_idx{s}", [P, GROUPS, SUB], I32) for s in range(SORTS)]
        slot_loc = sb("slot_loc", [P, GROUPS, SUB])
        slot_locb = [sb(f"slot_locb{s}", [P, GROUPS, SUB], BF16) for s in range(SORTS)]
        slot_rel = sb("slot_rel", [P, GROUPS, SUB])
        inv_deg = sb("inv_deg", [P, TILES, RELS])
        carve = Carve()
        QG = -(-GROUPS // P)
        rec_in = carve([SORTS, QG, GROUP])
        pk = carve([SORTS, GROUPS, SUB])
        nul = carve([GROUPS * SUB])
        qi = carve([GROUPS * SUB], I32)
        loc_i = carve([GROUPS * SUB], I32)
        rel_i = carve([GROUPS * SUB], I32)
        with ExitStack() as ps:
            pR = [psum(ps, f"pR{i}", [P, SUB, P]) for i in range(2)]
            rec_ld, rec_ps, rec_mv, p3 = sem("rec_ld"), sem("rec_ps"), sem("rec_mv"), sem("p3")
            blocks = [(s, q) for s in range(SORTS) for q in range(QG)]
            with nc.Block() as block:

                @block.sync
                def _(sp):
                    for s, q in blocks:
                        m = min(P, GROUPS - q * P)
                        rows = records[s * REGION:s * REGION + GROUPS * GPG, :].rearrange("(g r) w -> g (r w)", r=GPG)
                        sp.dma_start(rec_in[0:m, s, q, :], rows[q * P:q * P + m, :]).then_inc(rec_ld, 16)

                @block.tensor
                def _(pe):
                    pe.wait_ge(rec_ld, 16 * len(blocks))
                    for n, (s, q) in enumerate(blocks):
                        m = min(P, GROUPS - q * P)
                        if n >= 2:
                            pe.wait_ge(rec_mv, n - 1)
                        view = rec_in[0:m, s, q, :].rearrange("g (p j) -> g j p", j=SUB)
                        for j in range(SUB):
                            last = pe.transpose(pR[n % 2][:, j, 0:m], view[:, j, :], ident[0:m, 0:m])
                        last.then_inc(rec_ps, 1)

                @block.vector
                def _(v):
                    n = [0]

                    def chain(ins):
                        n[0] += 1
                        ins.then_inc(p3, 1)
                        v.wait_ge(p3, n[0])
                    for i, (s, q) in enumerate(blocks):
                        m = min(P, GROUPS - q * P)
                        v.wait_ge(rec_ps, i + 1)
                        v.tensor_copy(pk[:, s, q * P:q * P + m, :].rearrange("p g j -> p j g"), pR[i % 2][:, :, 0:m]).then_inc(rec_mv, 1)
                    v.wait_ge(rec_mv, len(blocks))
                    for s in range(SORTS):
                        val = pk[:, s, :, :].rearrange("p g j -> p (g j)")
                        loc = slot_loc[:, :, :].rearrange("p g j -> p (g j)")
                        row = slot_idx[s][:, :, :].rearrange("p g j -> p (g j)")
                        v.tensor_scalar(nul, val, 0.0, PADLOC, ALU.is_equal, ALU.mult)
                        chain(v.tensor_scalar(qi, val, -1.0, 0.0, ALU.add, ALU.max))
                        v.tensor_single_scalar(row, qi, 7, ALU.arith_shift_right)
                        chain(v.tensor_single_scalar(loc_i, qi, P - 1, ALU.bitwise_and))
                        chain(v.tensor_tensor(loc, loc_i, nul, ALU.add))
                        chain(v.tensor_copy(slot_locb[s][:, :, :].rearrange("p g j -> p (g j)"), loc))
                    chain(v.tensor_single_scalar(rel_i, slot_idx[1][:, :, :].rearrange("p g j -> p (g j)"), RELS - 1, ALU.bitwise_and))
                    chain(v.tensor_copy(slot_rel[:, :, :].rearrange("p g j -> p (g j)"), rel_i))

        RING = 8
        MRING = 4
        carve = Carve(ACCW)
        G = [carve([SUB, TW]) for _ in range(RING)]
        member = [carve([SUB, P]) for _ in range(MRING)]
        other = [carve([SUB, P], BF16) for _ in range(RING)]
        masked = [carve([HEADS, SUB, P]) for _ in range(2)]
        weight = [carve([HEADS, SUB, P]) for _ in range(2)]
        idx_ring = [sb(f"idx_ring{i}", [P, SUB], I32) for i in range(RING)]
        tile_max = [sb(f"tile_max{i}", [P, HEADS]) for i in range(2)]
        above = [sb(f"above{i}", [P, HEADS]) for i in range(2)]
        drop = [sb(f"drop{i}", [P, HEADS]) for i in range(2)]
        fade = [sb(f"fade{i}", [P, HEADS]) for i in range(4)]
        z = [sb(f"z{i}", [P, SUB, HEADS]) for i in range(2)]
        e_rec = [sb(f"e_rec{i}", [P, SUB, HEADS]) for i in range(MRING)]
        expo = [sb(f"expo{i}", [P, SUB, HEADS]) for i in range(2)]
        DVE_MASKS = 2
        with ExitStack() as ps:
            pX = [psum(ps, f"pX{i}", [P, SUB, P]) for i in range(HEADS)]
            pA = [psum(ps, f"pA{i}", [P, 512]) for i in range(2)]
            pM = psum(ps, "pM", [P, SUB, P], BF16)
            pS = psum(ps, "pS", [P, 512])
            pMx = psum(ps, "pMx", [P, 512])
            (acc_zero, idx_ready, other_ready, otherT, member_ready, s_rec, z_ready, e_ready, mask_act, mask_dve, maskedT, reduced, above_ready,
             m_ready, drop_ready, fade_ready, m_rec, expo_ready, weight_ready, agg_ps, acc_done) = (sem(x) for x in (
                 "acc_zero", "idx_ready", "other_ready", "otherT", "member_ready", "s_rec", "z_ready", "e_ready", "mask_act", "mask_dve",
                 "maskedT", "reduced", "above_ready", "m_ready", "drop_ready", "fade_ready", "m_rec", "expo_ready", "weight_ready",
                 "agg_ps", "acc_done"))
            got = [sem(f"got{i}") for i in range(RING)]
            with nc.Block() as block:

                @block.gpsimd
                def _(g):
                    def gather(k):
                        sl = k.slot(RING)
                        g.wait_ge(idx_ready, k.v + 1)
                        if k.past(RING):
                            g.wait_ge(agg_ps, k.v - (RING - 1))
                        g.nop(nofuse=True)
                        for c in range(SUB):
                            g.indirect_dma_start(G[sl][:, c, :], None, wh_table,
                                                 bass.IndirectOffsetOnAxis(ap=idx_ring[sl][:, c:c + 1], axis=0)).then_inc(got[sl], 16)
                    repeat(g, GROUPS, RING, [(0, gather)])

                @block.scalar
                def _(act):
                    def index(k):
                        sl = k.slot(RING)
                        if k.past(RING):
                            act.wait_ge(got[sl], k.round * (16 * SUB))
                        act.copy(idx_ring[sl][:, :], slot_idx[0][:, bass.ds(k.v, 1), :].rearrange("p g j -> p (g j)")).then_inc(idx_ready, 1)

                    def weigh(k):
                        act.wait_ge(expo_ready, k.v + 1)
                        if k.past(2):
                            act.wait_ge(agg_ps, k.v - 1)
                        for h in range(HEADS):
                            for c in range(SUB):
                                last = act.activation(weight[k.slot(2)][:, h, c, :], other[k.slot(RING)][:, c, :], ACT.Exp,
                                                      bias=expo[k.slot(2)][:, c, h:h + 1], scale=-BIG)
                        last.then_inc(weight_ready, 1)

                    def fades(k):
                        act.wait_ge(drop_ready, k.v + 1)
                        if k.past(4):
                            act.wait_ge(acc_done, k.v - 3)
                        act.activation(fade[k.slot(4)][:, :], drop[k.slot(2)][:, :], ACT.Exp).then_inc(fade_ready, 1)

                    def mask(k):
                        act.wait_ge(e_ready, k.v + 1)
                        if k.past(2):
                            act.wait_ge(maskedT, k.v - 1)
                        for n in range(DVE_MASKS, HEADS * SUB):
                            h, c = divmod(n, SUB)
                            last = act.activation(masked[k.slot(2)][:, h, c, :], other[k.slot(RING)][:, c, :], ACT.Identity,
                                                  bias=e_rec[k.slot(MRING)][:, c, h:h + 1], scale=-BIG)
                        last.then_inc(mask_act, 1)
                    repeat(act, GROUPS, RING, [(0, index), (7, weigh), (6, fades), (4, mask)])

                @block.tensor
                def _(pe):
                    def transpose_other(k):
                        pe.wait_ge(other_ready, k.v + 1)
                        if k.past(1):
                            pe.wait_ge(member_ready, k.v)
                        for c in range(SUB):
                            last = pe.transpose(pM[:, c, :], other[k.slot(RING)][:, c, :], identb[:, :])
                        last.then_inc(otherT, 1)

                    def expand(k, first, to, ready, read):
                        b = pe.value_load(gtile[0:1, 0, bass.ds(k.v, 1)], min_val=0, max_val=TILES - 1)
                        pe.wait_ge(ready, k.v + 1)
                        if k.past(1):
                            pe.wait_ge(read, k.v)
                        for c in range(SUB):
                            last = pe.matmul(to[:, HEADS * c:HEADS * (c + 1)], member[k.slot(MRING)][:, c, :],
                                             SM[:, bass.ds(b, 1), first:first + HEADS].rearrange("p t c -> p (t c)"), start=True, stop=True)
                        return last

                    def expand_s(k):
                        expand(k, 0, pS, member_ready, z_ready).then_inc(s_rec, 1)

                    def expand_m(k):
                        expand(k, HEADS, pMx, m_ready, expo_ready).then_inc(m_rec, 1)

                    def transpose_masked(k):
                        pe.wait_ge(mask_act, k.v + 1)
                        pe.wait_ge(mask_dve, k.v + 1)
                        for h in range(HEADS):
                            if k.past(1):
                                pe.wait_ge(reduced, HEADS * k.v + h - 1)
                            for c in range(SUB):
                                last = pe.transpose(pX[h][:, c, :], masked[k.slot(2)][:, h, c, :], ident[:, :])
                        last.then_inc(maskedT, 1)

                    def aggregate(k):
                        sl = k.slot(2)
                        pe.wait_ge(weight_ready, k.v + 1)
                        pe.wait_ge(got[k.slot(RING)], (k.round + 1) * (16 * SUB))
                        if k.past(2):
                            pe.wait_ge(acc_done, k.v - 1)
                        for h in range(HEADS):
                            for c in range(SUB):
                                last = pe.matmul(pA[sl][:, h * HW:(h + 1) * HW], weight[sl][:, h, c, :],
                                                 G[k.slot(RING)][:, c, h * HW:(h + 1) * HW], start=(c == 0), stop=(c == SUB - 1))
                        last.then_inc(agg_ps, 1)
                    repeat(pe, GROUPS, RING, [(5, transpose_masked), (2, transpose_other), (6, expand_m), (3, expand_s), (7, aggregate)])

                @block.vector
                def _(v):
                    v.memset(arena[:, 0:ACCW], 0.0).then_inc(acc_zero, 1)
                    v.wait_ge(acc_zero, 1)
                    full = [P, SUB, P]

                    def tile_register(k):
                        return v.value_load(gtile[0:1, 0, bass.ds(k.v, 1)], min_val=0, max_val=TILES - 1)

                    def others(k):
                        if k.past(RING):
                            v.wait_ge(weight_ready, k.v - (RING - 1))
                        v.tensor_tensor(other[k.slot(RING)], iotab[:, None, :].to_broadcast(full),
                                        slot_locb[0][:, bass.ds(k.v, 1), :].rearrange("p g j -> p (g j)")[:, :, None].to_broadcast(full),
                                        ALU.not_equal).then_inc(other_ready, 1)

                    def members(k):
                        v.wait_ge(otherT, k.v + 1)
                        if k.past(MRING):
                            v.wait_ge(m_rec, k.v - (MRING - 1))
                        v.tensor_scalar(member[k.slot(MRING)], pM[:, :, :], -1.0, 1.0, ALU.mult, ALU.add).then_inc(member_ready, 1)

                    def score(k):
                        v.wait_ge(s_rec, k.v + 1)
                        v.wait_ge(got[k.slot(RING)], (k.round + 1) * (16 * SUB))
                        v.tensor_tensor(z[k.slot(2)][:, :, :], G[k.slot(RING)][:, :, TCOL:TCOL + HEADS],
                                        pS[:, 0:HEADS * SUB].rearrange("p (c h) -> p c h", h=HEADS), ALU.add).then_inc(z_ready, 1)

                    def leaky(k):
                        v.wait_ge(z_ready, k.v + 1)
                        v.scalar_tensor_tensor(e_rec[k.slot(MRING)][:, :, :], z[k.slot(2)][:, :, :], SLOPE, z[k.slot(2)][:, :, :],
                                               ALU.mult, ALU.max).then_inc(e_ready, 1)

                    def mask(k):
                        v.wait_ge(e_ready, k.v + 1)
                        if k.past(2):
                            v.wait_ge(maskedT, k.v - 1)
                        for n in range(DVE_MASKS):
                            h, c = divmod(n, SUB)
                            last = v.tensor_scalar(masked[k.slot(2)][:, h, c, :], other[k.slot(RING)][:, c, :], -BIG,
                                                   e_rec[k.slot(MRING)][:, c, h:h + 1], ALU.mult, ALU.add)
                        last.then_inc(mask_dve, 1)

                    def reduce(k):
                        v.wait_ge(maskedT, k.v + 1)
                        for h in range(HEADS):
                            v.tensor_reduce(tile_max[k.slot(2)][:, h:h + 1], pX[h][:, :, :].rearrange("p c e -> p (c e)"),
                                            AX.X, ALU.max).then_inc(reduced, 1)

                    def running(k):
                        b = tile_register(k)
                        M = SM[:, bass.ds(b, 1), HEADS:2 * HEADS].rearrange("p t c -> p (t c)")
                        v.wait_ge(reduced, HEADS * (k.v + 1))
                        if k.past(1):
                            v.wait_ge(m_ready, k.v)
                            v.wait_ge(m_rec, k.v)
                        v.tensor_tensor(above[k.slot(2)][:, :], M, tile_max[k.slot(2)][:, :], ALU.subtract).then_inc(above_ready, 1)
                        v.tensor_tensor(M, M, tile_max[k.slot(2)][:, :], ALU.max).then_inc(m_ready, 1)

                    def drops(k):
                        v.wait_ge(above_ready, k.v + 1)
                        if k.past(2):
                            v.wait_ge(fade_ready, k.v - 1)
                        v.tensor_scalar(drop[k.slot(2)][:, :], above[k.slot(2)][:, :], 0.0, None, ALU.min).then_inc(drop_ready, 1)

                    def exponent(k):
                        v.wait_ge(m_rec, k.v + 1)
                        if k.past(2):
                            v.wait_ge(weight_ready, k.v - 1)
                        v.tensor_tensor(expo[k.slot(2)][:, :, :], e_rec[k.slot(MRING)][:, :, :],
                                        pMx[:, 0:HEADS * SUB].rearrange("p (c h) -> p c h", h=HEADS), ALU.subtract).then_inc(expo_ready, 1)

                    def add(k):
                        b = tile_register(k)
                        v.wait_ge(agg_ps, k.v + 1)
                        v.wait_ge(fade_ready, k.v + 1)
                        if k.past(1):
                            v.wait_ge(acc_done, k.v)
                        for h in range(HEADS):
                            a = acc[:, bass.ds(b, 1), h * HW:(h + 1) * HW].rearrange("p t c -> p (t c)")
                            last = v.scalar_tensor_tensor(a, a, fade[k.slot(4)][:, h:h + 1], pA[k.slot(2)][:, h * HW:(h + 1) * HW], ALU.mult, ALU.add)
                        last.then_inc(acc_done, 1)
                    repeat(v, GROUPS, RING, [(6, reduce), (2, others), (6, running), (4, score), (3, members), (6, drops), (4, leaky),
                                             (8, add), (6, exponent), (4, mask)])

        carve = Carve(ACCW)
        wr = carve([2, RELS * DIM])
        rel_out = [arena[:, 0:RELS * DIM], arena[:, RELS * DIM:2 * RELS * DIM]]
        W0T = carve([2, DIM])
        w0 = carve([2, DIM])
        own = [carve([TW]) for _ in range(2)]
        rden = carve([TILES, HEADS])
        alone = carve([TILES, HEADS])
        DEG = [-(-GROUPS // TILES), GROUPS // TILES]
        PAIR = sum(DEG)
        assert TILES // 2 * PAIR <= GROUPS <= TILES // 2 * PAIR + DEG[0]
        node_hot = [carve([DEG[0] * SUB, P], BF16) for _ in range(2)]
        rel_hot = [carve([DEG[0] * SUB, RELS], BF16) for _ in range(2)]
        deg_part = [carve([DEG[0], RELS]) for _ in range(2)]

        def deg_groups(k):
            m = min(DEG[k.slot(2)], GROUPS - (k.least // 2 * PAIR + k.slot(2) * DEG[0]))
            return k.round * PAIR + k.slot(2) * DEG[0], m
        with ExitStack() as ps:
            pT = [psum(ps, f"qT{i}", [P, 2, P]) for i in range(1)]
            pO = [psum(ps, f"qO{i}", [P, 512]) for i in range(1)]
            pH = [psum(ps, f"qH{i}", [P, 512]) for i in range(UNROLL)]
            w_ld, own_ready, d_c, x_c, x2_done, st2, st2_done, std2, ln2 = (sem(x) for x in (
                "w_ld", "own_ready", "d_c", "x_c", "x2_done", "st2", "st2_done", "std2", "ln2"))
            own_in = [sem(f"own_in{i}") for i in range(2)]
            own_used = sem("own_used")
            h2_ready, h2T_ps, h2T_ready, root_ps, root_add, rel_ps, w0_ps, w0_ready = (sem(x) for x in (
                "h2_ready", "h2T_ps", "h2T_ready", "root_ps", "root_add", "rel_ps", "w0_ps", "w0_ready"))
            rel_act, rel_dve = sem("rel_act"), sem("rel_dve")
            pD = [psum(ps, f"pD{i}", [P, 512]) for i in range(2)]
            deg_zero, deg_hot, deg_ps, deg_moved, deg_add, deg_done = (sem(x) for x in (
                "deg_zero", "deg_hot", "deg_ps", "deg_moved", "deg_add", "deg_done"))
            rel_st = [sem(f"rel_st{i}") for i in range(2)]
            with nc.Block() as block:

                @block.sync
                def _(sp):
                    for k in range(2):
                        sp.dma_start(wr[:, k, :].rearrange("p (r n) -> p r n", r=RELS),
                                     A["L1_gnn_W_r"][:, k * P:(k + 1) * P, :].rearrange("r p n -> p r n")).then_inc(w_ld, 16)
                    sp.dma_start(w0[:, :, :], A["L1_gnn_W0_w"].rearrange("(k p) n -> p k n", p=P)).then_inc(w_ld, 16)
                    sp.dma_start(row2[:, :], A["L1_gnn_W0_b"].rearrange("(o n) -> o n", o=1)).then_inc(w_ld, 16)

                    def own_rows(k):
                        if k.past(2):
                            sp.wait_ge(own_used, k.v - 1)
                        sp.dma_start(own[k.slot(2)][:, :], wh_table.rearrange("(t p) c -> t p c", p=P)[bass.ds(k.v, 1), :, :].rearrange("t p c -> p (t c)")
                                     ).then_inc(own_in[k.slot(2)], 16)
                    repeat(sp, TILES, 2, [(0, own_rows)])

                    def store(k):
                        sp.wait_ge(rel_act, (k.v + 1) * 4)
                        sp.wait_ge(rel_dve, (k.v + 1) * 4)
                        sp.dma_start(rel_table.rearrange("(t p r) n -> t p (r n)", p=P, r=RELS)[bass.ds(k.v, 1), :, :].rearrange("t p c -> p (t c)"),
                                     rel_out[k.slot(2)]).then_inc(rel_st[k.slot(2)], 16)
                    repeat(sp, TILES, 2, [(0, store)])
                    sp.wait_ge(rel_st[0], 16 * (TILES - TILES // 2))
                    sp.wait_ge(rel_st[1], 16 * (TILES // 2))

                @block.gpsimd
                def _(g):
                    g.memset(inv_deg[:, :, :], 0.0).then_inc(deg_zero, 1)
                    g.wait_ge(deg_zero, 1)

                    def add_degrees(k):
                        first, m = deg_groups(k)
                        for i in range(m):
                            b = g.value_load(gtile[0:1, 1, bass.ds(first + i, 1)], min_val=0, max_val=TILES - 1)
                            if i == 0:
                                g.wait_ge(deg_moved, k.v + 1)
                            if i or k.past(1):
                                g.wait_ge(deg_add, first + i)
                            d = inv_deg[:, bass.ds(b, 1), :].rearrange("p t r -> p (t r)")
                            g.tensor_tensor(d, d, deg_part[k.slot(2)][:, i, :], ALU.add).then_inc(deg_add, 1)
                    repeat(g, TILES, 2, [(0, add_degrees)])
                    g.wait_ge(deg_add, GROUPS)

                @block.vector
                def _(v):
                    den = acc[:, :, :].rearrange("p t (h w) -> p t h w", w=HW)[:, :, :, HD]
                    v.tensor_scalar(alone[:, :, :], den, 0.0, None, ALU.is_equal)
                    v.tensor_scalar(rden[:, :, :], den, 1e-30, None, ALU.max).then_inc(d_c, 1)
                    v.wait_ge(d_c, 1)
                    v.reciprocal(rden[:, :, :], rden[:, :, :]).then_inc(d_c, 1)
                    v.wait_ge(d_c, 2)

                    def residual(k):
                        t = bass.ds(k.v, 1)
                        for h in range(HEADS):
                            x = X[:, t, h * HD:(h + 1) * HD].rearrange("p t d -> p (t d)")
                            last = v.scalar_tensor_tensor(x, acc[:, t, h * HW:h * HW + HD].rearrange("p t d -> p (t d)"),
                                                          rden[:, t, h], x, ALU.mult, ALU.add)
                        last.then_inc(x_c, 1)
                        v.wait_ge(x_c, k.v + 1)
                        v.wait_ge(own_in[k.slot(2)], (k.round + 1) * 16)
                        for h in range(HEADS):
                            x = X[:, t, h * HD:(h + 1) * HD].rearrange("p t d -> p (t d)")
                            last = v.scalar_tensor_tensor(x, own[k.slot(2)][:, h * HW:h * HW + HD], alone[:, t, h], x, ALU.mult, ALU.add)
                        last.then_inc(own_used, 1)

                    def stat(k):
                        v.bn_stats(stats[:, bass.ds(k.v, 1), :].rearrange("p t c -> p (t c)"),
                                   X[:, bass.ds(k.v, 1), :].rearrange("p t d -> p (t d)")).then_inc(st2, 1)
                    repeat(v, TILES, 2, [(0, residual)])
                    v.wait_ge(own_used, TILES)
                    repeat(v, TILES, 2, [(0, stat)])
                    v.wait_ge(st2, TILES)
                    for t in range(TILES):
                        v.bn_aggr(mv[:, t, :], stats[:, t, :]).then_inc(st2_done, 1)
                    v.wait_ge(std2, 1)
                    v.reciprocal(rstd[:, :], rstd[:, :]).then_inc(std2, 1)
                    v.wait_ge(std2, 2)
                    v.scalar_tensor_tensor(nbias[:, :], mv[:, :, 0], -1.0, rstd[:, :], ALU.mult, ALU.mult).then_inc(ln2, 1)
                    v.wait_ge(w0_ps, 1)
                    v.tensor_copy(W0T[:, :, :].rearrange("p k n -> p (k n)"), pO[0][:, :]).then_inc(w0_ready, 1)

                    def move_hT(k):
                        v.wait_ge(h2T_ps, k.v + 1)
                        if k.past(2):
                            v.wait_ge(rel_ps, (k.v - 1) * 8)
                        v.tensor_copy(hT[k.slot(2)][:, :, :], pT[0][:, :, :]).then_inc(h2T_ready, 1)

                    def root(k):
                        v.wait_ge(root_ps, k.v + 1)
                        v.wait_ge(h2_ready, k.v + 1)
                        x = X[:, bass.ds(k.v, 1), :].rearrange("p t d -> p (t d)")
                        v.tensor_tensor(x, x, pO[0][:, 0:DIM], ALU.add).then_inc(root_add, 1)

                    def move_rel(k):
                        if k.past(2):
                            v.wait_ge(rel_st[k.slot(2)], k.round * 16)
                        for j in range(1, 8, 2):
                            v.wait_ge(rel_ps, k.v * 8 + j + 1)
                            v.tensor_copy(rel_out[k.slot(2)][:, j * 512:(j + 1) * 512], pH[j % 4][:, :]).then_inc(rel_dve, 1)

                    def degree_hots(k):
                        first, m = deg_groups(k)
                        if k.past(2):
                            v.wait_ge(deg_ps, k.v - 1)
                        v.tensor_tensor(node_hot[k.slot(2)][:, 0:m * SUB, :], iotab[:, None, :].to_broadcast([P, m * SUB, P]),
                                        slot_locb[1][:, bass.ds(first, m), :].rearrange("p g j -> p (g j)")[:, :, None].to_broadcast([P, m * SUB, P]), ALU.is_equal)
                        v.tensor_tensor(rel_hot[k.slot(2)][:, 0:m * SUB, :], iota[:, None, 0:RELS].to_broadcast([P, m * SUB, RELS]),
                                        slot_rel[:, bass.ds(first, m), :].rearrange("p g j -> p (g j)")[:, :, None].to_broadcast([P, m * SUB, RELS]), ALU.is_equal).then_inc(deg_hot, 1)
                    repeat(v, TILES, 2, [(0, move_hT), (1, root), (0, degree_hots), (1, move_rel)])
                    v.wait_ge(deg_add, GROUPS)
                    v.tensor_scalar(inv_deg[:, :, :], inv_deg[:, :, :], 1.0, None, ALU.max).then_inc(deg_done, 1)
                    v.wait_ge(deg_done, 1)
                    v.reciprocal(inv_deg[:, :, :], inv_deg[:, :, :])

                @block.scalar
                def _(act):
                    act.wait_ge(st2_done, TILES)
                    act.activation(rstd[:, :], mv[:, :, 1], ACT.Sqrt, bias=eps[:, 0:1]).then_inc(std2, 1)
                    act.wait_ge(ln2, 1)

                    def norm(k):
                        if k.past(2):
                            act.wait_ge(h2T_ps, k.v - 1)
                        act.activation(hbuf[k.slot(2)][:, :], X[:, bass.ds(k.v, 1), :].rearrange("p t d -> p (t d)"), ACT.Relu,
                                       bias=nbias[:, bass.ds(k.v, 1)], scale=rstd[:, bass.ds(k.v, 1)]).then_inc(h2_ready, 1)

                    def move_rel(k):
                        if k.past(2):
                            act.wait_ge(rel_st[k.slot(2)], k.round * 16)
                        for j in range(0, 8, 2):
                            act.wait_ge(rel_ps, k.v * 8 + j + 1)
                            act.activation(rel_out[k.slot(2)][:, j * 512:(j + 1) * 512], pH[j % 4][:, :], ACT.Copy).then_inc(rel_act, 1)

                    def move_degrees(k):
                        _, m = deg_groups(k)
                        act.wait_ge(deg_ps, k.v + 1)
                        if k.past(2):
                            act.wait_ge(deg_add, deg_groups(k)[0] - DEG[1 - k.slot(2)])
                        act.activation(deg_part[k.slot(2)][:, 0:m, :].rearrange("p g r -> p (g r)"), pD[k.slot(2)][:, 0:m * RELS], ACT.Copy).then_inc(deg_moved, 1)
                    repeat(act, TILES, 2, [(0, norm), (2, move_rel), (2, move_degrees)])

                @block.tensor
                def _(pe):
                    pe.wait_ge(w_ld, 64)
                    for k in range(2):
                        for m in range(2):
                            last = pe.transpose(pO[0][:, k * DIM + m * P:k * DIM + (m + 1) * P], w0[:, m, k * P:(k + 1) * P], ident[:, :])
                    last.then_inc(w0_ps, 1)
                    pe.wait_ge(w0_ready, 1)

                    def transpose_h(k):
                        pe.wait_ge(h2_ready, k.v + 1)
                        if k.past(1):
                            pe.wait_ge(h2T_ready, k.v)
                        for j in range(2):
                            last = pe.transpose(pT[0][:, j, :], hbuf[k.slot(2)][:, j * P:(j + 1) * P], ident[:, :])
                        last.then_inc(h2T_ps, 1)

                    def products(k):
                        h = hT[k.slot(2)]
                        pe.wait_ge(h2T_ready, k.v + 1)
                        if k.past(1):
                            pe.wait_ge(root_add, k.v)
                        pe.matmul(pO[0][:, 0:DIM], h[:, 0, :], W0T[:, 0, :], start=True, stop=False)
                        pe.matmul(pO[0][:, 0:DIM], h[:, 1, :], W0T[:, 1, :], start=False, stop=False)
                        pe.matmul(pO[0][:, 0:DIM], ones_row[0:1, :], row2[0:1, :], start=False, stop=True).then_inc(root_ps, 1)
                        for j in range(8):
                            moved = rel_dve if j % 2 else rel_act
                            if k.past(1) or j >= 4:
                                pe.wait_ge(moved, k.v * 4 + (j // 2 - 1))
                            for i in range(2):
                                last = pe.matmul(pH[j % 4][:, :], h[:, i, :], wr[:, i, j * 512:(j + 1) * 512], start=(i == 0), stop=(i == 1))
                            last.then_inc(rel_ps, 1)

                    def count(k):
                        _, m = deg_groups(k)
                        pe.wait_ge(deg_hot, k.v + 1)
                        if k.past(2):
                            pe.wait_ge(deg_moved, k.v - 1)
                        for i in range(m):
                            for c in range(i * SUB, (i + 1) * SUB):
                                last = pe.matmul(pD[k.slot(2)][:, i * RELS:(i + 1) * RELS], node_hot[k.slot(2)][:, c, :], rel_hot[k.slot(2)][:, c, :],
                                                 start=(c == i * SUB), stop=(c == (i + 1) * SUB - 1))
                        last.then_inc(deg_ps, 1)
                    repeat(pe, TILES, 2, [(0, transpose_h), (1, products), (1, count)])

        carve = Carve()
        G1 = [carve([SUB, DIM]) for _ in range(RING)]
        hot = [carve([SUB, P], BF16) for _ in range(2)]
        rhot = [carve([SUB, RELS]) for _ in range(4)]
        rprod = [carve([SUB, RELS]) for _ in range(2)]
        OT1 = [carve([SUB, P]) for _ in range(2)]
        W1 = [carve([SUB, P]) for _ in range(2)]
        wt = [carve([SUB]) for _ in range(2)]
        with ExitStack() as ps:
            qX = [psum(ps, f"rX{i}", [P, SUB, P], BF16) for i in range(2)]
            qE = [psum(ps, f"rE{i}", [P, 512]) for i in range(2)]
            qA = [psum(ps, f"rA{i}", [P, 512]) for i in range(2)]
            idx1, hot1, hotT, ot1, deg_ex, rhot1, w_prod, w_sum, w1_done, agg1, add1 = (sem(x) for x in (
                "idx1", "hot1", "hotT", "ot1", "deg_ex", "rhot1", "w_prod", "w_sum", "w1_done", "agg1", "add1"))
            got1 = [sem(f"got1{i}") for i in range(RING)]
            out_done = sem("out_done")
            with nc.Block() as block:

                @block.gpsimd
                def _(g):
                    def gather(k):
                        sl = k.slot(RING)
                        g.wait_ge(idx1, k.v + 1)
                        if k.past(RING):
                            g.wait_ge(agg1, k.v - (RING - 1))
                        g.nop(nofuse=True)
                        for c in range(SUB):
                            g.indirect_dma_start(G1[sl][:, c, :], None, rel_table,
                                                 bass.IndirectOffsetOnAxis(ap=idx_ring[sl][:, c:c + 1], axis=0)).then_inc(got1[sl], 16)
                    repeat(g, GROUPS, RING, [(0, gather)])

                @block.scalar
                def _(act):
                    def index(k):
                        sl = k.slot(RING)
                        if k.past(RING):
                            act.wait_ge(got1[sl], k.round * (16 * SUB))
                        act.copy(idx_ring[sl][:, :], slot_idx[1][:, bass.ds(k.v, 1), :].rearrange("p g j -> p (g j)")).then_inc(idx1, 1)

                    def move(k):
                        act.wait_ge(hotT, k.v + 1)
                        if k.past(2):
                            act.wait_ge(deg_ex, k.v - 1)
                        act.activation(OT1[k.slot(2)], qX[k.slot(2)][:, :, :], ACT.Copy).then_inc(ot1, 1)
                    repeat(act, GROUPS, RING, [(0, index), (2, move)])

                @block.tensor
                def _(pe):
                    def spread(k):
                        sl = k.slot(2)
                        pe.wait_ge(hot1, k.v + 1)
                        if k.past(2):
                            pe.wait_ge(ot1, k.v - 1)
                        for c in range(SUB):
                            last = pe.transpose(qX[sl][:, c, :], hot[sl][:, c, :], identb[:, :])
                        last.then_inc(hotT, 1)

                    def expand(k):
                        sl = k.slot(2)
                        b = pe.value_load(gtile[0:1, 1, bass.ds(k.v, 1)], min_val=0, max_val=TILES - 1)
                        pe.wait_ge(ot1, k.v + 1)
                        if k.past(2):
                            pe.wait_ge(w_prod, k.v - 1)
                        for c in range(SUB):
                            last = pe.matmul(qE[sl][:, c * RELS:(c + 1) * RELS], OT1[sl][:, c, :],
                                             inv_deg[:, bass.ds(b, 1), :].rearrange("p t r -> p (t r)"), start=True, stop=True)
                        last.then_inc(deg_ex, 1)

                    def aggregate(k):
                        sl = k.slot(2)
                        pe.wait_ge(w1_done, k.v + 1)
                        pe.wait_ge(got1[k.slot(RING)], (k.round + 1) * (16 * SUB))
                        if k.past(2):
                            pe.wait_ge(add1, k.v - 1)
                        for c in range(SUB):
                            last = pe.matmul(qA[sl][:, 0:DIM], W1[sl][:, c, :], G1[k.slot(RING)][:, c, :], start=(c == 0), stop=(c == SUB - 1))
                        last.then_inc(agg1, 1)
                    repeat(pe, GROUPS, RING, [(1, spread), (2, expand), (4, aggregate)])

                @block.vector
                def _(v):
                    def hots1(k):
                        if k.past(2):
                            v.wait_ge(hotT, k.v - 1)
                        v.tensor_tensor(hot[k.slot(2)], iotab[:, None, :].to_broadcast([P, SUB, P]),
                                        slot_locb[1][:, bass.ds(k.v, 1), :].rearrange("p g j -> p (g j)")[:, :, None].to_broadcast([P, SUB, P]), ALU.is_equal).then_inc(hot1, 1)

                    def rel_hots(k):
                        if k.past(4):
                            v.wait_ge(w_prod, k.v - 3)
                        v.tensor_tensor(rhot[k.slot(4)], iota[:, None, 0:RELS].to_broadcast([P, SUB, RELS]),
                                        slot_rel[:, bass.ds(k.v, 1), :].rearrange("p g j -> p (g j)")[:, :, None].to_broadcast([P, SUB, RELS]), ALU.is_equal).then_inc(rhot1, 1)

                    def pick(k):
                        sl = k.slot(2)
                        v.wait_ge(deg_ex, k.v + 1)
                        v.wait_ge(rhot1, k.v + 1)
                        if k.past(2):
                            v.wait_ge(w_sum, k.v - 1)
                        v.tensor_tensor(rprod[sl], rhot[k.slot(4)], qE[sl][:, 0:SUB * RELS].rearrange("p (c r) -> p c r", r=RELS), ALU.mult).then_inc(w_prod, 1)

                    def pick_sum(k):
                        v.wait_ge(w_prod, k.v + 1)
                        if k.past(2):
                            v.wait_ge(w1_done, k.v - 1)
                        v.tensor_reduce(wt[k.slot(2)], rprod[k.slot(2)], AX.X, ALU.add).then_inc(w_sum, 1)

                    def weigh(k):
                        v.wait_ge(w_sum, k.v + 1)
                        if k.past(2):
                            v.wait_ge(agg1, k.v - 1)
                        for c in range(SUB):
                            last = v.tensor_scalar(W1[k.slot(2)][:, c, :], iota[:, :], slot_loc[:, bass.ds(k.v, 1), c], wt[k.slot(2)][:, c:c + 1], ALU.is_equal, ALU.mult)
                        last.then_inc(w1_done, 1)

                    def add(k):
                        sl = k.slot(2)
                        b = v.value_load(gtile[0:1, 1, bass.ds(k.v, 1)], min_val=0, max_val=TILES - 1)
                        v.wait_ge(agg1, k.v + 1)
                        if k.past(1):
                            v.wait_ge(add1, k.v)
                        x = X[:, bass.ds(b, 1), :].rearrange("p t d -> p (t d)")
                        v.tensor_tensor(x, x, qA[sl][:, 0:DIM], ALU.add).then_inc(add1, 1)
                    repeat(v, GROUPS, RING, [(4, weigh), (1, hots1), (3, pick), (1, rel_hots), (3, pick_sum), (5, add)])

                @block.sync
                def _(sp):
                    sp.wait_ge(add1, GROUPS)
                    sp.dma_start(out[0:FULL * P, :].rearrange("(t p) d -> p t d", p=P), X[:, 0:FULL, :]).then_inc(out_done, 16)
                    sp.dma_start(out[FULL * P:NODES, :], X[0:REST, FULL, :]).then_inc(out_done, 16)
                    sp.wait_ge(out_done, 32)



_INS = ["x", "src", "dst", "edge_type_16", "L0_gnn_W_w", "L0_gnn_W_b", "L0_gnn_a", "L1_gnn_W_r", "L1_gnn_W0_w", "L1_gnn_W0_b"]


def kernel(**inputs):
    import concourse.bacc as bacc
    from concourse.bass_utils import run_bass_kernel_spmd as run

    nc = bacc.Bacc("TRN2", target_bir_lowering=False, num_devices=1)
    arrays, args = {}, {}
    for name in _INS:
        a = np.ascontiguousarray(inputs[name])
        arrays[f"in_{name}"] = a
        args[name] = nc.dram_tensor(f"in_{name}", a.shape, mybir.dt.from_np(a.dtype), kind="ExternalInput").ap()
    out = nc.dram_tensor("out", (NODES, DIM), F32, kind="ExternalOutput").ap()
    build(nc, args, out)
    r = run(nc, [arrays], core_ids=[0])
    return r.results[0]["out"]
```

```python
from contextlib import ExitStack

import numpy as np

import concourse.bass as bass
from concourse import mybir

F32 = mybir.dt.float32
BF16 = mybir.dt.bfloat16
F16 = mybir.dt.float16
I32 = mybir.dt.int32
ALU = mybir.AluOpType
ACT = mybir.ActivationFunctionType
AX = mybir.AxisListType

P = 128
NODES, DIM, HEADS, HD, RELS, EDGES = 6250, 256, 2, 128, 16, 106250
TILES = -(-NODES // P)
FULL = NODES // P
REST = NODES - FULL * P
EPART = 125
ECOL = EDGES // EPART
CCOL = 50
CHUNKS = ECOL // CCOL
SORTS = 2
ALLC = SORTS * CHUNKS
GRAN = 8
GCOLS = -(-(EPART * CCOL + TILES * (GRAN - 1)) // (P * GRAN))
HI = GCOLS * GRAN
SUB = 4
GROUP = SUB * P
GPG = GROUP // GRAN
UNROLL = 4
MAXGRAN = (EDGES + CHUNKS * TILES * (GRAN - 1)) // GRAN
GROUPS = (MAXGRAN + TILES * (GPG - 1)) // GPG
GROUPS = -(-GROUPS // UNROLL) * UNROLL
REGION = GROUPS * GPG + CHUNKS * GCOLS * P
PADLOC = 1000.0
BIG = float(2.0 ** 100)
LOW = 12
CENTER = (P * NODES * RELS >> LOW) // 2
SLOPE = 0.2
EPS = 1e-5
TW = 260
HW = HD + 1
TCOL = 2 * HW


class Step:

    def __init__(self, v, least, rnd):
        self.v, self.least, self.round = v, least, rnd

    def slot(self, ring):
        return self.least % ring

    def past(self, n):
        return self.least >= n


def repeat(eng, n, unroll, stages, start=0):
    lags = [lag for lag, _ in stages]
    first = -(-(max(lags) + unroll) // unroll) * unroll
    rounds = max(0, (n - first) // unroll)

    def static(j):
        for lag, fn in stages:
            if 0 <= j - lag < n:
                fn(Step(start + j - lag, start + j - lag, (j - lag) // unroll))

    for j in range(first):
        static(j)
    if rounds:
        with eng.Fori(0, rounds) as it:
            for u in range(unroll):
                for lag, fn in stages:
                    base = first + u - lag
                    fn(Step(it * unroll + (start + base), start + base, it + base // unroll))
    for j in range(first + rounds * unroll, n + max(lags)):
        static(j)


def build(nc, A, out):
    ctx = ExitStack()
    with ctx:
        def sb(name, shape, dt=F32):
            return ctx.enter_context(nc.sbuf_tensor(name, shape, dt))

        def sem(name):
            return ctx.enter_context(nc.semaphore(name))

        wh_table = nc.dram_tensor("wh_table", [TILES * P, TW], F32, kind="Internal").ap()
        rel_table = nc.dram_tensor("rel_table", [TILES * P * RELS, DIM], F32, kind="Internal").ap()
        records = nc.dram_tensor("records", [SORTS * REGION, GRAN], F32, kind="Internal").ap()
        gtile_dram = nc.dram_tensor("gtile_dram", [SORTS, 3 * P], I32, kind="Internal").ap()

        X = sb("X", [P, TILES, DIM])
        ident = sb("ident", [P, P])
        identb = sb("identb", [P, P], BF16)
        iota = sb("iota", [P, P])
        iotab = sb("iotab", [P, P], BF16)
        gtile = sb("gtile", [1, SORTS, GROUPS], I32)
        SM = sb("SM", [P, TILES, 4])
        mv = sb("mv", [P, TILES, 2])
        rstd = sb("rstd", [P, TILES])
        nbias = sb("nbias", [P, TILES])
        eps = sb("eps", [P, 1])
        ones_row = sb("ones_row", [1, P])
        row1 = sb("row1", [1, TW + 2])
        row2 = sb("row2", [1, DIM])
        ARENA = 29190
        arena = sb("arena", [P, ARENA])
        ACCW = TILES * TCOL
        acc = arena[:, 0:ACCW].rearrange("p (t c) -> p t c", c=TCOL)

        class Carve:
            def __init__(self, at=0):
                self.at = at

            def __call__(self, shape, dt=F32):
                n = int(np.prod(shape))
                w = n if dt in (F32, I32) else -(-n // 2)
                v = arena[:, self.at:self.at + w]
                if dt is not F32:
                    v = v.bitcast(dt)
                self.at += w
                assert self.at <= ARENA, self.at
                if len(shape) == 1:
                    return v
                names = "abcd"[:len(shape)]
                return v.rearrange(f"p ({' '.join(names)}) -> p {' '.join(names)}",
                                   **{m: s for m, s in zip(names[1:], shape[1:])})

        def psum(stack, name, shape, dt=F32):
            return stack.enter_context(nc.psum_tensor(name, shape, dt))

        carve = Carve()
        tile_hot = [carve([TILES, CCOL], BF16) for _ in range(2)]
        rank = [carve([TILES, CCOL]) for _ in range(2)]
        lo_hot = [carve([CCOL, P], F16)]
        hi_hot = [carve([CCOL, HI], F16) for _ in range(2)]
        hi_val = [carve([CCOL, 2, HI], F16)]
        scan_keep = carve([TILES, CCOL], BF16)
        edge_tile = carve([SORTS, ECOL])
        edge_val = carve([SORTS, ECOL])
        edge_low = carve([SORTS, ECOL])
        hi_val.append(Carve(carve.at)([CCOL, 2, HI], F16))
        edge_i = carve([3, ECOL], I32)
        ints = carve([2, ECOL], I32)
        zero = carve([512])
        abc = carve([2 * HD])
        w_in = carve([2, DIM])
        prod = carve([HD])
        early = ctx.enter_context(ExitStack())

        def sbe(name, shape, dt=F32):
            return early.enter_context(nc.sbuf_tensor(name, shape, dt))

        hbuf = [sb(f"hbuf{i}", [P, DIM]) for i in range(2)]
        hT = [sb(f"hT{i}", [P, 2, P]) for i in range(2)]
        proj = [sb(f"proj{i}", [P, TW + 2]) for i in range(2)]
        stats = sb("stats", [P, TILES, 6])
        Wx = sbe("Wx", [P, 2, TW + 2])
        b_in = sbe("b_in", [1, DIM])
        below = sbe("below", [P, P], BF16)
        allone = sbe("allone", [P, P], BF16)
        iota_i = sbe("iota_i", [P, P], I32)
        totals = [sbe(f"totals{i}", [P, TILES], BF16) for i in range(2)]
        gran_i = [sbe(f"gran_i{i}", [P, 2, TILES], I32) for i in range(2)]
        gran_f = [sbe(f"gran_f{i}", [P, 2, TILES]) for i in range(2)]
        pos_f = [sbe(f"pos_f{i}", [P, CCOL]) for i in range(2)]
        pos_i = [sbe(f"pos_i{i}", [P, 4, CCOL], I32) for i in range(2)]
        gran_n = sbe("gran_n", [P, TILES, ALLC])
        gran_at = sbe("gran_at", [P, ALLC, TILES + 1])
        packed = sbe("packed", [P, ALLC, 2, HI], F16)
        one_row = sbe("one_row", [P, TILES])


        with ExitStack() as ps:
            pT = [psum(ps, f"pT{i}", [P, 2, P]) for i in range(2)]
            pP = [psum(ps, f"pP{i}", [P, 512]) for i in range(2)]
            pB = [psum(ps, f"pB{i}", [P, 512]) for i in range(2)]
            pC = [psum(ps, f"pC{i}", [P, 512]) for i in range(2)]
            edges_in, weights_in, x_in, zeroed = sem("edges_in"), sem("weights_in"), sem("x_in"), sem("zeroed")
            pool_c, consts, dve_c = sem("pool_c"), sem("consts"), sem("dve_c")
            x_padded, stats_done, std_done, ln_ready = (sem("x_padded"), sem("stats_done"), sem("std_done"), sem("ln_ready"))
            w_ready = sem("w_ready")
            h_ready, hT_ps, hT_ready, proj_ps, proj_ready = (sem("h_ready"), sem("hT_ps"), sem("hT_ready"),
                                                             sem("proj_ps"), sem("proj_ready"))
            proj_out = [sem(f"proj_out{i}") for i in range(2)]
            st_a = sem("st_a")
            (tile_hots, ranks, totals_ready, counted, padded, in_granules, tile_ends, tile_starts, bases, based, masked_ranks,
             ranked, places, fields, columns, lo_hots, hi_hots, values, compact, packed_ready) = (sem(x) for x in (
                 "tile_hots", "ranks", "totals_ready", "counted", "padded", "in_granules", "tile_ends", "tile_starts", "bases", "based",
                 "masked_ranks", "ranked", "places", "fields", "columns", "lo_hots", "hi_hots", "values", "compact", "packed_ready"))
            SPLIT = 2 * CHUNKS - 1
            assert SPLIT + CHUNKS - 1 == TILES

            def tiles_beside(stages):
                def run(k):
                    second = k.least >= CHUNKS
                    j = k.least - second * CHUNKS
                    n = 2 if second == (j == CHUNKS - 1) else 1
                    for i in range(n):
                        for lag, fn in stages:
                            if second:
                                v, least = k.v + (SPLIT - CHUNKS + i - lag), j + SPLIT + i - lag
                                half = k.round + (SPLIT + j % 2 + i - lag) // 2
                            else:
                                v, least = k.v * 2 + (i - lag), j * 2 + i - lag
                                half = k.round * 2 + (j % 2 * 2 + i - lag) // 2
                            if 0 <= least < TILES:
                                fn(Step(v, least, half))
                return run
            with nc.Block() as block:

                @block.sync
                def _(sp):
                    for n, name in enumerate(("src", "dst", "edge_type_16")):
                        sp.dma_start(edge_i[0:EPART, n, :], A[name].rearrange("(p c) -> p c", c=ECOL)).then_inc(edges_in, 16)
                    sp.wait_ge(x_padded, 1)
                    sp.dma_start(X[:, 0:FULL, :], A["x"][0:FULL * P, :].rearrange("(t p) d -> p t d", p=P)).then_inc(x_in, 16)
                    sp.dma_start(X[0:REST, FULL, :], A["x"][FULL * P:NODES, :]).then_inc(x_in, 16)
                    sp.dma_start(w_in[:, :, :], A["L0_gnn_W_w"].rearrange("(k p) n -> p k n", p=P)).then_inc(weights_in, 16)
                    sp.dma_start(abc, A["L0_gnn_a"].rearrange("(o n) -> o n", o=1).to_broadcast([P, 2 * HD])).then_inc(weights_in, 16)
                    sp.dma_start(b_in[:, :], A["L0_gnn_W_b"].rearrange("(o n) -> o n", o=1)).then_inc(weights_in, 16)
                    sp.wait_ge(x_padded, 2)
                    for s in range(SORTS):
                        rows = records[s * REGION:s * REGION + GROUPS * GPG, :].rearrange("(g r) w -> g (r w)", r=GPG)
                        for g in range(0, GROUPS, P):
                            m = min(P, GROUPS - g)
                            sp.dma_start(rows[g:g + m, :], zero[0:m, :]).then_inc(zeroed, 16)

                    def store(k):
                        sp.wait_ge(proj_ready, k.v + 1)
                        sp.dma_start(wh_table.rearrange("(t p) c -> t p c", p=P)[bass.ds(k.v, 1), :, :].rearrange("t p c -> p (t c)"),
                                     proj[k.slot(2)][:, 0:TW]).then_inc(proj_out[k.slot(2)], 16)
                    repeat(sp, TILES, 2, [(0, store)])
                    sp.wait_ge(proj_out[0], 16 * (TILES - TILES // 2))
                    sp.wait_ge(proj_out[1], 16 * (TILES // 2))
                    sp.wait_ge(zeroed, 16 * SORTS * -(-GROUPS // P))

                @block.gpsimd
                def _(g):
                    g.iota(iota_i[:, :], pattern=[[1, P]], base=0, channel_multiplier=0).then_inc(pool_c, 1)
                    g.memset(ident[:, :], 0.0).then_inc(pool_c, 1)
                    g.memset(below[:, :], 1.0).then_inc(pool_c, 1)
                    g.wait_ge(pool_c, 3)
                    g.affine_select(out=ident[:, :], in_=ident[:, :], compare_op=ALU.not_equal, fill=1.0, base=0,
                                    pattern=[[-1, P]], channel_multiplier=1).then_inc(pool_c, 1)
                    g.affine_select(out=below[:, :], in_=below[:, :], compare_op=ALU.is_gt, fill=0.0, base=0,
                                    pattern=[[1, P]], channel_multiplier=-1).then_inc(pool_c, 1)

                    def add_bases(k):
                        sl = k.slot(2)
                        g.wait_ge(bases, k.v + 1)
                        g.tensor_tensor(rank[sl], rank[sl], gran_f[sl][:, 0, :, None].to_broadcast([P, TILES, CCOL]), ALU.add).then_inc(based, 1)

                    def mask_ranks(k):
                        sl = k.slot(2)
                        g.wait_ge(based, k.v + 1)
                        g.tensor_tensor(rank[sl], rank[sl], tile_hot[sl], ALU.mult).then_inc(masked_ranks, 1)

                    def put_values(k):
                        g.wait_ge(hi_hots, k.v + 1)
                        if k.past(2):
                            g.wait_ge(compact, 2 * k.v - 2)
                        for i, field in enumerate((edge_val, edge_low)):
                            part = field.rearrange("p s c -> p (s c)")[:, bass.ds(k.v * CCOL, CCOL)]
                            last = g.tensor_tensor(hi_val[k.slot(2)][:, :, i, :], hi_hot[k.slot(2)],
                                                   part[:, :, None].to_broadcast([P, CCOL, HI]), ALU.mult)
                        last.then_inc(values, 1)
                    for s in range(SORTS):
                        repeat(g, CHUNKS, 2, [(3, put_values), (1, add_bases), (1, mask_ranks)], start=s * CHUNKS)

                @block.scalar
                def _(act):
                    act.wait_ge(stats_done, TILES)
                    act.activation(rstd[:, :], mv[:, :, 1], ACT.Sqrt, bias=eps[:, 0:1]).then_inc(std_done, 1)
                    act.wait_ge(ln_ready, 1)

                    def norm(k):
                        if k.past(2):
                            act.wait_ge(hT_ps, k.v - 1)
                        act.activation(hbuf[k.slot(2)][:, :], X[:, bass.ds(k.v, 1), :].rearrange("p t d -> p (t d)"), ACT.Relu,
                                       bias=nbias[:, bass.ds(k.v, 1)], scale=rstd[:, bass.ds(k.v, 1)]).then_inc(h_ready, 1)

                    def move_hT(k):
                        act.wait_ge(hT_ps, k.v + 1)
                        if k.past(2):
                            act.wait_ge(proj_ps, k.v - 1)
                        act.activation(hT[k.slot(2)][:, :, :], pT[k.slot(2)][:, :, :], ACT.Copy).then_inc(hT_ready, 1)

                    def move_proj(k):
                        act.wait_ge(proj_ps, k.v + 1)
                        if k.past(2):
                            act.wait_ge(proj_out[k.slot(2)], k.round * 16)
                        act.activation(proj[k.slot(2)][:, 0:TW], pP[k.slot(2)][:, 0:TW], ACT.Copy)
                        act.activation(SM[:, bass.ds(k.v, 1), 0:2].rearrange("p t c -> p (t c)"), pP[k.slot(2)][:, TW:TW + 2], ACT.Copy).then_inc(proj_ready, 1)
                    def move_packed(k):
                        act.wait_ge(compact, 2 * k.v + 2)
                        act.activation(packed[:, bass.ds(k.v, 1), :, :].rearrange("p c f h -> p (c f h)"),
                                       pC[k.slot(2)][:, 0:2 * HI], ACT.Copy).then_inc(packed_ready, 1)
                    for s in range(SORTS):
                        repeat(act, CHUNKS, 2, [(4, move_packed), (0, tiles_beside([(0, norm), (1, move_hT), (2, move_proj)]))],
                               start=s * CHUNKS)

                def layernorm_stats(v):
                    def one(k):
                        v.bn_stats(stats[:, bass.ds(k.v, 1), :].rearrange("p t c -> p (t c)"),
                                   X[:, bass.ds(k.v, 1), :].rearrange("p t d -> p (t d)")).then_inc(st_a, 1)
                    repeat(v, TILES, 2, [(0, one)])
                    v.wait_ge(st_a, TILES)
                    for t in range(TILES):
                        v.bn_aggr(mv[:, t, :], stats[:, t, :]).then_inc(stats_done, 1)
                    v.wait_ge(std_done, 1)
                    v.reciprocal(rstd[:, :], rstd[:, :]).then_inc(std_done, 1)
                    v.wait_ge(std_done, 2)
                    v.scalar_tensor_tensor(nbias[:, :], mv[:, :, 0], -1.0, rstd[:, :], ALU.mult, ALU.mult).then_inc(ln_ready, 1)

                @block.vector
                def _(v):
                    n = [0]

                    def chain(ins):
                        n[0] += 1
                        ins.then_inc(dve_c, 1)
                        v.wait_ge(dve_c, n[0])

                    v.memset(X[:, FULL, :], 0.0).then_inc(x_padded, 1)
                    v.memset(zero, 0.0).then_inc(x_padded, 1)
                    v.memset(eps[:, :], EPS)
                    v.memset(ones_row[:, :], 1.0)
                    v.memset(allone[:, :], 1.0)
                    v.memset(one_row[:, :], 1.0)
                    v.memset(SM[:, :, 2:4], -BIG)
                    v.memset(scan_keep[:, :, :], 1.0)
                    v.memset(edge_tile[:, :, :], -1.0)
                    v.memset(edge_val[:, :, :], 0.0)
                    v.memset(edge_low[:, :, :], 0.0)
                    v.memset(Wx[:, :, :], 0.0)
                    chain(v.memset(row1[:, :], 0.0))
                    v.memset(scan_keep[:, :, 0:1], 0.0)
                    v.memset(row1[:, HD:HD + 1], 1.0)
                    v.memset(row1[:, HW + HD:HW + HD + 1], 1.0)
                    v.wait_ge(pool_c, 5)
                    v.tensor_copy(iota[:, :], iota_i[:, :])
                    v.tensor_copy(identb[:, :], ident[:, :])
                    v.tensor_copy(iotab[:, :], iota_i[:, :])
                    E = slice(0, EPART)
                    v.wait_ge(edges_in, 48)
                    v.tensor_single_scalar(ints[E, 0, :], edge_i[E, 0, :], 7, ALU.arith_shift_right)
                    chain(v.tensor_single_scalar(ints[E, 1, :], edge_i[E, 0, :], 127, ALU.bitwise_and))
                    v.tensor_copy(edge_tile[E, 0, :], ints[E, 0, :])
                    chain(v.scalar_tensor_tensor(edge_val[E, 0, :], edge_i[E, 1, :], float(P), ints[E, 1, :], ALU.mult, ALU.add))
                    chain(v.tensor_scalar(edge_val[E, 0, :], edge_val[E, 0, :], 1.0, None, ALU.add))
                    v.scalar_tensor_tensor(edge_val[E, 1, :], edge_i[E, 0, :], float(RELS), edge_i[E, 2, :], ALU.mult, ALU.add)
                    v.tensor_single_scalar(ints[E, 0, :], edge_i[E, 1, :], 7, ALU.arith_shift_right)
                    chain(v.tensor_single_scalar(ints[E, 1, :], edge_i[E, 1, :], 127, ALU.bitwise_and))
                    v.tensor_copy(edge_tile[E, 1, :], ints[E, 0, :])
                    chain(v.scalar_tensor_tensor(edge_val[E, 1, :], edge_val[E, 1, :], float(P), ints[E, 1, :], ALU.mult, ALU.add))
                    chain(v.tensor_scalar(edge_val[E, 1, :], edge_val[E, 1, :], 1.0, None, ALU.add))
                    chain(v.tensor_copy(ints[E, :, :], edge_val[E, :, :]))
                    chain(v.tensor_single_scalar(edge_i[E, 0:2, :], ints[E, :, :], LOW, ALU.arith_shift_right))
                    chain(v.tensor_scalar(edge_val[E, :, :], edge_i[E, 0:2, :], float(-CENTER), None, ALU.add))
                    chain(v.tensor_single_scalar(edge_i[E, 0:2, :], ints[E, :, :], 2 ** LOW - 1, ALU.bitwise_and))
                    chain(v.tensor_scalar(edge_low[E, :, :], edge_i[E, 0:2, :], float(2 ** (LOW - 1)), None, ALU.is_ge))
                    chain(v.scalar_tensor_tensor(edge_low[E, :, :], edge_i[E, 0:2, :], -float(2 ** (LOW - 1)), edge_low[E, :, :], ALU.add, ALU.add))
                    v.wait_ge(weights_in, 48)
                    for k in range(3):
                        w_rows, w_to = (w_in[:, k, :], Wx[:, k, :]) if k < 2 else (b_in[0:1, :], row1[0:1, :])
                        q = slice(0, P if k < 2 else 1)
                        for h in range(HEADS):
                            v.tensor_copy(w_to[:, h * HW:h * HW + HD], w_rows[:, h * HD:(h + 1) * HD])
                            for c, a in ((TCOL + h, HD), (TW + h, 0)):
                                chain(v.tensor_tensor_reduce(out=prod[q], in0=w_rows[:, h * HD:(h + 1) * HD], in1=abc[q, a:a + HD],
                                                             scale=1.0, scalar=0.0, op0=ALU.mult, op1=ALU.add,
                                                             accum_out=w_to[:, c:c + 1]))
                    v.tensor_copy(row1[0:1, HD:HD + 1], row1[0:1, HD:HD + 1]).then_inc(w_ready, 1)
                    v.wait_ge(x_in, 32)
                    layernorm_stats(v)

                    def chunk(a, k):
                        return a.rearrange("p s c -> p (s c)")[:, bass.ds(k.v * CCOL, CCOL)]

                    def hot_tiles(k):
                        v.tensor_tensor(tile_hot[k.slot(2)], chunk(edge_tile, k)[:, None, :].to_broadcast([P, TILES, CCOL]),
                                        iota[:, 0:TILES, None].to_broadcast([P, TILES, CCOL]), ALU.is_equal).then_inc(tile_hots, 1)

                    def rank_edges(k):
                        v.wait_ge(tile_hots, k.v + 1)
                        v.tensor_tensor_scan(rank[k.slot(2)].rearrange("p b t -> p (b t)"), scan_keep.rearrange("p b t -> p (b t)"),
                                             tile_hot[k.slot(2)].rearrange("p b t -> p (b t)"), 0.0, ALU.mult, ALU.add).then_inc(ranks, 1)

                    def total_tiles(k):
                        v.wait_ge(ranks, k.v + 1)
                        v.tensor_copy(totals[k.slot(2)][:, :], rank[k.slot(2)][:, :, CCOL - 1]).then_inc(totals_ready, 1)

                    def pad(k):
                        v.wait_ge(counted, k.v + 1)
                        v.tensor_scalar(gran_i[k.slot(2)][:, 0, :], pB[k.slot(2)][:, TILES:2 * TILES], float(GRAN - 1), None, ALU.add).then_inc(padded, 1)

                    def to_granules(k):
                        gi = gran_i[k.slot(2)]
                        v.wait_ge(padded, k.v + 1)
                        v.tensor_single_scalar(gi[:, 1, :], gi[:, 0, :], GRAN.bit_length() - 1, ALU.arith_shift_right).then_inc(in_granules, 1)

                    def ends(k):
                        gi, gf = gran_i[k.slot(2)], gran_f[k.slot(2)]
                        v.wait_ge(in_granules, k.v + 1)
                        v.tensor_scalar(gran_n[:, :, bass.ds(k.v, 1)].rearrange("p b c -> p (b c)"), gi[:, 1, :], 0.0, None, ALU.add)
                        v.tensor_tensor_scan(gf[:, 0, :], one_row[:, :], gi[:, 1, :], 0.0, ALU.mult, ALU.add).then_inc(tile_ends, 1)

                    def starts(k):
                        gi, gf = gran_i[k.slot(2)], gran_f[k.slot(2)]
                        v.wait_ge(tile_ends, k.v + 1)
                        v.tensor_scalar(gran_at[:, bass.ds(k.v, 1), TILES:TILES + 1].rearrange("p c b -> p (c b)"), gf[:, 0, TILES - 1:TILES], 0.0, None, ALU.add)
                        v.tensor_tensor(gf[:, 1, :], gf[:, 0, :], gi[:, 1, :], ALU.subtract).then_inc(tile_starts, 1)

                    def base(k):
                        gf = gran_f[k.slot(2)]
                        v.wait_ge(tile_starts, k.v + 1)
                        v.tensor_scalar(gran_at[:, bass.ds(k.v, 1), 0:TILES].rearrange("p c b -> p (c b)"), gf[:, 1, :], 0.0, None, ALU.add)
                        v.scalar_tensor_tensor(gf[:, 0, :], gf[:, 1, :], float(GRAN), pB[k.slot(2)][:, 0:TILES], ALU.mult, ALU.add).then_inc(bases, 1)

                    def rank_sum(k):
                        v.wait_ge(masked_ranks, k.v + 1)
                        v.tensor_reduce(pos_f[k.slot(2)][:, :], rank[k.slot(2)].rearrange("p b t -> p t b"), AX.X, ALU.add).then_inc(ranked, 1)

                    def place(k):
                        v.wait_ge(ranked, k.v + 1)
                        v.tensor_scalar(pos_i[k.slot(2)][:, 0, :], pos_f[k.slot(2)][:, :], -1.0, 0.0, ALU.add, ALU.max).then_inc(places, 1)

                    def split_place(k):
                        pi = pos_i[k.slot(2)]
                        v.wait_ge(places, k.v + 1)
                        v.tensor_scalar(pi[:, 1, :], pi[:, 0, :], 3, P - 1, ALU.arith_shift_right, ALU.bitwise_and)
                        v.tensor_scalar(pi[:, 2, :], pi[:, 0, :], 10, 3, ALU.arith_shift_right, ALU.logical_shift_left)
                        v.tensor_single_scalar(pi[:, 3, :], pi[:, 0, :], GRAN - 1, ALU.bitwise_and).then_inc(fields, 1)

                    def column(k):
                        pi = pos_i[k.slot(2)]
                        v.wait_ge(fields, k.v + 1)
                        v.tensor_tensor(pi[:, 3, :], pi[:, 3, :], pi[:, 2, :], ALU.bitwise_or).then_inc(columns, 1)

                    def hot_rows(part):
                        c = slice(part * CCOL // 2, (part + 1) * CCOL // 2)

                        def half(k):
                            if k.past(1):
                                v.wait_ge(compact, 2 * k.v - 1 + part)
                            v.tensor_tensor(lo_hot[0][:, c, :], iota[:, None, :].to_broadcast([P, CCOL // 2, P]),
                                            pos_i[k.slot(2)][:, 1, c, None].to_broadcast([P, CCOL // 2, P]), ALU.is_equal).then_inc(lo_hots, 1)
                        return half

                    def hot_columns(k):
                        v.wait_ge(columns, k.v + 1)
                        if k.past(2):
                            v.wait_ge(values, k.v - 1)
                        v.tensor_tensor(hi_hot[k.slot(2)], iota[:, None, 0:HI].to_broadcast([P, CCOL, HI]),
                                        pos_i[k.slot(2)][:, 3, :, None].to_broadcast([P, CCOL, HI]), ALU.is_equal).then_inc(hi_hots, 1)
                    for s in range(SORTS):
                        repeat(v, CHUNKS, 2, [(3, column), (3, hot_columns), (3, hot_rows(0)), (1, pad), (2, rank_sum), (1, to_granules), (3, hot_rows(1)), (1, ends), (2, place), (1, starts), (0, hot_tiles), (1, base), (0, rank_edges), (2, split_place), (0, total_tiles)], start=s * CHUNKS)

                @block.tensor
                def _(pe):
                    pe.wait_ge(w_ready, 1)

                    def transpose_h(k):
                        pe.wait_ge(h_ready, k.v + 1)
                        if k.past(2):
                            pe.wait_ge(hT_ready, k.v - 1)
                        for j in range(2):
                            last = pe.transpose(pT[k.slot(2)][:, j, :], hbuf[k.slot(2)][:, j * P:(j + 1) * P], ident[:, :])
                        last.then_inc(hT_ps, 1)

                    def project(k):
                        pe.wait_ge(hT_ready, k.v + 1)
                        if k.past(2):
                            pe.wait_ge(proj_ready, k.v - 1)
                        o = pP[k.slot(2)][:, 0:TW + 2]
                        pe.matmul(o, hT[k.slot(2)][:, 0, :], Wx[:, 0, :], start=True, stop=False)
                        pe.matmul(o, hT[k.slot(2)][:, 1, :], Wx[:, 1, :], start=False, stop=False)
                        pe.matmul(o, ones_row[0:1, :], row1[0:1, :], start=False, stop=True).then_inc(proj_ps, 1)
                    def count(k):
                        pe.wait_ge(totals_ready, k.v + 1)
                        if k.past(2):
                            pe.wait_ge(bases, k.v - 1)
                        pe.matmul(pB[k.slot(2)][:, 0:TILES], below[:, :], totals[k.slot(2)][:, :], start=True, stop=True)
                        pe.matmul(pB[k.slot(2)][:, TILES:2 * TILES], allone[:, :], totals[k.slot(2)][:, :], start=True, stop=True).then_inc(counted, 1)

                    def compaction(k):
                        pe.wait_ge(values, k.v + 1)
                        if k.past(2):
                            pe.wait_ge(packed_ready, k.v - 1)
                        for half in range(2):
                            pe.wait_ge(lo_hots, 2 * k.v + half + 1)
                            for t in range(half * CCOL // 2, (half + 1) * CCOL // 2):
                                last = pe.matmul(pC[k.slot(2)][:, 0:2 * HI], lo_hot[0][:, t, :], hi_val[k.slot(2)][:, t, :, :].rearrange("p f h -> p (f h)"), start=(t == 0), stop=(t == CCOL - 1))
                            last.then_inc(compact, 1)
                    for s in range(SORTS):
                        repeat(pe, CHUNKS, 2, [(3, compaction), (0, count), (0, tiles_beside([(0, transpose_h), (1, project)]))],
                               start=s * CHUNKS)

        carve = Carve()
        number = carve([ALLC, HI])
        part = [carve([ALLC, HI]) for _ in range(2)]
        after = carve([TILES, ALLC])
        keep_c = carve([TILES, ALLC])
        shift = carve([ALLC, TILES + 1])
        delta = carve([ALLC, TILES + 1])
        ge = carve([CHUNKS, GCOLS, TILES + 1])
        dest = carve([ALLC, GCOLS])
        dest_i = carve([ALLC, GCOLS], I32)
        gid = carve([GCOLS])
        gid_i = carve([GCOLS], I32)
        unused = carve([ALLC])
        unused_i = carve([ALLC], I32)
        group_id = carve([3])
        group_i = carve([3], I32)
        sup_i = carve([SORTS, TILES], I32)
        sup_f = carve([2, SORTS, TILES])
        tile_of = carve([3, TILES])
        tile_f = carve([3])
        tile_i = carve([SORTS, 3], I32)
        EVEN = CHUNKS // 2 * 2
        with ExitStack() as ps:
            p2p, p2, dest_ready, gtile_ready, gt_out, gt_in = (sem("p2p"), sem("p2"), sem("dest_ready"), sem("gtile_ready"),
                                                               sem("gt_out"), sem("gt_in"))
            staged = sem("staged")
            scattered = [sem(f"scattered{i}") for i in range(2)]
            stage_v = [sbe(f"stage_v{i}", [P, GCOLS, GRAN]) for i in range(2)]
            stage_d = [sbe(f"stage_d{i}", [P, GCOLS], I32) for i in range(2)]
            with nc.Block() as block:

                @block.gpsimd
                def _(g):
                    g.iota(gid_i, pattern=[[P, GCOLS]], base=0, channel_multiplier=1).then_inc(p2p, 1)
                    g.iota(group_i, pattern=[[P, 3]], base=0, channel_multiplier=1).then_inc(p2p, 1)
                    for s in range(SORTS):
                        g.iota(unused_i[:, s * CHUNKS:(s + 1) * CHUNKS], pattern=[[GCOLS * P, CHUNKS]],
                               base=s * REGION + GROUPS * GPG, channel_multiplier=0).then_inc(p2p, 1)

                    def scatter(k):
                        sl = k.slot(2)
                        g.wait_ge(staged, k.v + 1)
                        g.nop(nofuse=True)
                        for j in range(GCOLS):
                            g.indirect_dma_start(records, bass.IndirectOffsetOnAxis(ap=stage_d[sl][:, j:j + 1], axis=0),
                                                 stage_v[sl][:, j, :], None).then_inc(scattered[sl], 16)
                    repeat(g, ALLC, 2, [(0, scatter)])
                    for i in range(2):
                        g.wait_ge(scattered[i], 16 * GCOLS * ALLC // 2)

                @block.scalar
                def _(act):
                    def stage(k):
                        sl = k.slot(2)
                        if k.past(2):
                            uses = k.round + (EVEN // 2 if k.past(EVEN) else 0)
                            act.wait_ge(scattered[sl], uses * (16 * GCOLS))
                        act.activation(stage_v[sl].rearrange("p g r -> p (g r)"), number[:, bass.ds(k.v, 1), :].rearrange("p c h -> p (c h)"), ACT.Copy)
                        act.copy(stage_d[sl][:, :], dest_i[:, bass.ds(k.v, 1), :].rearrange("p c g -> p (c g)")).then_inc(staged, 1)
                    act.wait_ge(dest_ready, 1)
                    repeat(act, EVEN, 2, [(0, stage)])
                    act.wait_ge(dest_ready, 2)
                    repeat(act, ALLC - EVEN, 2, [(0, stage)], start=EVEN)

                @block.sync
                def _(sp):
                    sp.wait_ge(gtile_ready, 1)
                    for s in range(SORTS):
                        with nc.allow_non_contiguous_dma(reason="three numbers of a partition"):
                            sp.dma_start(gtile_dram[s, :].rearrange("(q p) -> p q", p=P), tile_i[:, s, :]).then_inc(gt_out, 16)
                    sp.wait_ge(gt_out, 16 * SORTS)
                    sp.dma_start(gtile[0:1, :, :], gtile_dram[:, 0:GROUPS].rearrange("(o s) g -> o s g", o=1)).then_inc(gt_in, 16)
                    sp.wait_ge(gt_in, 16)

                @block.vector
                def _(v):
                    n = [0]

                    def chain(ins):
                        n[0] += 1
                        ins.then_inc(p2, 1)
                        v.wait_ge(p2, n[0])
                    high, low = packed[:, :, 0, :], packed[:, :, 1, :]
                    v.tensor_scalar(part[0], low, 0.0, -1.0, ALU.is_gt, ALU.mult)
                    v.tensor_scalar(part[1], low, 0.0, float((CENTER << LOW) + 2 ** (LOW - 1)), ALU.not_equal, ALU.mult)
                    chain(v.scalar_tensor_tensor(number, high, float(2 ** LOW), low, ALU.mult, ALU.add))
                    chain(v.tensor_tensor(number, number, part[0], ALU.add))
                    chain(v.tensor_tensor(number, number, part[1], ALU.add))
                    chain(v.memset(keep_c[:, :, :], 1.0))
                    v.memset(keep_c[:, :, 0:1], 0.0)
                    chain(v.memset(keep_c[:, :, CHUNKS:CHUNKS + 1], 0.0))
                    v.wait_ge(p2p, 4)
                    v.tensor_copy(gid, gid_i)
                    v.tensor_copy(group_id, group_i)
                    v.tensor_copy(unused, unused_i)
                    chain(v.tensor_tensor_scan(after.rearrange("p b c -> p (b c)"), keep_c.rearrange("p b c -> p (b c)"),
                                               gran_n[:, :, :].rearrange("p b c -> p (b c)"), 0.0, ALU.mult, ALU.add))
                    for s in range(SORTS):
                        total = after[:, :, s * CHUNKS + CHUNKS - 1]
                        chain(v.tensor_scalar(sup_i[:, s, :], total, float(GPG - 1), None, ALU.add))
                        chain(v.tensor_single_scalar(sup_i[:, s, :], sup_i[:, s, :], GPG.bit_length() - 1, ALU.arith_shift_right))
                        chain(v.tensor_tensor_scan(sup_f[:, 0, s, :], one_row[:, :], sup_i[:, s, :], 0.0, ALU.mult, ALU.add))
                        chain(v.tensor_tensor(sup_f[:, 0, s, :], sup_f[:, 0, s, :], sup_i[:, s, :], ALU.subtract))
                        chain(v.tensor_tensor(tile_of, group_id[:, :, None].to_broadcast([P, 3, TILES]),
                                              sup_f[:, 0, s, None, :].to_broadcast([P, 3, TILES]), ALU.is_ge))
                        chain(v.tensor_reduce(tile_f, tile_of, AX.X, ALU.add))
                        chain(v.tensor_scalar(tile_i[:, s, :], tile_f, -1.0, None, ALU.add))
                        chain(v.tensor_scalar(sup_f[:, 1, s, :], sup_f[:, 0, s, :], float(GPG), float(s * REGION), ALU.mult, ALU.add))
                    v.tensor_copy(tile_i[:, 0, 0:1], tile_i[:, 0, 0:1]).then_inc(gtile_ready, 1)
                    chain(v.tensor_tensor(after, after, gran_n[:, :, :], ALU.subtract))
                    for s in range(SORTS):
                        cs = slice(s * CHUNKS, (s + 1) * CHUNKS)
                        v.tensor_tensor(shift[:, cs, 0:TILES].rearrange("p c b -> p b c"), after[:, :, cs],
                                        sup_f[:, 1, s, :, None].to_broadcast([P, TILES, CHUNKS]), ALU.add)
                    chain(v.tensor_copy(shift[:, :, TILES], unused))
                    chain(v.tensor_tensor(shift[:, :, 0:TILES], shift[:, :, 0:TILES], gran_at[:, :, 0:TILES], ALU.subtract))
                    v.tensor_copy(delta[:, :, 0], shift[:, :, 0])
                    chain(v.tensor_tensor(delta[:, :, 1:], shift[:, :, 1:], shift[:, :, 0:TILES], ALU.subtract))
                    for s in range(SORTS):
                        cs = slice(s * CHUNKS, (s + 1) * CHUNKS)
                        full = [P, CHUNKS, GCOLS, TILES + 1]
                        chain(v.tensor_tensor(ge, gid[:, None, :, None].to_broadcast(full), gran_at[:, cs, None, :].to_broadcast(full), ALU.is_ge))
                        chain(v.tensor_tensor(ge, ge, delta[:, cs, None, :].to_broadcast(full), ALU.mult))
                        chain(v.tensor_reduce(dest[:, cs, :], ge, AX.X, ALU.add))
                        v.tensor_tensor(dest_i[:, cs, :], dest[:, cs, :], gid[:, None, :].to_broadcast([P, CHUNKS, GCOLS]), ALU.add).then_inc(dest_ready, 1)

        early.close()
        slot_idx = [sb(f"slot_idx{s}", [P, GROUPS, SUB], I32) for s in range(SORTS)]
        slot_loc = sb("slot_loc", [P, GROUPS, SUB])
        slot_locb = [sb(f"slot_locb{s}", [P, GROUPS, SUB], BF16) for s in range(SORTS)]
        slot_rel = sb("slot_rel", [P, GROUPS, SUB])
        inv_deg = sb("inv_deg", [P, TILES, RELS])
        carve = Carve()
        QG = -(-GROUPS // P)
        rec_in = carve([SORTS, QG, GROUP])
        pk = carve([SORTS, GROUPS, SUB])
        nul = carve([GROUPS * SUB])
        qi = carve([GROUPS * SUB], I32)
        loc_i = carve([GROUPS * SUB], I32)
        rel_i = carve([GROUPS * SUB], I32)
        with ExitStack() as ps:
            pR = [psum(ps, f"pR{i}", [P, SUB, P]) for i in range(2)]
            rec_ld, rec_ps, rec_mv, p3 = sem("rec_ld"), sem("rec_ps"), sem("rec_mv"), sem("p3")
            blocks = [(s, q) for s in range(SORTS) for q in range(QG)]
            with nc.Block() as block:

                @block.sync
                def _(sp):
                    for s, q in blocks:
                        m = min(P, GROUPS - q * P)
                        rows = records[s * REGION:s * REGION + GROUPS * GPG, :].rearrange("(g r) w -> g (r w)", r=GPG)
                        sp.dma_start(rec_in[0:m, s, q, :], rows[q * P:q * P + m, :]).then_inc(rec_ld, 16)

                @block.tensor
                def _(pe):
                    pe.wait_ge(rec_ld, 16 * len(blocks))
                    for n, (s, q) in enumerate(blocks):
                        m = min(P, GROUPS - q * P)
                        if n >= 2:
                            pe.wait_ge(rec_mv, n - 1)
                        view = rec_in[0:m, s, q, :].rearrange("g (p j) -> g j p", j=SUB)
                        for j in range(SUB):
                            last = pe.transpose(pR[n % 2][:, j, 0:m], view[:, j, :], ident[0:m, 0:m])
                        last.then_inc(rec_ps, 1)

                @block.vector
                def _(v):
                    n = [0]

                    def chain(ins):
                        n[0] += 1
                        ins.then_inc(p3, 1)
                        v.wait_ge(p3, n[0])
                    for i, (s, q) in enumerate(blocks):
                        m = min(P, GROUPS - q * P)
                        v.wait_ge(rec_ps, i + 1)
                        v.tensor_copy(pk[:, s, q * P:q * P + m, :].rearrange("p g j -> p j g"), pR[i % 2][:, :, 0:m]).then_inc(rec_mv, 1)
                    v.wait_ge(rec_mv, len(blocks))
                    for s in range(SORTS):
                        val = pk[:, s, :, :].rearrange("p g j -> p (g j)")
                        loc = slot_loc[:, :, :].rearrange("p g j -> p (g j)")
                        row = slot_idx[s][:, :, :].rearrange("p g j -> p (g j)")
                        v.tensor_scalar(nul, val, 0.0, PADLOC, ALU.is_equal, ALU.mult)
                        chain(v.tensor_scalar(qi, val, -1.0, 0.0, ALU.add, ALU.max))
                        v.tensor_single_scalar(row, qi, 7, ALU.arith_shift_right)
                        chain(v.tensor_single_scalar(loc_i, qi, P - 1, ALU.bitwise_and))
                        chain(v.tensor_tensor(loc, loc_i, nul, ALU.add))
                        chain(v.tensor_copy(slot_locb[s][:, :, :].rearrange("p g j -> p (g j)"), loc))
                    chain(v.tensor_single_scalar(rel_i, slot_idx[1][:, :, :].rearrange("p g j -> p (g j)"), RELS - 1, ALU.bitwise_and))
                    chain(v.tensor_copy(slot_rel[:, :, :].rearrange("p g j -> p (g j)"), rel_i))

        RING = 8
        MRING = 4
        carve = Carve(ACCW)
        G = [carve([SUB, TW]) for _ in range(RING)]
        member = [carve([SUB, P]) for _ in range(MRING)]
        other = [carve([SUB, P], BF16) for _ in range(RING)]
        masked = [carve([HEADS, SUB, P]) for _ in range(2)]
        weight = [carve([HEADS, SUB, P]) for _ in range(2)]
        idx_ring = [sb(f"idx_ring{i}", [P, SUB], I32) for i in range(RING)]
        tile_max = [sb(f"tile_max{i}", [P, HEADS]) for i in range(2)]
        above = [sb(f"above{i}", [P, HEADS]) for i in range(2)]
        drop = [sb(f"drop{i}", [P, HEADS]) for i in range(2)]
        fade = [sb(f"fade{i}", [P, HEADS]) for i in range(4)]
        z = [sb(f"z{i}", [P, SUB, HEADS]) for i in range(2)]
        e_rec = [sb(f"e_rec{i}", [P, SUB, HEADS]) for i in range(MRING)]
        expo = [sb(f"expo{i}", [P, SUB, HEADS]) for i in range(2)]
        with ExitStack() as ps:
            pX = [psum(ps, f"pX{i}", [P, SUB, P]) for i in range(HEADS)]
            pA = [psum(ps, f"pA{i}", [P, 512]) for i in range(2)]
            pM = psum(ps, "pM", [P, SUB, P], BF16)
            pS = psum(ps, "pS", [P, 512])
            pMx = psum(ps, "pMx", [P, 512])
            (acc_zero, idx_ready, other_ready, otherT, member_ready, s_rec, z_ready, e_ready, masks_ready, maskedT, reduced, above_ready,
             m_ready, drop_ready, fade_ready, m_rec, expo_ready, weight_ready, agg_ps, acc_done) = (sem(x) for x in (
                 "acc_zero", "idx_ready", "other_ready", "otherT", "member_ready", "s_rec", "z_ready", "e_ready", "masks_ready",
                 "maskedT", "reduced", "above_ready", "m_ready", "drop_ready", "fade_ready", "m_rec", "expo_ready", "weight_ready",
                 "agg_ps", "acc_done"))
            got = [sem(f"got{i}") for i in range(RING)]
            with nc.Block() as block:

                @block.gpsimd
                def _(g):
                    def gather(k):
                        sl = k.slot(RING)
                        g.wait_ge(idx_ready, k.v + 1)
                        if k.past(RING):
                            g.wait_ge(agg_ps, k.v - (RING - 1))
                        g.nop(nofuse=True)
                        for c in range(SUB):
                            g.indirect_dma_start(G[sl][:, c, :], None, wh_table,
                                                 bass.IndirectOffsetOnAxis(ap=idx_ring[sl][:, c:c + 1], axis=0)).then_inc(got[sl], 16)
                    repeat(g, GROUPS, RING, [(0, gather)])

                @block.scalar
                def _(act):
                    def index(k):
                        sl = k.slot(RING)
                        if k.past(RING):
                            act.wait_ge(got[sl], k.round * (16 * SUB))
                        act.copy(idx_ring[sl][:, :], slot_idx[0][:, bass.ds(k.v, 1), :].rearrange("p g j -> p (g j)")).then_inc(idx_ready, 1)

                    def weigh(k):
                        act.wait_ge(expo_ready, k.v + 1)
                        if k.past(2):
                            act.wait_ge(agg_ps, k.v - 1)
                        for h in range(HEADS):
                            for c in range(SUB):
                                last = act.activation(weight[k.slot(2)][:, h, c, :], other[k.slot(RING)][:, c, :], ACT.Exp,
                                                      bias=expo[k.slot(2)][:, c, h:h + 1], scale=-BIG)
                        last.then_inc(weight_ready, 1)

                    def fades(k):
                        act.wait_ge(drop_ready, k.v + 1)
                        if k.past(4):
                            act.wait_ge(acc_done, k.v - 3)
                        act.activation(fade[k.slot(4)][:, :], drop[k.slot(2)][:, :], ACT.Exp).then_inc(fade_ready, 1)

                    def members(k):
                        act.wait_ge(otherT, k.v + 1)
                        if k.past(MRING):
                            act.wait_ge(m_rec, k.v - (MRING - 1))
                        act.activation(member[k.slot(MRING)], pM[:, :, :], ACT.Exp, scale=-BIG).then_inc(member_ready, 1)
                    repeat(act, GROUPS, RING, [(0, index), (3, members), (7, fades), (7, weigh)])

                @block.tensor
                def _(pe):
                    def transpose_other(k):
                        pe.wait_ge(other_ready, k.v + 1)
                        if k.past(1):
                            pe.wait_ge(member_ready, k.v)
                        for c in range(SUB):
                            last = pe.transpose(pM[:, c, :], other[k.slot(RING)][:, c, :], identb[:, :])
                        last.then_inc(otherT, 1)

                    def expand(k, first, to, ready, read):
                        b = pe.value_load(gtile[0:1, 0, bass.ds(k.v, 1)], min_val=0, max_val=TILES - 1)
                        pe.wait_ge(ready, k.v + 1)
                        if k.past(1):
                            pe.wait_ge(read, k.v)
                        for c in range(SUB):
                            last = pe.matmul(to[:, HEADS * c:HEADS * (c + 1)], member[k.slot(MRING)][:, c, :],
                                             SM[:, bass.ds(b, 1), first:first + HEADS].rearrange("p t c -> p (t c)"), start=True, stop=True)
                        return last

                    def expand_s(k):
                        expand(k, 0, pS, member_ready, z_ready).then_inc(s_rec, 1)

                    def expand_m(k):
                        expand(k, HEADS, pMx, m_ready, expo_ready).then_inc(m_rec, 1)

                    def transpose_masked(k):
                        for h in range(HEADS):
                            pe.wait_ge(masks_ready, HEADS * k.v + h + 1)
                            if k.past(1):
                                pe.wait_ge(reduced, HEADS * k.v + h - 1)
                            for c in range(SUB):
                                last = pe.transpose(pX[h][:, c, :], masked[k.slot(2)][:, h, c, :], ident[:, :])
                        last.then_inc(maskedT, 1)

                    def aggregate(k):
                        sl = k.slot(2)
                        pe.wait_ge(weight_ready, k.v + 1)
                        pe.wait_ge(got[k.slot(RING)], (k.round + 1) * (16 * SUB))
                        if k.past(2):
                            pe.wait_ge(acc_done, k.v - 1)
                        for h in range(HEADS):
                            for c in range(SUB):
                                last = pe.matmul(pA[sl][:, h * HW:(h + 1) * HW], weight[sl][:, h, c, :],
                                                 G[k.slot(RING)][:, c, h * HW:(h + 1) * HW], start=(c == 0), stop=(c == SUB - 1))
                        last.then_inc(agg_ps, 1)
                    repeat(pe, GROUPS, RING, [(5, transpose_masked), (2, transpose_other), (3, expand_s), (7, aggregate), (5, expand_m)])

                @block.vector
                def _(v):
                    v.memset(arena[:, 0:ACCW], 0.0).then_inc(acc_zero, 1)
                    v.wait_ge(acc_zero, 1)
                    full = [P, SUB, P]

                    def tile_register(k):
                        return v.value_load(gtile[0:1, 0, bass.ds(k.v, 1)], min_val=0, max_val=TILES - 1)

                    def others(k):
                        if k.past(RING):
                            v.wait_ge(weight_ready, k.v - (RING - 1))
                        v.tensor_tensor(other[k.slot(RING)], iotab[:, None, :].to_broadcast(full),
                                        slot_locb[0][:, bass.ds(k.v, 1), :].rearrange("p g j -> p (g j)")[:, :, None].to_broadcast(full),
                                        ALU.not_equal).then_inc(other_ready, 1)

                    def score(k):
                        v.wait_ge(s_rec, k.v + 1)
                        v.wait_ge(got[k.slot(RING)], (k.round + 1) * (16 * SUB))
                        v.tensor_tensor(z[k.slot(2)][:, :, :], G[k.slot(RING)][:, :, TCOL:TCOL + HEADS],
                                        pS[:, 0:HEADS * SUB].rearrange("p (c h) -> p c h", h=HEADS), ALU.add).then_inc(z_ready, 1)

                    def leaky(k):
                        v.wait_ge(z_ready, k.v + 1)
                        v.scalar_tensor_tensor(e_rec[k.slot(MRING)][:, :, :], z[k.slot(2)][:, :, :], SLOPE, z[k.slot(2)][:, :, :],
                                               ALU.mult, ALU.max).then_inc(e_ready, 1)

                    def mask(k):
                        v.wait_ge(e_ready, k.v + 1)
                        if k.past(2):
                            v.wait_ge(maskedT, k.v - 1)
                        for h in range(HEADS):
                            v.scalar_tensor_tensor(masked[k.slot(2)][:, h, :, :], other[k.slot(RING)], -BIG,
                                                   e_rec[k.slot(MRING)][:, :, h:h + 1].to_broadcast([P, SUB, P]),
                                                   ALU.mult, ALU.add).then_inc(masks_ready, 1)

                    def reduce(k):
                        v.wait_ge(maskedT, k.v + 1)
                        for h in range(HEADS):
                            v.tensor_reduce(tile_max[k.slot(2)][:, h:h + 1], pX[h][:, :, :].rearrange("p c e -> p (c e)"),
                                            AX.X, ALU.max).then_inc(reduced, 1)

                    def running(k):
                        b = tile_register(k)
                        M = SM[:, bass.ds(b, 1), HEADS:2 * HEADS].rearrange("p t c -> p (t c)")
                        v.wait_ge(reduced, HEADS * (k.v + 1))
                        if k.past(1):
                            v.wait_ge(m_ready, k.v)
                            v.wait_ge(m_rec, k.v)
                        v.tensor_tensor(above[k.slot(2)][:, :], M, tile_max[k.slot(2)][:, :], ALU.subtract).then_inc(above_ready, 1)
                        v.tensor_tensor(M, M, tile_max[k.slot(2)][:, :], ALU.max).then_inc(m_ready, 1)

                    def drops(k):
                        v.wait_ge(above_ready, k.v + 1)
                        if k.past(2):
                            v.wait_ge(fade_ready, k.v - 1)
                        v.tensor_scalar(drop[k.slot(2)][:, :], above[k.slot(2)][:, :], 0.0, None, ALU.min).then_inc(drop_ready, 1)

                    def exponent(k):
                        v.wait_ge(m_rec, k.v + 1)
                        if k.past(2):
                            v.wait_ge(weight_ready, k.v - 1)
                        v.tensor_tensor(expo[k.slot(2)][:, :, :], e_rec[k.slot(MRING)][:, :, :],
                                        pMx[:, 0:HEADS * SUB].rearrange("p (c h) -> p c h", h=HEADS), ALU.subtract).then_inc(expo_ready, 1)

                    def add(k):
                        b = tile_register(k)
                        v.wait_ge(agg_ps, k.v + 1)
                        v.wait_ge(fade_ready, k.v + 1)
                        if k.past(1):
                            v.wait_ge(acc_done, k.v)
                        for h in range(HEADS):
                            a = acc[:, bass.ds(b, 1), h * HW:(h + 1) * HW].rearrange("p t c -> p (t c)")
                            last = v.scalar_tensor_tensor(a, a, fade[k.slot(4)][:, h:h + 1], pA[k.slot(2)][:, h * HW:(h + 1) * HW], ALU.mult, ALU.add)
                        last.then_inc(acc_done, 1)
                    repeat(v, GROUPS, RING, [(2, others), (8, add), (6, exponent), (4, score), (5, reduce), (4, leaky), (5, running), (4, mask), (5, drops)])

        carve = Carve(ACCW)
        wr = carve([2, RELS * DIM])
        rel_out = [arena[:, 0:RELS * DIM], arena[:, RELS * DIM:2 * RELS * DIM]]
        W0T = carve([2, DIM])
        w0 = carve([2, DIM])
        own = [carve([TW]) for _ in range(2)]
        rden = carve([TILES, HEADS])
        alone = carve([TILES, HEADS])
        DEG = [-(-GROUPS // TILES), GROUPS // TILES]
        PAIR = sum(DEG)
        assert TILES // 2 * PAIR <= GROUPS <= TILES // 2 * PAIR + DEG[0]
        node_hot = [carve([DEG[0] * SUB, P], BF16) for _ in range(2)]
        rel_hot = [carve([DEG[0] * SUB, RELS], BF16) for _ in range(2)]
        deg_part = [carve([DEG[0], RELS]) for _ in range(2)]

        def deg_groups(k):
            m = min(DEG[k.slot(2)], GROUPS - (k.least // 2 * PAIR + k.slot(2) * DEG[0]))
            return k.round * PAIR + k.slot(2) * DEG[0], m
        with ExitStack() as ps:
            pT = [psum(ps, f"qT{i}", [P, 2, P]) for i in range(1)]
            pO = [psum(ps, f"qO{i}", [P, 512]) for i in range(1)]
            pH = [psum(ps, f"qH{i}", [P, 512]) for i in range(UNROLL)]
            w_ld, own_ready, d_c, x_c, x2_done, st2, st2_done, std2, ln2 = (sem(x) for x in (
                "w_ld", "own_ready", "d_c", "x_c", "x2_done", "st2", "st2_done", "std2", "ln2"))
            own_in = [sem(f"own_in{i}") for i in range(2)]
            own_used = sem("own_used")
            h2_ready, h2T_ps, h2T_ready, root_ps, root_add, rel_ps, w0_ps, w0_ready = (sem(x) for x in (
                "h2_ready", "h2T_ps", "h2T_ready", "root_ps", "root_add", "rel_ps", "w0_ps", "w0_ready"))
            rel_act, rel_dve = sem("rel_act"), sem("rel_dve")
            pD = [psum(ps, f"pD{i}", [P, 512]) for i in range(2)]
            deg_zero, deg_hot, deg_ps, deg_moved, deg_add, deg_done = (sem(x) for x in (
                "deg_zero", "deg_hot", "deg_ps", "deg_moved", "deg_add", "deg_done"))
            rel_st = [sem(f"rel_st{i}") for i in range(2)]
            with nc.Block() as block:

                @block.sync
                def _(sp):
                    for k in range(2):
                        sp.dma_start(wr[:, k, :].rearrange("p (r n) -> p r n", r=RELS),
                                     A["L1_gnn_W_r"][:, k * P:(k + 1) * P, :].rearrange("r p n -> p r n")).then_inc(w_ld, 16)
                    sp.dma_start(w0[:, :, :], A["L1_gnn_W0_w"].rearrange("(k p) n -> p k n", p=P)).then_inc(w_ld, 16)
                    sp.dma_start(row2[:, :], A["L1_gnn_W0_b"].rearrange("(o n) -> o n", o=1)).then_inc(w_ld, 16)

                    def own_rows(k):
                        if k.past(2):
                            sp.wait_ge(own_used, k.v - 1)
                        sp.dma_start(own[k.slot(2)][:, :], wh_table.rearrange("(t p) c -> t p c", p=P)[bass.ds(k.v, 1), :, :].rearrange("t p c -> p (t c)")
                                     ).then_inc(own_in[k.slot(2)], 16)
                    repeat(sp, TILES, 2, [(0, own_rows)])

                    def store(k):
                        sp.wait_ge(rel_act, (k.v + 1) * 4)
                        sp.wait_ge(rel_dve, (k.v + 1) * 4)
                        sp.dma_start(rel_table.rearrange("(t p r) n -> t p (r n)", p=P, r=RELS)[bass.ds(k.v, 1), :, :].rearrange("t p c -> p (t c)"),
                                     rel_out[k.slot(2)]).then_inc(rel_st[k.slot(2)], 16)
                    repeat(sp, TILES, 2, [(0, store)])
                    sp.wait_ge(rel_st[0], 16 * (TILES - TILES // 2))
                    sp.wait_ge(rel_st[1], 16 * (TILES // 2))

                @block.gpsimd
                def _(g):
                    g.memset(inv_deg[:, :, :], 0.0).then_inc(deg_zero, 1)
                    g.wait_ge(deg_zero, 1)

                    def add_degrees(k):
                        first, m = deg_groups(k)
                        for i in range(m):
                            b = g.value_load(gtile[0:1, 1, bass.ds(first + i, 1)], min_val=0, max_val=TILES - 1)
                            if i == 0:
                                g.wait_ge(deg_moved, k.v + 1)
                            if i or k.past(1):
                                g.wait_ge(deg_add, first + i)
                            d = inv_deg[:, bass.ds(b, 1), :].rearrange("p t r -> p (t r)")
                            g.tensor_tensor(d, d, deg_part[k.slot(2)][:, i, :], ALU.add).then_inc(deg_add, 1)
                    repeat(g, TILES, 2, [(0, add_degrees)])
                    g.wait_ge(deg_add, GROUPS)

                @block.vector
                def _(v):
                    den = acc[:, :, :].rearrange("p t (h w) -> p t h w", w=HW)[:, :, :, HD]
                    v.tensor_scalar(alone[:, :, :], den, 0.0, None, ALU.is_equal)
                    v.tensor_scalar(rden[:, :, :], den, 1e-30, None, ALU.max).then_inc(d_c, 1)
                    v.wait_ge(d_c, 1)
                    v.reciprocal(rden[:, :, :], rden[:, :, :]).then_inc(d_c, 1)
                    v.wait_ge(d_c, 2)

                    def residual(k):
                        t = bass.ds(k.v, 1)
                        for h in range(HEADS):
                            x = X[:, t, h * HD:(h + 1) * HD].rearrange("p t d -> p (t d)")
                            last = v.scalar_tensor_tensor(x, acc[:, t, h * HW:h * HW + HD].rearrange("p t d -> p (t d)"),
                                                          rden[:, t, h], x, ALU.mult, ALU.add)
                        last.then_inc(x_c, 1)

                    def residual_alone(k):
                        t = bass.ds(k.v, 1)
                        v.wait_ge(x_c, k.v + 1)
                        v.wait_ge(own_in[k.slot(2)], (k.round + 1) * 16)
                        for h in range(HEADS):
                            x = X[:, t, h * HD:(h + 1) * HD].rearrange("p t d -> p (t d)")
                            last = v.scalar_tensor_tensor(x, own[k.slot(2)][:, h * HW:h * HW + HD], alone[:, t, h], x, ALU.mult, ALU.add)
                        last.then_inc(own_used, 1)

                    def stat(k):
                        v.wait_ge(own_used, k.v + 1)
                        v.nop(nofuse=True)
                        v.bn_stats(stats[:, bass.ds(k.v, 1), :].rearrange("p t c -> p (t c)"),
                                   X[:, bass.ds(k.v, 1), :].rearrange("p t d -> p (t d)")).then_inc(st2, 1)
                    repeat(v, TILES, 2, [(0, residual), (1, residual_alone), (2, stat)])
                    v.wait_ge(st2, TILES)
                    for t in range(TILES):
                        v.bn_aggr(mv[:, t, :], stats[:, t, :]).then_inc(st2_done, 1)
                    v.wait_ge(std2, 1)
                    v.reciprocal(rstd[:, :], rstd[:, :]).then_inc(std2, 1)
                    v.wait_ge(std2, 2)
                    v.scalar_tensor_tensor(nbias[:, :], mv[:, :, 0], -1.0, rstd[:, :], ALU.mult, ALU.mult).then_inc(ln2, 1)
                    v.wait_ge(w0_ps, 1)
                    v.tensor_copy(W0T[:, :, :].rearrange("p k n -> p (k n)"), pO[0][:, :]).then_inc(w0_ready, 1)

                    def move_hT(k):
                        v.wait_ge(h2T_ps, k.v + 1)
                        if k.past(2):
                            v.wait_ge(rel_ps, (k.v - 1) * 8)
                        v.tensor_copy(hT[k.slot(2)][:, :, :], pT[0][:, :, :]).then_inc(h2T_ready, 1)

                    def root(k):
                        v.wait_ge(root_ps, k.v + 1)
                        v.wait_ge(h2_ready, k.v + 1)
                        x = X[:, bass.ds(k.v, 1), :].rearrange("p t d -> p (t d)")
                        v.tensor_tensor(x, x, pO[0][:, 0:DIM], ALU.add).then_inc(root_add, 1)

                    def move_rel(k):
                        if k.past(2):
                            v.wait_ge(rel_st[k.slot(2)], k.round * 16)
                        for j in range(1, 8, 2):
                            v.wait_ge(rel_ps, k.v * 8 + j + 1)
                            v.tensor_copy(rel_out[k.slot(2)][:, j * 512:(j + 1) * 512], pH[j % 4][:, :]).then_inc(rel_dve, 1)

                    def degree_hots(k):
                        first, m = deg_groups(k)
                        if k.past(2):
                            v.wait_ge(deg_ps, k.v - 1)
                        v.tensor_tensor(node_hot[k.slot(2)][:, 0:m * SUB, :], iotab[:, None, :].to_broadcast([P, m * SUB, P]),
                                        slot_locb[1][:, bass.ds(first, m), :].rearrange("p g j -> p (g j)")[:, :, None].to_broadcast([P, m * SUB, P]), ALU.is_equal)
                        v.tensor_tensor(rel_hot[k.slot(2)][:, 0:m * SUB, :], iota[:, None, 0:RELS].to_broadcast([P, m * SUB, RELS]),
                                        slot_rel[:, bass.ds(first, m), :].rearrange("p g j -> p (g j)")[:, :, None].to_broadcast([P, m * SUB, RELS]), ALU.is_equal).then_inc(deg_hot, 1)
                    repeat(v, TILES, 2, [(0, move_hT), (1, root), (0, degree_hots), (1, move_rel)])
                    v.wait_ge(deg_add, GROUPS)
                    v.tensor_scalar(inv_deg[:, :, :], inv_deg[:, :, :], 1.0, None, ALU.max).then_inc(deg_done, 1)
                    v.wait_ge(deg_done, 1)
                    v.reciprocal(inv_deg[:, :, :], inv_deg[:, :, :])

                @block.scalar
                def _(act):
                    act.wait_ge(st2_done, TILES)
                    act.activation(rstd[:, :], mv[:, :, 1], ACT.Sqrt, bias=eps[:, 0:1]).then_inc(std2, 1)
                    act.wait_ge(ln2, 1)

                    def norm(k):
                        if k.past(2):
                            act.wait_ge(h2T_ps, k.v - 1)
                        act.activation(hbuf[k.slot(2)][:, :], X[:, bass.ds(k.v, 1), :].rearrange("p t d -> p (t d)"), ACT.Relu,
                                       bias=nbias[:, bass.ds(k.v, 1)], scale=rstd[:, bass.ds(k.v, 1)]).then_inc(h2_ready, 1)

                    def move_rel(k):
                        if k.past(2):
                            act.wait_ge(rel_st[k.slot(2)], k.round * 16)
                        for j in range(0, 8, 2):
                            act.wait_ge(rel_ps, k.v * 8 + j + 1)
                            act.activation(rel_out[k.slot(2)][:, j * 512:(j + 1) * 512], pH[j % 4][:, :], ACT.Copy).then_inc(rel_act, 1)

                    def move_degrees(k):
                        _, m = deg_groups(k)
                        act.wait_ge(deg_ps, k.v + 1)
                        if k.past(2):
                            act.wait_ge(deg_add, deg_groups(k)[0] - DEG[1 - k.slot(2)])
                        act.activation(deg_part[k.slot(2)][:, 0:m, :].rearrange("p g r -> p (g r)"), pD[k.slot(2)][:, 0:m * RELS], ACT.Copy).then_inc(deg_moved, 1)
                    repeat(act, TILES, 2, [(0, norm), (2, move_rel), (2, move_degrees)])

                @block.tensor
                def _(pe):
                    pe.wait_ge(w_ld, 64)
                    for k in range(2):
                        for m in range(2):
                            last = pe.transpose(pO[0][:, k * DIM + m * P:k * DIM + (m + 1) * P], w0[:, m, k * P:(k + 1) * P], ident[:, :])
                    last.then_inc(w0_ps, 1)
                    pe.wait_ge(w0_ready, 1)

                    def transpose_h(k):
                        pe.wait_ge(h2_ready, k.v + 1)
                        if k.past(1):
                            pe.wait_ge(h2T_ready, k.v)
                        for j in range(2):
                            last = pe.transpose(pT[0][:, j, :], hbuf[k.slot(2)][:, j * P:(j + 1) * P], ident[:, :])
                        last.then_inc(h2T_ps, 1)

                    def products(k):
                        h = hT[k.slot(2)]
                        pe.wait_ge(h2T_ready, k.v + 1)
                        if k.past(1):
                            pe.wait_ge(root_add, k.v)
                        pe.matmul(pO[0][:, 0:DIM], h[:, 0, :], W0T[:, 0, :], start=True, stop=False)
                        pe.matmul(pO[0][:, 0:DIM], h[:, 1, :], W0T[:, 1, :], start=False, stop=False)
                        pe.matmul(pO[0][:, 0:DIM], ones_row[0:1, :], row2[0:1, :], start=False, stop=True).then_inc(root_ps, 1)
                        for j in range(8):
                            moved = rel_dve if j % 2 else rel_act
                            if k.past(1) or j >= 4:
                                pe.wait_ge(moved, k.v * 4 + (j // 2 - 1))
                            for i in range(2):
                                last = pe.matmul(pH[j % 4][:, :], h[:, i, :], wr[:, i, j * 512:(j + 1) * 512], start=(i == 0), stop=(i == 1))
                            last.then_inc(rel_ps, 1)

                    def count(k):
                        _, m = deg_groups(k)
                        pe.wait_ge(deg_hot, k.v + 1)
                        if k.past(2):
                            pe.wait_ge(deg_moved, k.v - 1)
                        for i in range(m):
                            for c in range(i * SUB, (i + 1) * SUB):
                                last = pe.matmul(pD[k.slot(2)][:, i * RELS:(i + 1) * RELS], node_hot[k.slot(2)][:, c, :], rel_hot[k.slot(2)][:, c, :],
                                                 start=(c == i * SUB), stop=(c == (i + 1) * SUB - 1))
                        last.then_inc(deg_ps, 1)
                    repeat(pe, TILES, 2, [(0, transpose_h), (1, products), (1, count)])

        carve = Carve()
        G1 = [carve([SUB, DIM]) for _ in range(RING)]
        hot = [carve([SUB, P], BF16) for _ in range(2)]
        rhot = [carve([SUB, RELS]) for _ in range(4)]
        rprod = [carve([SUB, RELS]) for _ in range(2)]
        OT1 = [carve([SUB, P]) for _ in range(2)]
        W1 = [carve([SUB, P]) for _ in range(2)]
        wt = [carve([SUB]) for _ in range(2)]
        with ExitStack() as ps:
            qX = [psum(ps, f"rX{i}", [P, SUB, P], BF16) for i in range(2)]
            qE = [psum(ps, f"rE{i}", [P, 512]) for i in range(2)]
            qA = [psum(ps, f"rA{i}", [P, 512]) for i in range(2)]
            idx1, hot1, hotT, ot1, deg_ex, rhot1, w_prod, w_sum, w1_done, agg1, add1 = (sem(x) for x in (
                "idx1", "hot1", "hotT", "ot1", "deg_ex", "rhot1", "w_prod", "w_sum", "w1_done", "agg1", "add1"))
            got1 = [sem(f"got1{i}") for i in range(RING)]
            out_done = sem("out_done")
            with nc.Block() as block:

                @block.gpsimd
                def _(g):
                    def gather(k):
                        sl = k.slot(RING)
                        g.wait_ge(idx1, k.v + 1)
                        if k.past(RING):
                            g.wait_ge(agg1, k.v - (RING - 1))
                        g.nop(nofuse=True)
                        for c in range(SUB):
                            g.indirect_dma_start(G1[sl][:, c, :], None, rel_table,
                                                 bass.IndirectOffsetOnAxis(ap=idx_ring[sl][:, c:c + 1], axis=0)).then_inc(got1[sl], 16)
                    repeat(g, GROUPS, RING, [(0, gather)])

                @block.scalar
                def _(act):
                    def index(k):
                        sl = k.slot(RING)
                        if k.past(RING):
                            act.wait_ge(got1[sl], k.round * (16 * SUB))
                        act.copy(idx_ring[sl][:, :], slot_idx[1][:, bass.ds(k.v, 1), :].rearrange("p g j -> p (g j)")).then_inc(idx1, 1)

                    def move(k):
                        act.wait_ge(hotT, k.v + 1)
                        if k.past(2):
                            act.wait_ge(deg_ex, k.v - 1)
                        act.activation(OT1[k.slot(2)], qX[k.slot(2)][:, :, :], ACT.Copy).then_inc(ot1, 1)
                    repeat(act, GROUPS, RING, [(0, index), (2, move)])

                @block.tensor
                def _(pe):
                    def spread(k):
                        sl = k.slot(2)
                        pe.wait_ge(hot1, k.v + 1)
                        if k.past(2):
                            pe.wait_ge(ot1, k.v - 1)
                        for c in range(SUB):
                            last = pe.transpose(qX[sl][:, c, :], hot[sl][:, c, :], identb[:, :])
                        last.then_inc(hotT, 1)

                    def expand(k):
                        sl = k.slot(2)
                        b = pe.value_load(gtile[0:1, 1, bass.ds(k.v, 1)], min_val=0, max_val=TILES - 1)
                        pe.wait_ge(ot1, k.v + 1)
                        if k.past(2):
                            pe.wait_ge(w_prod, k.v - 1)
                        for c in range(SUB):
                            last = pe.matmul(qE[sl][:, c * RELS:(c + 1) * RELS], OT1[sl][:, c, :],
                                             inv_deg[:, bass.ds(b, 1), :].rearrange("p t r -> p (t r)"), start=True, stop=True)
                        last.then_inc(deg_ex, 1)

                    def aggregate(k):
                        sl = k.slot(2)
                        pe.wait_ge(w1_done, k.v + 1)
                        pe.wait_ge(got1[k.slot(RING)], (k.round + 1) * (16 * SUB))
                        if k.past(2):
                            pe.wait_ge(add1, k.v - 1)
                        for c in range(SUB):
                            last = pe.matmul(qA[sl][:, 0:DIM], W1[sl][:, c, :], G1[k.slot(RING)][:, c, :], start=(c == 0), stop=(c == SUB - 1))
                        last.then_inc(agg1, 1)
                    repeat(pe, GROUPS, RING, [(1, spread), (2, expand), (4, aggregate)])

                @block.vector
                def _(v):
                    def hots1(k):
                        if k.past(2):
                            v.wait_ge(hotT, k.v - 1)
                        v.tensor_tensor(hot[k.slot(2)], iotab[:, None, :].to_broadcast([P, SUB, P]),
                                        slot_locb[1][:, bass.ds(k.v, 1), :].rearrange("p g j -> p (g j)")[:, :, None].to_broadcast([P, SUB, P]), ALU.is_equal).then_inc(hot1, 1)

                    def rel_hots(k):
                        if k.past(4):
                            v.wait_ge(w_prod, k.v - 3)
                        v.tensor_tensor(rhot[k.slot(4)], iota[:, None, 0:RELS].to_broadcast([P, SUB, RELS]),
                                        slot_rel[:, bass.ds(k.v, 1), :].rearrange("p g j -> p (g j)")[:, :, None].to_broadcast([P, SUB, RELS]), ALU.is_equal).then_inc(rhot1, 1)

                    def pick(k):
                        sl = k.slot(2)
                        v.wait_ge(deg_ex, k.v + 1)
                        v.wait_ge(rhot1, k.v + 1)
                        if k.past(2):
                            v.wait_ge(w_sum, k.v - 1)
                        v.tensor_tensor(rprod[sl], rhot[k.slot(4)], qE[sl][:, 0:SUB * RELS].rearrange("p (c r) -> p c r", r=RELS), ALU.mult).then_inc(w_prod, 1)

                    def pick_sum(k):
                        v.wait_ge(w_prod, k.v + 1)
                        if k.past(2):
                            v.wait_ge(w1_done, k.v - 1)
                        v.tensor_reduce(wt[k.slot(2)], rprod[k.slot(2)], AX.X, ALU.add).then_inc(w_sum, 1)

                    def weigh(k):
                        v.wait_ge(w_sum, k.v + 1)
                        if k.past(2):
                            v.wait_ge(agg1, k.v - 1)
                        for c in range(SUB):
                            last = v.tensor_scalar(W1[k.slot(2)][:, c, :], iota[:, :], slot_loc[:, bass.ds(k.v, 1), c], wt[k.slot(2)][:, c:c + 1], ALU.is_equal, ALU.mult)
                        last.then_inc(w1_done, 1)

                    def add(k):
                        sl = k.slot(2)
                        b = v.value_load(gtile[0:1, 1, bass.ds(k.v, 1)], min_val=0, max_val=TILES - 1)
                        v.wait_ge(agg1, k.v + 1)
                        if k.past(1):
                            v.wait_ge(add1, k.v)
                        x = X[:, bass.ds(b, 1), :].rearrange("p t d -> p (t d)")
                        v.tensor_tensor(x, x, qA[sl][:, 0:DIM], ALU.add).then_inc(add1, 1)
                    repeat(v, GROUPS, RING, [(4, weigh), (1, hots1), (3, pick), (1, rel_hots), (3, pick_sum), (5, add)])

                @block.sync
                def _(sp):
                    sp.wait_ge(add1, GROUPS)
                    sp.dma_start(out[0:FULL * P, :].rearrange("(t p) d -> p t d", p=P), X[:, 0:FULL, :]).then_inc(out_done, 16)
                    sp.dma_start(out[FULL * P:NODES, :], X[0:REST, FULL, :]).then_inc(out_done, 16)
                    sp.wait_ge(out_done, 32)



_INS = ["x", "src", "dst", "edge_type_16", "L0_gnn_W_w", "L0_gnn_W_b", "L0_gnn_a", "L1_gnn_W_r", "L1_gnn_W0_w", "L1_gnn_W0_b"]


def kernel(**inputs):
    import concourse.bacc as bacc
    from concourse.bass_utils import run_bass_kernel_spmd as run

    nc = bacc.Bacc("TRN2", target_bir_lowering=False, num_devices=1)
    arrays, args = {}, {}
    for name in _INS:
        a = np.ascontiguousarray(inputs[name])
        arrays[f"in_{name}"] = a
        args[name] = nc.dram_tensor(f"in_{name}", a.shape, mybir.dt.from_np(a.dtype), kind="ExternalInput").ap()
    out = nc.dram_tensor("out", (NODES, DIM), F32, kind="ExternalOutput").ap()
    build(nc, args, out)
    r = run(nc, [arrays], core_ids=[0])
    return r.results[0]["out"]
```
